# Optimizing a Trainium2 kernel written in Bass

```python
import numpy as np
import jax
import jax.numpy as jnp

def _softmax(x, axis=-1):
    return jax.nn.softmax(x, axis=axis)

def _gelu(x):
    return jax.nn.gelu(x, approximate=True)

def _silu(x):
    return jax.nn.silu(x)

def _sigmoid(x):
    return jax.nn.sigmoid(x)

def _layernorm(x, axis=-1, eps=1e-05):
    m = jnp.mean(x, axis=axis, keepdims=True)
    v = jnp.var(x, axis=axis, keepdims=True)
    return (x - m) / jnp.sqrt(v + eps)

def _scatter_add(tgt, idx, src, axis=0):
    return tgt.at[idx].add(src)

def _segment_sum(src, seg, n):
    return jax.ops.segment_sum(src, seg, n)
kernel_name = 'mk_adj_ffn_d2_adj_r2_249f7d'

def setup_inputs(seed: int=0):
    np.random.seed(seed)
    _w = jnp.asarray

    def _rec_inputs():
        import jax
        import jax.numpy as jnp
        _gk = jax.random.key(seed)
        x = -0.000929 + 1 * jax.random.normal(jax.random.fold_in(_gk, 1), (2048, 128), jnp.float32)
        _a = jax.random.bernoulli(jax.random.fold_in(_gk, 2), 0.00390625, (2048, 2048))
        _a = jnp.logical_or(_a, jnp.swapaxes(_a, -1, -2))
        _a = jnp.logical_or(_a, jnp.eye(2048, dtype=bool))
        _af = _a.astype(jnp.float32)
        _af = _af * jax.random.uniform(jax.random.fold_in(_gk, 3), (2048, 2048), jnp.float32, 0.05, 1)
        adj = _af
        return (x, adj)
    x, adj = _rec_inputs()

    def _L0_gnn_setup():
        import jax, jax.numpy as jnp
        import numpy as np
        N, H, HEADS = (2048, 128, 3)
        ALPHA = 0.2
        NEG_INF = -9000000000000000.0

        def _sign_adj(key, n, density):
            k1, k2 = jax.random.split(key)
            mask = jax.random.uniform(k1, (n, n)) < density
            sign = jnp.where(jax.random.uniform(k2, (n, n)) < 0.5, -1.0, 1.0)
            adj = jnp.where(mask, sign, 0.0).astype(jnp.float32)
            idx = jnp.arange(n)
            return adj.at[idx, idx].set(1.0)

        def _gru_cell(x, hstate, Wih, Whh, bih, bhh):
            gi = x @ Wih.T + bih
            gh = hstate @ Whh.T + bhh
            ir, iz, inn = jnp.split(gi, 3, axis=1)
            hr, hz, hn = jnp.split(gh, 3, axis=1)
            r = jax.nn.sigmoid(ir + hr)
            z = jax.nn.sigmoid(iz + hz)
            n = jnp.tanh(inn + r * hn)
            return (1.0 - z) * n + z * hstate

        def _gat_head(h, node_adj, edge_adj, W, a):
            hW = h @ W
            hp = (node_adj > 0).astype(hW.dtype) @ hW
            hm = (node_adj < 0).astype(hW.dtype) @ hW
            e_plus = jax.nn.leaky_relu(jnp.concatenate([hp, hm], axis=1) @ a, ALPHA)[:, 0]
            e_minus = jax.nn.leaky_relu(jnp.concatenate([hm, hp], axis=1) @ a, ALPHA)[:, 0]
            att = jnp.where(edge_adj > 0, e_plus[None, :], NEG_INF)
            att = jnp.where(edge_adj < 0, e_minus[None, :], att)
            att = jax.nn.softmax(att, axis=1)
            return att * edge_adj @ hW
        key = jax.random.key(seed)
        ks = jax.random.split(key, 16)
        std = 0.01
        gain = 1.414
        return {'h': jax.random.normal(ks[0], (N, H), jnp.float32), 'node_adj': _sign_adj(ks[1], N, 0.005), 'edge_adj': _sign_adj(ks[2], N, 0.005), 'gat_W': jax.random.normal(ks[3], (HEADS, H, H), jnp.float32) * (gain / np.sqrt(H, dtype=np.float32)), 'gat_a': jax.random.normal(ks[4], (HEADS, 2 * H, 1), jnp.float32) * 0.1, 'edge_Wih': jax.random.normal(ks[5], (3 * H, H), jnp.float32) * std, 'edge_Whh': jax.random.normal(ks[6], (3 * H, H), jnp.float32) * std, 'edge_bih': jnp.zeros((3 * H,), jnp.float32), 'edge_bhh': jnp.zeros((3 * H,), jnp.float32), 'node_Wih': jax.random.normal(ks[7], (3 * H, H), jnp.float32) * std, 'node_Whh': jax.random.normal(ks[8], (3 * H, H), jnp.float32) * std, 'node_bih': jnp.zeros((3 * H,), jnp.float32), 'node_bhh': jnp.zeros((3 * H,), jnp.float32)}
    _L0_gnn_all = _L0_gnn_setup()
    _L0_gnn_in = {k: v for k, v in _L0_gnn_all.items() if k in ('gat_W', 'gat_a', 'edge_Wih', 'edge_Whh', 'edge_bih', 'edge_bhh', 'node_Wih', 'node_Whh', 'node_bih', 'node_bhh')}
    del _L0_gnn_all

    def _L0_ffn_setup():
        import jax, jax.numpy as jnp
        import numpy as np
        H, P, G, NS, K = (8, 64, 64, 64, 3)
        D_INNER = H * P
        CONV_DIM = D_INNER + 2 * NS
        D_IN_PROJ = 2 * D_INNER + 2 * NS + 2 * H

        def _hydra(u, in_w, conv_w, conv_b, dt_bias, A_log, Dp, fcD_w, norm_w, out_w):
            Bt, L, _ = u.shape
            zxbcdt = u @ in_w.T
            z = zxbcdt[..., :D_INNER]
            xBC = zxbcdt[..., D_INNER:D_INNER + CONV_DIM]
            dt = zxbcdt[..., -2 * H:]
            dt = jnp.concatenate([dt[..., :H], jnp.flip(dt[..., H:], axis=1)], axis=0)
            dt = jax.nn.softplus(dt + dt_bias)
            xp = jnp.pad(xBC, ((0, 0), (K - 1, 0), (0, 0)))
            xBC = sum((xp[:, k:k + L, :] * conv_w[:, k] for k in range(K))) + conv_b
            xBC = jax.nn.silu(xBC)
            x = xBC[..., :D_INNER]
            Bm = xBC[..., D_INNER:D_INNER + NS]
            Cm = xBC[..., D_INNER + NS:]
            x_og = x
            x2 = jnp.concatenate([x, jnp.flip(x, 1)], 0).reshape(2 * Bt, L, H, P)
            B2 = jnp.concatenate([Bm, jnp.flip(Bm, 1)], 0)
            C2 = jnp.concatenate([Cm, jnp.flip(Cm, 1)], 0)
            dA = jnp.exp(dt * -jnp.exp(A_log))
            dBx = jnp.einsum('blh,bln,blhp->blhpn', dt, B2, x2)

            def step(h, inp):
                dA_t, dBx_t, C_t = inp
                h = h * dA_t[:, :, None, None] + dBx_t
                return (h, jnp.einsum('bhpn,bn->bhp', h, C_t))
            h0 = jnp.zeros((2 * Bt, H, P, NS), u.dtype)
            _, ys = jax.lax.scan(step, h0, (dA.transpose(1, 0, 2), dBx.transpose(1, 0, 2, 3, 4), C2.transpose(1, 0, 2)))
            y = ys.transpose(1, 0, 2, 3).reshape(2 * Bt, L, D_INNER)
            y_fw, y_bw = (y[:Bt], jnp.flip(y[Bt:], 1))
            y = jnp.pad(y_fw[:, :-1], ((0, 0), (1, 0), (0, 0))) + jnp.pad(y_bw[:, 1:], ((0, 0), (0, 1), (0, 0)))
            y = y + x_og * jnp.repeat(x_og @ fcD_w.T + Dp, P, axis=-1)
            yg = y * jax.nn.silu(z)
            yg = yg * jax.lax.rsqrt(jnp.mean(jnp.square(yg), -1, keepdims=True) + 1e-05) * norm_w
            return yg @ out_w.T
        key = jax.random.key(seed)
        ks = jax.random.split(key, 10)
        dim, Bsz, N = (128, 4, 4096)
        s = 0.02
        return {'x': jax.random.normal(ks[0], (Bsz, N, dim), jnp.float32), 'W_fx': jax.random.normal(ks[1], (D_INNER, dim), jnp.float32) * s, 'b_fx': jnp.zeros((D_INNER,), jnp.float32), 'W_x': jax.random.normal(ks[2], (D_INNER, dim), jnp.float32) * s, 'b_x': jnp.zeros((D_INNER,), jnp.float32), 'W_slice': jax.random.normal(ks[3], (G, P), jnp.float32) * s, 'b_slice': jnp.zeros((G,), jnp.float32), 'temperature': jnp.full((1, H, 1, 1), 0.5, jnp.float32), 'hy_in_w': jax.random.normal(ks[4], (D_IN_PROJ, D_INNER), jnp.float32) * s, 'hy_conv_w': jax.random.normal(ks[5], (CONV_DIM, K), jnp.float32) * s, 'hy_conv_b': jnp.zeros((CONV_DIM,), jnp.float32), 'hy_dt_bias': jnp.log(jnp.expm1(jnp.full((H,), 0.01, jnp.float32))), 'hy_A_log': jnp.log(jnp.linspace(1.0, 16.0, H)).astype(jnp.float32), 'hy_D': jnp.ones((H,), jnp.float32), 'hy_fcD_w': jax.random.normal(ks[6], (H, D_INNER), jnp.float32) * s, 'hy_norm_w': jnp.ones((D_INNER,), jnp.float32), 'hy_out_w': jax.random.normal(ks[7], (D_INNER, D_INNER), jnp.float32) * s, 'out_w': jax.random.normal(ks[8], (dim, D_INNER), jnp.float32) * s, 'out_b': jnp.zeros((dim,), jnp.float32)}
    _L0_ffn_all = _L0_ffn_setup()
    _L0_ffn_in = {k: v for k, v in _L0_ffn_all.items() if k in ('W_fx', 'b_fx', 'W_x', 'b_x', 'W_slice', 'b_slice', 'temperature', 'hy_in_w', 'hy_conv_w', 'hy_conv_b', 'hy_dt_bias', 'hy_A_log', 'hy_D', 'hy_fcD_w', 'hy_norm_w', 'hy_out_w', 'out_w', 'out_b')}
    del _L0_ffn_all

    def _L1_gnn_setup():
        import jax, jax.numpy as jnp
        import numpy as np
        N = 4096
        D = 128
        DENSITY = 0.02
        key = jax.random.key(seed)
        k1, k2, k3, k4 = jax.random.split(key, 4)
        inputs = jax.random.normal(k1, (N, D), dtype=jnp.float32)
        vals = jax.random.uniform(k2, (N, N), dtype=jnp.float32, minval=0.1, maxval=1.0)
        mask = jax.random.uniform(k3, (N, N), dtype=jnp.float32) < DENSITY
        adj = jnp.where(mask, vals, 0.0)
        H_v = 0.1 * jax.random.normal(k4, (D, 1), dtype=jnp.float32)
        return {'inputs': inputs, 'adj': adj, 'H_v': H_v}
    _L1_gnn_all = _L1_gnn_setup()
    _L1_gnn_in = {k: v for k, v in _L1_gnn_all.items() if k in ('H_v',)}
    del _L1_gnn_all

    def _L1_ffn_setup():
        import jax, jax.numpy as jnp
        import numpy as np
        E = 8
        K = 2
        D = 128
        H = 256
        DOUT = 128
        EPS = 1e-05
        key = jax.random.key(seed)
        ks = jax.random.split(key, 9)
        s = 0.02
        return {'x': jax.random.normal(ks[0], (4, 4096, D), jnp.float32), 'gamma': 1.0 + 0.05 * jax.random.normal(ks[1], (D,), jnp.float32), 'beta': 0.05 * jax.random.normal(ks[2], (D,), jnp.float32), 'Wr': 0.01 * jax.random.normal(ks[3], (D, E), jnp.float32), 'br': jnp.zeros((E,), jnp.float32), 'W1': s * jax.random.normal(ks[4], (E, D, H), jnp.float32), 'b1': s * jax.random.normal(ks[5], (E, H), jnp.float32), 'W2': s * jax.random.normal(ks[6], (E, H, DOUT), jnp.float32), 'b2': s * jax.random.normal(ks[7], (E, DOUT), jnp.float32)}
    _L1_ffn_all = _L1_ffn_setup()
    _L1_ffn_in = {k: v for k, v in _L1_ffn_all.items() if k in ('gamma', 'beta', 'Wr', 'br', 'W1', 'b1', 'W2', 'b2')}
    del _L1_ffn_all
    return {'x': x, 'adj': adj, 'L0_gnn_gat_W': _L0_gnn_in['gat_W'], 'L0_gnn_gat_a': _L0_gnn_in['gat_a'], 'L0_gnn_edge_Wih': _L0_gnn_in['edge_Wih'], 'L0_gnn_edge_Whh': _L0_gnn_in['edge_Whh'], 'L0_gnn_edge_bih': _L0_gnn_in['edge_bih'], 'L0_gnn_edge_bhh': _L0_gnn_in['edge_bhh'], 'L0_gnn_node_Wih': _L0_gnn_in['node_Wih'], 'L0_gnn_node_Whh': _L0_gnn_in['node_Whh'], 'L0_gnn_node_bih': _L0_gnn_in['node_bih'], 'L0_gnn_node_bhh': _L0_gnn_in['node_bhh'], 'L0_ffn_W_fx': _L0_ffn_in['W_fx'], 'L0_ffn_b_fx': _L0_ffn_in['b_fx'], 'L0_ffn_W_x': _L0_ffn_in['W_x'], 'L0_ffn_b_x': _L0_ffn_in['b_x'], 'L0_ffn_W_slice': _L0_ffn_in['W_slice'], 'L0_ffn_b_slice': _L0_ffn_in['b_slice'], 'L0_ffn_temperature': _L0_ffn_in['temperature'], 'L0_ffn_hy_in_w': _L0_ffn_in['hy_in_w'], 'L0_ffn_hy_conv_w': _L0_ffn_in['hy_conv_w'], 'L0_ffn_hy_conv_b': _L0_ffn_in['hy_conv_b'], 'L0_ffn_hy_dt_bias': _L0_ffn_in['hy_dt_bias'], 'L0_ffn_hy_A_log': _L0_ffn_in['hy_A_log'], 'L0_ffn_hy_D': _L0_ffn_in['hy_D'], 'L0_ffn_hy_fcD_w': _L0_ffn_in['hy_fcD_w'], 'L0_ffn_hy_norm_w': _L0_ffn_in['hy_norm_w'], 'L0_ffn_hy_out_w': _L0_ffn_in['hy_out_w'], 'L0_ffn_out_w': _L0_ffn_in['out_w'], 'L0_ffn_out_b': _L0_ffn_in['out_b'], 'L1_gnn_H_v': _L1_gnn_in['H_v'], 'L1_ffn_gamma': _L1_ffn_in['gamma'], 'L1_ffn_beta': _L1_ffn_in['beta'], 'L1_ffn_Wr': _L1_ffn_in['Wr'], 'L1_ffn_br': _L1_ffn_in['br'], 'L1_ffn_W1': _L1_ffn_in['W1'], 'L1_ffn_b1': _L1_ffn_in['b1'], 'L1_ffn_W2': _L1_ffn_in['W2'], 'L1_ffn_b2': _L1_ffn_in['b2']}

def reference(x, adj, L0_gnn_gat_W, L0_gnn_gat_a, L0_gnn_edge_Wih, L0_gnn_edge_Whh, L0_gnn_edge_bih, L0_gnn_edge_bhh, L0_gnn_node_Wih, L0_gnn_node_Whh, L0_gnn_node_bih, L0_gnn_node_bhh, L0_ffn_W_fx, L0_ffn_b_fx, L0_ffn_W_x, L0_ffn_b_x, L0_ffn_W_slice, L0_ffn_b_slice, L0_ffn_temperature, L0_ffn_hy_in_w, L0_ffn_hy_conv_w, L0_ffn_hy_conv_b, L0_ffn_hy_dt_bias, L0_ffn_hy_A_log, L0_ffn_hy_D, L0_ffn_hy_fcD_w, L0_ffn_hy_norm_w, L0_ffn_hy_out_w, L0_ffn_out_w, L0_ffn_out_b, L1_gnn_H_v, L1_ffn_gamma, L1_ffn_beta, L1_ffn_Wr, L1_ffn_br, L1_ffn_W1, L1_ffn_b1, L1_ffn_W2, L1_ffn_b2):
    import jax
    import jax.numpy as jnp

    def _L0_gnn_ref(h, node_adj, edge_adj, gat_W, gat_a, edge_Wih, edge_Whh, edge_bih, edge_bhh, node_Wih, node_Whh, node_bih, node_bhh):
        import jax, jax.numpy as jnp
        import numpy as np
        N, H, HEADS = (2048, 128, 3)
        ALPHA = 0.2
        NEG_INF = -9000000000000000.0

        def _sign_adj(key, n, density):
            k1, k2 = jax.random.split(key)
            mask = jax.random.uniform(k1, (n, n)) < density
            sign = jnp.where(jax.random.uniform(k2, (n, n)) < 0.5, -1.0, 1.0)
            adj = jnp.where(mask, sign, 0.0).astype(jnp.float32)
            idx = jnp.arange(n)
            return adj.at[idx, idx].set(1.0)

        def _gru_cell(x, hstate, Wih, Whh, bih, bhh):
            gi = x @ Wih.T + bih
            gh = hstate @ Whh.T + bhh
            ir, iz, inn = jnp.split(gi, 3, axis=1)
            hr, hz, hn = jnp.split(gh, 3, axis=1)
            r = jax.nn.sigmoid(ir + hr)
            z = jax.nn.sigmoid(iz + hz)
            n = jnp.tanh(inn + r * hn)
            return (1.0 - z) * n + z * hstate

        def _gat_head(h, node_adj, edge_adj, W, a):
            hW = h @ W
            hp = (node_adj > 0).astype(hW.dtype) @ hW
            hm = (node_adj < 0).astype(hW.dtype) @ hW
            e_plus = jax.nn.leaky_relu(jnp.concatenate([hp, hm], axis=1) @ a, ALPHA)[:, 0]
            e_minus = jax.nn.leaky_relu(jnp.concatenate([hm, hp], axis=1) @ a, ALPHA)[:, 0]
            att = jnp.where(edge_adj > 0, e_plus[None, :], NEG_INF)
            att = jnp.where(edge_adj < 0, e_minus[None, :], att)
            att = jax.nn.softmax(att, axis=1)
            return att * edge_adj @ hW
        dn = jnp.diag(node_adj)
        de = jnp.diag(edge_adj)
        idx = jnp.arange(node_adj.shape[0])
        node_adj_norm = node_adj.at[idx, idx].add(-dn)
        edge_adj_norm = edge_adj.at[idx, idx].add(-de)
        node_support = node_adj_norm @ h
        edge_output = _gru_cell(node_support, h, edge_Wih, edge_Whh, edge_bih, edge_bhh)
        edge_support = _gat_head(h, node_adj_norm, edge_adj_norm, gat_W[0], gat_a[0])
        for i in range(1, HEADS):
            edge_support = edge_support + _gat_head(h, node_adj_norm, edge_adj_norm, gat_W[i], gat_a[i])
        edge_support = edge_support / HEADS
        node_output = _gru_cell(edge_support, h, node_Wih, node_Whh, node_bih, node_bhh)
        return de[:, None] * edge_output + dn[:, None] * node_output

    def _L0_ffn_ref(x, W_fx, b_fx, W_x, b_x, W_slice, b_slice, temperature, hy_in_w, hy_conv_w, hy_conv_b, hy_dt_bias, hy_A_log, hy_D, hy_fcD_w, hy_norm_w, hy_out_w, out_w, out_b):
        import jax, jax.numpy as jnp
        import numpy as np
        H, P, G, NS, K = (8, 64, 64, 64, 3)
        D_INNER = H * P
        CONV_DIM = D_INNER + 2 * NS
        D_IN_PROJ = 2 * D_INNER + 2 * NS + 2 * H

        def _hydra(u, in_w, conv_w, conv_b, dt_bias, A_log, Dp, fcD_w, norm_w, out_w):
            Bt, L, _ = u.shape
            zxbcdt = u @ in_w.T
            z = zxbcdt[..., :D_INNER]
            xBC = zxbcdt[..., D_INNER:D_INNER + CONV_DIM]
            dt = zxbcdt[..., -2 * H:]
            dt = jnp.concatenate([dt[..., :H], jnp.flip(dt[..., H:], axis=1)], axis=0)
            dt = jax.nn.softplus(dt + dt_bias)
            xp = jnp.pad(xBC, ((0, 0), (K - 1, 0), (0, 0)))
            xBC = sum((xp[:, k:k + L, :] * conv_w[:, k] for k in range(K))) + conv_b
            xBC = jax.nn.silu(xBC)
            x = xBC[..., :D_INNER]
            Bm = xBC[..., D_INNER:D_INNER + NS]
            Cm = xBC[..., D_INNER + NS:]
            x_og = x
            x2 = jnp.concatenate([x, jnp.flip(x, 1)], 0).reshape(2 * Bt, L, H, P)
            B2 = jnp.concatenate([Bm, jnp.flip(Bm, 1)], 0)
            C2 = jnp.concatenate([Cm, jnp.flip(Cm, 1)], 0)
            dA = jnp.exp(dt * -jnp.exp(A_log))
            dBx = jnp.einsum('blh,bln,blhp->blhpn', dt, B2, x2)

            def step(h, inp):
                dA_t, dBx_t, C_t = inp
                h = h * dA_t[:, :, None, None] + dBx_t
                return (h, jnp.einsum('bhpn,bn->bhp', h, C_t))
            h0 = jnp.zeros((2 * Bt, H, P, NS), u.dtype)
            _, ys = jax.lax.scan(step, h0, (dA.transpose(1, 0, 2), dBx.transpose(1, 0, 2, 3, 4), C2.transpose(1, 0, 2)))
            y = ys.transpose(1, 0, 2, 3).reshape(2 * Bt, L, D_INNER)
            y_fw, y_bw = (y[:Bt], jnp.flip(y[Bt:], 1))
            y = jnp.pad(y_fw[:, :-1], ((0, 0), (1, 0), (0, 0))) + jnp.pad(y_bw[:, 1:], ((0, 0), (0, 1), (0, 0)))
            y = y + x_og * jnp.repeat(x_og @ fcD_w.T + Dp, P, axis=-1)
            yg = y * jax.nn.silu(z)
            yg = yg * jax.lax.rsqrt(jnp.mean(jnp.square(yg), -1, keepdims=True) + 1e-05) * norm_w
            return yg @ out_w.T
        B, N, _ = x.shape
        fx = (x @ W_fx.T + b_fx).reshape(B, N, H, P).transpose(0, 2, 1, 3)
        xm = (x @ W_x.T + b_x).reshape(B, N, H, P).transpose(0, 2, 1, 3)
        temp = jnp.maximum(temperature, 1e-06)
        sw = jax.nn.softmax((xm @ W_slice.T + b_slice) / temp, axis=-1)
        snorm = sw.sum(2)
        st = jnp.einsum('bhnc,bhng->bhgc', fx, sw) / (snorm + 1e-05)[..., None]
        st = st.transpose(0, 2, 1, 3).reshape(B, G, D_INNER)
        ot = _hydra(st, hy_in_w, hy_conv_w, hy_conv_b, hy_dt_bias, hy_A_log, hy_D, hy_fcD_w, hy_norm_w, hy_out_w)
        ot = ot.reshape(B, G, H, P).transpose(0, 2, 1, 3)
        out = jnp.einsum('bhgc,bhng->bhnc', ot, sw).transpose(0, 2, 1, 3).reshape(B, N, D_INNER)
        return out @ out_w.T + out_b

    def _L1_gnn_ref(inputs, adj, H_v):
        import jax, jax.numpy as jnp
        import numpy as np
        N = 4096
        D = 128
        DENSITY = 0.02
        scores = jnp.squeeze(inputs @ H_v, -1)
        mask = adj != 0.0
        logits = adj * scores[None, :]
        neg = jnp.asarray(jnp.finfo(logits.dtype).min, logits.dtype)
        logits = jnp.where(mask, logits, neg)
        m = jnp.max(logits, axis=1, keepdims=True)
        e = jnp.where(mask, jnp.exp(logits - m), 0.0)
        s = jnp.sum(e, axis=1, keepdims=True)
        weights = e / jnp.where(s > 0, s, 1.0)
        return weights @ inputs

    def _L1_ffn_ref(x, gamma, beta, Wr, br, W1, b1, W2, b2):
        import jax, jax.numpy as jnp
        import numpy as np
        E = 8
        K = 2
        D = 128
        H = 256
        DOUT = 128
        EPS = 1e-05
        mu = jnp.mean(x, axis=-1, keepdims=True)
        var = jnp.mean(jnp.square(x - mu), axis=-1, keepdims=True)
        xn = (x - mu) * jax.lax.rsqrt(var + EPS) * gamma + beta
        logits = jnp.einsum('bsd,de->bse', xn, Wr) + br
        top_vals, top_idx = jax.lax.top_k(logits, K)
        w = jax.nn.softmax(top_vals, axis=-1)
        w_full = jnp.einsum('bsk,bske->bse', w, jax.nn.one_hot(top_idx, E, dtype=w.dtype))
        y = jnp.zeros(x.shape[:-1] + (DOUT,), x.dtype)
        for e in range(E):
            h = jax.nn.gelu(jnp.einsum('bsd,dh->bsh', xn, W1[e]) + b1[e], approximate=False)
            y_e = jnp.einsum('bsh,hd->bsd', h, W2[e]) + b2[e]
            y = y + y_e * w_full[..., e, None]
        return y
    x = x + _L0_gnn_ref(_layernorm(x, axis=-1), adj, adj, L0_gnn_gat_W, L0_gnn_gat_a, L0_gnn_edge_Wih, L0_gnn_edge_Whh, L0_gnn_edge_bih, L0_gnn_edge_bhh, L0_gnn_node_Wih, L0_gnn_node_Whh, L0_gnn_node_bih, L0_gnn_node_bhh)
    x = x + _L0_ffn_ref(_layernorm(x, axis=-1)[None], L0_ffn_W_fx, L0_ffn_b_fx, L0_ffn_W_x, L0_ffn_b_x, L0_ffn_W_slice, L0_ffn_b_slice, L0_ffn_temperature, L0_ffn_hy_in_w, L0_ffn_hy_conv_w, L0_ffn_hy_conv_b, L0_ffn_hy_dt_bias, L0_ffn_hy_A_log, L0_ffn_hy_D, L0_ffn_hy_fcD_w, L0_ffn_hy_norm_w, L0_ffn_hy_out_w, L0_ffn_out_w, L0_ffn_out_b)[0]
    x = x + _L1_gnn_ref(_layernorm(x, axis=-1), adj, L1_gnn_H_v)
    x = x + _L1_ffn_ref(_layernorm(x, axis=-1)[None], L1_ffn_gamma, L1_ffn_beta, L1_ffn_Wr, L1_ffn_br, L1_ffn_W1, L1_ffn_b1, L1_ffn_W2, L1_ffn_b2)[0]
    return x

_drawn_inputs = setup_inputs


def setup_inputs(seed=0):
    import zlib

    import numpy as np

    out = dict(_drawn_inputs(seed))
    spreads = {'L0_gnn_edge_bih': (0.0, 0.277),
     'L0_gnn_edge_bhh': (0.0, 0.519),
     'L0_gnn_node_bih': (0.0, 0.285),
     'L0_gnn_node_bhh': (0.0, 0.49),
     'L0_ffn_b_fx': (0.0, 0.1),
     'L0_ffn_b_x': (0.0, 0.8),
     'L0_ffn_b_slice': (0.0, 0.8),
     'L0_ffn_temperature': (0.5, 0.6),
     'L0_ffn_hy_conv_b': (0.0, 0.1),
     'L0_ffn_hy_dt_bias': (-4.600166320800781, 0.6),
     'L0_ffn_hy_D': (1.0, 0.6),
     'L0_ffn_hy_norm_w': (1.0, 0.6),
     'L0_ffn_out_b': (0.0, 0.1),
     'L1_ffn_br': (0.0, 0.555)}
    factors = {'L0_gnn_gat_W': 5.671,
     'L0_gnn_gat_a': 6.141,
     'L0_gnn_edge_Whh': 3.772,
     'L0_gnn_node_Wih': 5.658,
     'L0_gnn_node_Whh': 3.707,
     'L0_ffn_W_fx': 8.0,
     'L0_ffn_W_x': 8.0,
     'L0_ffn_W_slice': 8.0,
     'L0_ffn_hy_conv_w': 8.0,
     'L0_ffn_hy_A_log': 8.0,
     'L0_ffn_hy_fcD_w': 8.0,
     'L1_ffn_gamma': 8.0,
     'L1_ffn_beta': 8.0,
     'L1_ffn_Wr': 3.988,
     'L1_ffn_W1': 3.583,
     'L1_ffn_b1': 8.0,
     'L1_ffn_W2': 3.518,
     'L1_ffn_b2': 6.766}
    for name, (base, spread) in spreads.items():
        noise = np.random.default_rng([zlib.crc32(name.encode()), seed]).standard_normal(out[name].shape)
        drawn = base * np.exp(spread * noise) if base else spread * noise
        out[name] = jnp.asarray(drawn.astype(out[name].dtype))
    for name, factor in factors.items():
        out[name] = (out[name] * factor).astype(out[name].dtype)
    return out
```

```python
from contextlib import ExitStack

import numpy as np

import concourse.bass as bass
from concourse import mybir

ALU = mybir.AluOpType
ACT = mybir.ActivationFunctionType
AX = mybir.AxisListType
F32 = mybir.dt.float32
BF16 = mybir.dt.bfloat16
U8 = mybir.dt.uint8

P = 128
N = 2048
D = 128
NT = N // P
CH = 512
NC = N // CH
TC = CH // P
HEADS = 3
NS = 2 * HEADS
K = NT * HEADS
RING = 6
EPS = 1e-5
FLOOR = 1e30
NEG = 9e15
FAR = 3e38
GAT_ALPHA = 0.2
SLOPES = 8
G = 64
DI = 512
CB = DI // P
EXPERTS = 8
HID = 256
HC = HID // P


def numbered(*names):
    return {name: n + 1 for n, name in enumerate(names)}


HY_PE = numbered("slice_w", "slice_b", "snorm", "tokens", "zx", "bcdt", "decay", "gram", "x_rows", "skip", "y",
                 "power", "out", "value")
HY_DVE = numbered("bias_cols", "inv_temp", "slice_w", "slice_b1", "slice_b", "snorm_eps", "snorm_inv", "tok_w", "snorm_n",
                  "tok_b0", "tok_b1", "tok0", "tok1", "pad", "dt_in", "dt_neg", "dt_nabs", "conv0", "conv1", "conv01",
                  "conv2", "conv012", "conv_b", "dt", "decay_rate", "decay_in", "silu_den", "silu_inv", "xbc", "x_twice",
                  "gram", "weight_dt", "weight", "z_den", "z_inv", "z", "skip_d", "skip", "y", "yg", "sq", "rms",
                  "yn", "ynw", "ot0", "ot1")
HY_ACT = numbered("rate", "z_copy", "dt_exp", "dt_ln", "conv_exp", "decay_exp", "x_rows", "z_exp", "rms_std", "value")


def reached(eng, sem, value):
    if isinstance(value, int) and value <= 0:
        return
    eng.wait_ge(sem, value)


def graph_block(nc: bass.Bass, a: dict, out: bass.AP):
    ctx = ExitStack()
    with ctx:
        def sb(name, shape, dt=F32):
            return ctx.enter_context(nc.sbuf_tensor(name, shape, dt))

        def sem(name):
            return ctx.enter_context(nc.semaphore(name))

        ps = ctx.enter_context(nc.psum_tensor("ps", [P, 8, CH], F32))

        ident = sb("ident", [P, P])
        noteye = sb("noteye", [P, P])
        eps_col = sb("eps_col", [P, 1])
        xr = sb("xr", [P, NT, D])
        hrow = sb("hrow", [P, NT, D])
        hT = sb("hT", [P, N])
        nsT = sb("nsT", [P, N])
        hW = sb("hW", [P, NT, HEADS * D])
        eb = sb("eb", [P, NS, N])
        arow = sb("arow", [P, 2, N])
        nb = sb("nb", [P, N])
        mneg = sb("mneg", [P, N], U8)
        ring = sb("ring", [P, RING, N])
        pat = sb("pat", [P, 2, N])
        esT = hrow[:, :, :].rearrange("p t d -> p (t d)")

        def cutter(area, size):
            at = [0]

            def piece(n):
                at[0] += n
                assert at[0] <= size, at
                return area[:, at[0] - n:at[0]]
            return piece

        st6 = sb("st6", [P, NT * 6])[:, :].rearrange("p (t s) -> p t s", t=NT)
        mv = sb("mv", [P, NT * 2])[:, :].rearrange("p (t s) -> p t s", t=NT)
        std = sb("std", [P, NT])[:, :]
        rstd = sb("rstd", [P, NT])[:, :]
        gatWT = sb("gatWT", [P, HEADS * D])[:, :]
        gatA = sb("gatA", [P, NS])[:, :].rearrange("p (s h) -> p s h", s=2)
        wa = sb("wa", [P, NS])[:, :]
        WT = [sb(f"WT{k}", [P, 3 * D])[:, :] for k in range(4)]
        gb = sb("gb", [P, 12])[:, :].rearrange("p (k g) -> p k g", k=4)
        gbs = sb("gbs", [P, 6])[:, :].rearrange("p (k g) -> p k g", k=2)
        diag = sb("diag", [P, NT])[:, :]
        mn = sb("mn", [P, RING])[:, :]
        den = sb("den", [P, RING])[:, :]
        rden = sb("rden", [P, RING])[:, :]
        esb = sb("esb", [P, 2 * D])[:, :].rearrange("p (u d) -> p u d", u=2)

        aT = [ring[:, s, :] for s in range(3)]
        masks = pat[:, :, :].rearrange("p u n -> p (u n)").bitcast(BF16).rearrange(
            "p (u s n) -> p u s n", u=2, s=2)
        mres = ring[:, 3, :]
        parts = ring[:, 4, 0:NT * 96].bitcast(BF16).rearrange(
            "p (v t q) -> p v t q", v=2, t=NT)
        sel = ring[:, 5, 0:NS * P].rearrange("p (q m) -> p q m", q=NS)
        piece5 = cutter(ring[:, 5, NS * P:N], N - NS * P)
        gatW = piece5(HEADS * D)
        uu = [piece5(NT * NS).rearrange("p (t q) -> p t q", t=NT) for _ in range(4)]
        gr, gz, gt = ([pat[:, u, k * CH:(k + 1) * CH] for u in range(2)] for k in range(3))
        gout = pat[:, :, 3 * CH:4 * CH]

        swT = eb[:, 0:CB, :]
        sw = [ring[:, t % 4, (t // 4) * CH:(t // 4 + 1) * CH] for t in range(8)]
        hWf = hW[:, :, :].rearrange("p t d -> p (t d)")
        cut_h = cutter(hWf, NT * HEADS * D)
        ZX = 2 * DI + 2 * G + 2 * SLOPES
        in_wT = cut_h(CB * ZX).rearrange("p (k n) -> p k n", k=CB)
        wx = cut_h(SLOPES * D).rearrange("p (h d) -> p h d", h=SLOPES)
        wsT = cut_h(G)
        outT = eb[:, 4, :].rearrange("p (k n) -> p k n", k=CB)
        fcDT = eb[:, 5, :].rearrange("p (k n) -> p k n", k=CB)
        cut4 = cutter(ring[:, 4, :], N)
        wfxT, w_slice, b_slice = cut4(DI), cut4(DI), cut4(DI)
        outwT = cut4(CB * D).rearrange("p (m d) -> p m d", m=CB)
        cut5 = cutter(ring[:, 5, :], N)
        bx_cols = cut5(SLOPES * P).rearrange("p (h m) -> p h m", h=SLOPES)
        swsum = cut5(DI)
        bsl, bx, temp = cut5(G), cut5(SLOPES), cut5(SLOPES)
        bfx, cw, cb = cut5(CB), cut5(6 * 3).rearrange("p (c k) -> p c k", c=6), cut5(6)
        dtb, alog, dcol, nwcol = cut5(SLOPES), cut5(SLOPES), cut5(CB), cut5(CB)
        dt_s = [cut5(SLOPES) for _ in range(5)]
        rate = cut5(SLOPES)
        mx8 = [cut5(SLOPES) for _ in range(4)]
        rs8 = [cut5(SLOPES) for _ in range(4)]
        cutn = cutter(nb, N)
        outb = cutn(D)
        m_rs, m_rt, m_st = cutn(P), cutn(G), cutn(G)
        ones = cutn(P)
        tok_n, sn_n, rsn = cutn(DI), cutn(DI), cutn(DI)
        hy = [ring[:, k, 2 * CH:4 * CH] for k in range(4)]
        tokT = hy[0][:, 0:CB * G].rearrange("p (k g) -> p k g", k=CB)
        tokb = hy[0][:, CB * G:2 * CB * G].rearrange("p (k g) -> p k g", k=CB)
        PADW = G + 2
        xp = hy[0][:, 512:512 + 6 * PADW].rearrange("p (c l) -> p c l", c=6)
        xs = hy[1][:, 0:6 * PADW].rearrange("p (c l) -> p c l", c=6)
        cva = hy[1][:, 400:400 + 6 * G].rearrange("p (c l) -> p c l", c=6)
        cvt = hy[2][:, 0:6 * G].rearrange("p (c l) -> p c l", c=6)
        gramm = hy[2][:, 384:384 + G]
        x2 = hy[2][:, 512:1024]
        dec = hy[3][:, 0:512].rearrange("p (h t) -> p h t", h=SLOPES)
        xd = hy[3][:, 512:1024].rearrange("p (m v g) -> p m v g", m=CB, v=2)
        cutp = cutter(pat[:, 0, :], N)
        zz, z1, y1, ysq = (cutp(CB * G).rearrange("p (k g) -> p k g", k=CB) for _ in range(4))
        bd = cutp(CB * P).rearrange("p (m r) -> p m r", m=CB)
        rms = cutp(G)
        val = pat[:, 1, 0:CB * D].rearrange("p (m d) -> p m d", m=CB)

        sbn = eb[:, 0, :]
        hv_cols = nsT[:, 0:D]
        cute = cutter(nsT[:, D:N], N - D)
        wexp = [(cute(HID), cute(HC * D).rearrange("p (c d) -> p c d", c=HC)) for _ in range(2)]
        wr, hv, gamma, beta = cute(EXPERTS), cute(1), cute(1), cute(1)
        b1 = cute(EXPERTS * HC).rearrange("p (e c) -> p e c", e=EXPERTS)
        b2, br, prio = cute(D), cute(EXPERTS), cute(EXPERTS)
        hid = pat[:, :, 0:2 * CH].rearrange("p u (c n) -> p u c n", c=HC)
        cutr = cutter(nb, N)
        route, top, hot1, hot2, wfull = (cutr(NT * EXPERTS).rearrange("p (t e) -> p t e", t=NT) for _ in range(5))
        v1, v2, ky, ew, w1 = (cutr(NT) for _ in range(5))
        wT = eb[0:EXPERTS, 1, :]
        OUT_COUNT = 16 * NC

        ld_x, ld_c, ld_gat, ld_gru = sem("ld_x"), sem("ld_c"), sem("ld_gat"), sem("ld_gru")
        aT_in = [sem(f"aT_in{s}") for s in range(3)]
        dve_seq = sem("dve_seq")
        out_stored = sem("out_stored")
        ln_stats, ln_std, ln_rstd, ln_row, ln_tp, ln_hT = (
            sem("ln_" + s) for s in ("stats", "std", "rstd", "row", "tp", "hT"))
        wa_mm, wa_sb, u_mm, parts_ok = sem("wa_mm"), sem("wa_sb"), sem("u_mm"), sem("parts_ok")
        hw_mm, hw_sb = sem("hw_mm"), sem("hw_sb")
        masks_ok, aT_used, ns_sb, mres_sb = sem("masks_ok"), sem("aT_used"), sem("ns_sb"), sem("mres_sb")
        bc_mm, bc_sb, eb_ok = sem("bc_mm"), sem("bc_sb"), sem("eb_ok")
        gru_mm, gru_r, gru_z, gru_t, gru_n, gru_out = (
            sem("gru_" + s) for s in ("mm", "r", "z", "t", "n", "out"))
        gru_pool, gbs_ok = sem("gru_pool"), sem("gbs_ok")
        row_in = [sem("row_in0"), sem("row_in1")]
        row_free, picked, s_ready, z_ready, p_ready = (
            sem(s) for s in ("row_free", "picked", "s_ready", "z_ready", "p_ready"))
        prep = sem("prep")
        e_act, e_pool, tp_ready, tp_out, mm_done, es_acc = (
            sem(s) for s in ("e_act", "e_pool", "tp_ready", "tp_out", "mm_done", "es_acc"))
        rd_ok = sem("rd_ok")
        es_tp, es_T = sem("es_tp"), sem("es_T")
        x1_tp, x1_ok = sem("x1_tp"), sem("x1_ok")
        ld_slice, ld_hy = sem("ld_slice"), sem("ld_hy")
        hy_pe, hy_dve, hy_act = sem("hy_pe"), sem("hy_dve"), sem("hy_act")
        lg_mm, lg_max, lg_sub, lg_exp, lg_sum, sw_ok, sw_sum, sw_tp, sw_T, x2_mm, x2_ok, outb_ok = (
            sem(x) for x in ("lg_mm", "lg_max", "lg_sub", "lg_exp", "lg_sum", "sw_ok", "sw_sum", "sw_tp", "sw_T",
                             "x2_mm", "x2_ok", "outb_ok"))
        lg_in = sem("lg_in")
        ones_ok = sem("ones_ok")
        ld_moe, ld_exp = sem("ld_moe"), [sem("ld_exp0"), sem("ld_exp1")]
        hv_ok, sc_mm, sc_ok = sem("hv_ok"), sem("sc_mm"), sem("sc_ok")
        row2_in = [sem(f"row2_in{u}") for u in range(2)]
        g_prod, g_mask, g_min, g_score, g_exp, g_tp, g_out, g_mm, g_den, x3_ok = (
            sem("g_" + x) for x in ("prod", "mask", "min", "score", "exp", "tp", "out", "mm", "den", "x3_ok"))
        r_mm, r_dlt, r_exp, r_w, r_tp, r_wT, b2_mm, b2_ok = (
            sem(x) for x in ("r_mm", "r_dlt", "r_exp", "r_w", "r_tp", "r_wT", "b2_mm", "b2_ok"))
        up_mm, gelu_ok, down_mm, acc_ok = sem("up_mm"), sem("gelu_ok"), sem("down_mm"), sem("acc_ok")

        HY_LOADS = ((in_wT, "in_wT"), (wfxT, "wfxT"), (bfx, "bfx"), (cw, "cw"), (cb, "cb"), (dtb, "dtb"), (alog, "alog"),
                    (m_rs, "m_rs"), (m_rt, "m_rt"), (m_st, "m_st"), (outb, "outb"), (fcDT, "fcDT"), (dcol, "dcol"),
                    (nwcol, "nwcol"), (outT, "outT"), (outwT, "outwT"))

        MOE_LOADS = ((wr, "Wr"), (hv, "hv"), (gamma, "gamma"), (beta, "beta"), (b1, "b1"), (b2[0:EXPERTS, :], "b2"),
                     (br, "br"), (prio, "prio"))

        loop_waits = sem("loop_waits")

        def waited(eng):
            eng.sem_inc(loop_waits, 1)

        block = ctx.enter_context(nc.Block())

        @block.sync
        def _(sp):
            sp.dma_start(xr[:, :, :], a["x"].rearrange("(t p) d -> p t d", p=P)).then_inc(ld_x, 16)
            sp.dma_start(ident[:, :], a["ident"]).then_inc(ld_c, 16)
            sp.dma_start(noteye[:, :], a["noteye"]).then_inc(ld_c, 16)
            sp.dma_start(gatWT, a["gat_WT"]).then_inc(ld_gat, 16)
            sp.dma_start(gatA, a["gat_a"]).then_inc(ld_gat, 16)
            sp.dma_start(gatW, a["gat_W"]).then_inc(ld_gat, 16)
            sp.dma_start(sel[0:96, :, :], a["sel"]).then_inc(ld_gat, 16)
            for j in range(NT):
                if j >= 3:
                    sp.wait_ge(aT_used, j - 2)
                sp.dma_start(aT[j % 3], a["adjT"][j * P:(j + 1) * P, :]).then_inc(aT_in[j % 3], 16)
                if j == 2:
                    for k in range(4):
                        sp.dma_start(WT[k], a["gru_WT"][k]).then_inc(ld_gru, 16)
                    sp.dma_start(gb, a["gru_b"]).then_inc(ld_gru, 16)
                    sp.dma_start(diag, a["diag"]).then_inc(ld_gru, 16)

            def rows(t, u, i):
                reached(sp, p_ready, 3 * (t - 1))
                sp.dma_start(arow[:, u, :], a["adj_t"][t, :, :] if isinstance(t, int) else
                             a["adj_t"][bass.ds(t, 1), :, :].rearrange("a p n -> (a p) n")).then_inc(row_in[u], 16)
            rows(0, 0, 0)
            rows(1, 1, 0)
            with sp.Fori(1, NT // 2) as i:
                for u in range(2):
                    rows(2 * i + u, u, i)

            sp.wait_ge(es_T, NT)
            for to, name in ((wx[0:64, :, :], "wx"), (wsT[0:64, :], "wsT"), (bx[0:64, :], "bx"), (bsl, "b_slice"),
                             (temp, "temp")):
                sp.dma_start(to, a[name]).then_inc(ld_slice, 16)
            for to, name in HY_LOADS:
                sp.dma_start(to, a[name]).then_inc(ld_hy, 16)

            def rows2(t, u, i):
                reached(sp, g_prod, t - 1)
                reached(sp, g_mask, t - 1)
                sp.dma_start(arow[:, u, :], a["adj_t"][t, :, :] if isinstance(t, int) else
                             a["adj_t"][bass.ds(t, 1), :, :].rearrange("a p n -> (a p) n")).then_inc(row2_in[u], 16)
            rows2(0, 0, 0)
            rows2(1, 1, 0)
            sp.wait_ge(x1_tp, NT)
            for to, name in MOE_LOADS:
                sp.dma_start(to, a[name]).then_inc(ld_moe, 16)

            def expert(e, u):
                reached(sp, down_mm, 4 * (e - 1))
                for to, name in ((wexp[u][0], "W1"), (wexp[u][1], "W2")):
                    src = a[name][e] if isinstance(e, int) else a[name][bass.ds(e, 1)].rearrange(
                        "a p n -> (a p) n" if name == "W1" else "a p c n -> (a p) c n")
                    sp.dma_start(to, src).then_inc(ld_exp[u], 16)
            expert(0, 0)
            expert(1, 1)
            with sp.Fori(1, NT // 2) as i:
                for u in range(2):
                    rows2(2 * i + u, u, i)
            with sp.Fori(1, EXPERTS // 2) as i:
                for u in range(2):
                    expert(2 * i + u, u)
            for q in range(NC):
                sp.wait_ge(acc_ok, NC * (EXPERTS - 1) + q + 1)
                sp.dma_start(out[q * CH:(q + 1) * CH, :].rearrange("(t p) d -> p t d", p=P),
                             xr[:, q * TC:(q + 1) * TC, :]).then_inc(out_stored, 16)
            sp.wait_ge(out_stored, 16 * NC)

        @block.scalar
        def _(act):
            def norm_std(n):
                act.wait_ge(ln_stats, n + 1)
                act.activation(std, mv[:, :, 1], ACT.Sqrt, bias=eps_col[:, 0:1]).then_inc(ln_std, 1)

            def norm_T(n, banks):
                if n == 3:
                    act.wait_ge(ld_moe, 16 * len(MOE_LOADS))
                for g in range(NC):
                    act.wait_ge(ln_tp, n * NC + g + 1)
                    if n == 3:
                        act.activation(hT[:, g * CH:(g + 1) * CH], ps[:, banks[g], :], ACT.Identity,
                                       scale=gamma, bias=beta).then_inc(ln_hT, 1)
                        continue
                    act.activation(hT[:, g * CH:(g + 1) * CH], ps[:, banks[g], :], ACT.Copy).then_inc(ln_hT, 1)

            norm_std(0)
            norm_T(0, (0, 1, 2, 3))
            for j in range(NT):
                act.wait_ge(hw_mm, j + 1)
                act.activation(hW[:, j, :], ps[:, 4 + j % 4, 0:HEADS * D], ACT.Copy).then_inc(hw_sb, 1)
            act.wait_ge(aT_used, NT)
            for g in range(NC):
                act.activation(mres[0:96, g * CH:(g + 1) * CH], ps[0:96, 4 + g, :], ACT.Copy).then_inc(mres_sb, 1)
                act.activation(nsT[:, g * CH:(g + 1) * CH], ps[:, g, :], ACT.Copy).then_inc(ns_sb, 1)
            for n in range(NS * NC):
                act.wait_ge(bc_mm, n + 1)
                act.activation(eb[:, n // NC, (n % NC) * CH:(n % NC + 1) * CH], ps[:, n % 4, :], ACT.Copy,
                               scale=-1.0).then_inc(bc_sb, 1)

            def gru(n):
                act.wait_ge(gbs_ok, 1)
                for q in range(NC):
                    u, c = q % 2, n * NC + q
                    b = GRU_BANK(q)
                    act.wait_ge(gru_mm, 4 * c + 1)
                    if q >= 2:
                        act.wait_ge(gru_out, c - 1)
                    act.activation(gr[u], ps[:, b, :], ACT.Sigmoid, bias=gbs[:, n, 0:1]).then_inc(gru_r, 1)
                    act.wait_ge(gru_mm, 4 * c + 2)
                    act.activation(gz[u], ps[:, b + 1, :], ACT.Sigmoid, bias=gbs[:, n, 1:2]).then_inc(gru_z, 1)
                    act.wait_ge(gru_t, c + 1)
                    act.activation(gt[u], gt[u], ACT.Tanh, bias=gb[:, 2 * n, 2:3]).then_inc(gru_n, 1)

            gru(0)

            def e_copy(i, kk):
                h, s = kk % 3, kk % RING
                if h < 2:
                    k = 6 * i + kk
                    if not isinstance(i, int) or k >= 6:
                        act.wait_ge(tp_ready, 4 * (k - 5))
                    else:
                        act.wait_ge(eb_ok, h + 1)
                    act.activation(ring[:, s, :], eb[:, h, :], ACT.Copy).then_inc(e_act, 1)

            def exps(i, kk):
                k, s = 6 * i + kk, kk % RING
                act.wait_ge(s_ready, k + 1)
                act.activation(ring[:, s, :], ring[:, s, :], ACT.Exp, bias=mn[:, s:s + 1], scale=-1.0,
                               accum_out=den[:, s:s + 1]).then_inc(z_ready, 1)

            def evac(i, kk, banks):
                k = 6 * i + kk
                for b in banks:
                    if b == 0:
                        reached(act, mm_done, k - 1)
                    act.wait_ge(tp_ready, 4 * k + b + 1)
                    act.activation(pat[:, kk % 2, b * CH:(b + 1) * CH], ps[:, b, :], ACT.Copy).then_inc(tp_out, 1)

            def es_out(t, u):
                act.wait_ge(es_tp, t + 1)
                waited(act)
                act.activation(esT[:, bass.ds(t * P, P)], ps[:, 6 + u, 0:P], ACT.Copy,
                               scale=1.0 / HEADS).then_inc(es_T, 1)

            def steps(i, first=False, last=False):
                for kk in range(6):
                    if kk % 3 == 0 and not first:
                        es_out(2 * i + kk // 3 - 2, kk // 3)
                    evac(i, kk, (0, 1))
                    if not (last and kk + 2 >= 6):
                        exps(i, kk + 2)
                    evac(i, kk, (2, 3))
                    if not (last and kk + 4 >= 6):
                        e_copy(i, kk + 4)

            act.wait_ge(gru_out, NC)
            for kk in range(4):
                e_copy(0, kk)
            exps(0, 0)
            exps(0, 1)
            steps(0, first=True)
            with act.Fori(1, NT // 2 - 1) as i:
                steps(i)
            steps(NT // 2 - 1, last=True)
            es_out(NT - 2, 0)
            es_out(NT - 1, 1)
            gru(1)

            norm_std(1)
            norm_T(1, (0, 1, 2, 3))

            def sw_out(t):
                act.wait_ge(sw_tp, t + 1)
                act.activation(swT[:, :, t * P:(t + 1) * P], ps[:, t % 2, :].rearrange("p (m n) -> p m n", m=CB),
                               ACT.Copy).then_inc(sw_T, 1)

            for t in range(NT):
                act.wait_ge(lg_sub, t + 1)
                act.activation(sw[t % 8], sw[t % 8], ACT.Exp).then_inc(lg_exp, 1)
                if t >= 3:
                    sw_out(t - 3)
            for t in range(NT - 3, NT):
                sw_out(t)

            def hyd(name, ins):
                ins.then_inc(hy_act, 1)
                act.wait_ge(hy_act, HY_ACT[name])

            act.wait_ge(ld_hy, 16 * len(HY_LOADS))
            hyd("rate", act.activation(rate, alog, ACT.Exp))
            act.wait_ge(hy_pe, HY_PE["zx"])
            hyd("z_copy", act.activation(zz, ps[:, 1, 0:CB * G].rearrange("p (k g) -> p k g", k=CB), ACT.Copy))
            act.wait_ge(hy_dve, HY_DVE["dt_nabs"])
            hyd("dt_exp", act.activation(dt_s[2], dt_s[1], ACT.Exp))
            hyd("dt_ln", act.activation(dt_s[3], dt_s[2], ACT.Ln, bias=1.0))
            act.wait_ge(hy_dve, HY_DVE["conv_b"])
            hyd("conv_exp", act.activation(cvt, cva, ACT.Exp, scale=-1.0))
            act.wait_ge(hy_pe, HY_PE["decay"])
            hyd("decay_exp", act.activation(dec, ps[:, 5, :].rearrange("p (h t) -> p h t", h=SLOPES), ACT.Exp))
            act.wait_ge(hy_pe, HY_PE["x_rows"])
            hyd("x_rows", act.activation(x2, ps[:, 4, :], ACT.Copy))
            hyd("z_exp", act.activation(z1, zz, ACT.Exp, scale=-1.0))
            act.wait_ge(hy_pe, HY_PE["power"])
            hyd("rms_std", act.activation(rms, ps[:, 2, 0:G], ACT.Sqrt, scale=1.0 / DI, bias=eps_col[:, 0:1]))
            act.wait_ge(hy_pe, HY_PE["value"])
            hyd("value", act.activation(val, ps[:, 4, :].rearrange("p (m d) -> p m d", m=CB), ACT.Copy))

            norm_std(2)
            norm_T(2, (4, 5, 6, 7))
            for g in range(NC):
                act.wait_ge(sc_mm, g + 1)
                act.activation(sbn[:, g * CH:(g + 1) * CH], ps[:, g, :], ACT.Copy, scale=-1.0).then_inc(sc_ok, 1)

            def g_exps(i, kk):
                k = 4 * i + kk
                act.wait_ge(g_score, k + 1)
                reached(act, g_den, 2 * k - 7)
                act.activation(ring[:, kk % 4, :], ring[:, kk % 4, :], ACT.Exp, bias=mn[:, kk % 4:kk % 4 + 1], scale=-1.0,
                               accum_out=den[:, kk % 4:kk % 4 + 1]).then_inc(g_exp, 1)

            def g_evac(i, kk, banks):
                k = 4 * i + kk
                for b in banks:
                    if b == 0:
                        reached(act, g_mm, k - 1)
                    act.wait_ge(g_tp, 4 * k + b + 1)
                    act.activation(pat[:, kk % 2, b * CH:(b + 1) * CH], ps[:, b, :], ACT.Copy).then_inc(g_out, 1)

            def g_steps(i, last=False):
                for kk in range(4):
                    g_evac(i, kk, (0, 1))
                    if not (last and kk + 2 >= 4):
                        g_exps(i, kk + 2)
                    g_evac(i, kk, (2, 3))

            g_exps(0, 0)
            g_exps(0, 1)
            g_steps(0)
            with act.Fori(1, NT // 4 - 1) as i:
                g_steps(i)
            g_steps(NT // 4 - 1, last=True)

            norm_std(3)
            norm_T(3, (4, 5, 6, 7))
            act.wait_ge(r_dlt, 1)
            act.activation(ew, v2, ACT.Exp).then_inc(r_exp, 1)
            for g in range(NC):
                act.wait_ge(r_tp, g + 1)
                act.activation(wT[:, g * CH:(g + 1) * CH], ps[0:EXPERTS, g, :], ACT.Copy).then_inc(r_wT, 1)

            def gelus(i, v, first=False):
                for q in range(NC):
                    st = 8 * i + 4 * v + q
                    if not (first and st < 2):
                        act.wait_ge(down_mm, st - 1)
                    for c in range(HC):
                        act.wait_ge(up_mm, HC * st + c + 1)
                        waited(act)
                        act.activation(hid[:, q % 2, c, :], ps[:, 2 * (q % 2) + c, :], ACT.Gelu,
                                       bias=b1[:, 2 * i + v, c:c + 1] if isinstance(i, int) else
                                       b1[:, bass.ds(2 * i + v, 1), c]).then_inc(gelu_ok, 1)

            gelus(0, 0, first=True)
            gelus(0, 1)
            with act.Fori(1, EXPERTS // 2) as i:
                gelus(i, 0)
                gelus(i, 1)

        @block.vector
        def _(dve):
            count = [0]

            def link(ins):
                count[0] += 1
                ins.then_inc(dve_seq, 1)
                dve.wait_ge(dve_seq, count[0])

            def norm(n, rows_ready):
                for t in range(NT):
                    rows_ready(t)
                    ins = dve.bn_stats(st6[:, t, :], xr[:, t, :])
                    if t < NT - 1:
                        ins.then_inc(dve_seq, 1)
                        count[0] += 1
                    else:
                        link(ins)
                for t in range(NT):
                    ins = dve.bn_aggr(mv[:, t, :], st6[:, t, :])
                ins.then_inc(ln_stats, 1)
                dve.wait_ge(ln_std, n + 1)
                dve.reciprocal(rstd, std).then_inc(ln_rstd, 1)
                dve.wait_ge(ln_rstd, n + 1)
                for t in range(NT):
                    dve.tensor_scalar(hrow[:, t, :], xr[:, t, :], mv[:, t, 0:1], rstd[:, t:t + 1],
                                      ALU.subtract, ALU.mult).then_inc(ln_row, 1)

            dve.memset(eps_col[:, :], EPS)
            link(dve.memset(parts, 0.0))
            dve.wait_ge(ld_x, 16)
            norm(0, lambda t: None)
            dve.wait_ge(wa_mm, 1)
            dve.tensor_copy(wa, ps[:, 7, 0:NS]).then_inc(wa_sb, 1)
            dve.wait_ge(u_mm, 1)
            u_ps = ps[:, 6, 0:NT * NS].rearrange("p (t q) -> p t q", t=NT)
            swap = (slice(HEADS, NS), slice(0, HEADS))

            def part(c, src):
                dve.tensor_copy(parts[:, 0, :, 32 * c:32 * c + NS], src)
                dve.tensor_copy(parts[:, 1, :, 32 * c:32 * c + HEADS], src[:, :, swap[0]])
                return dve.tensor_copy(parts[:, 1, :, 32 * c + HEADS:32 * c + NS], src[:, :, swap[1]])

            link(dve.tensor_copy(uu[0], u_ps))
            link(part(0, uu[0]))
            link(dve.tensor_tensor(uu[1], uu[0], parts[:, 0, :, 0:NS], ALU.subtract))
            link(part(1, uu[1]))
            link(dve.tensor_tensor(uu[2], uu[1], parts[:, 0, :, 32:32 + NS], ALU.subtract))
            part(2, uu[2]).then_inc(parts_ok, 1)
            dve.wait_ge(ld_c, 32)
            for j in range(NT):
                dve.wait_ge(aT_in[j % 3], 16 * (j // 3 + 1))
                blk = aT[j % 3][:, j * P:(j + 1) * P]
                link(dve.tensor_tensor(blk, blk, noteye[:, :], ALU.mult))
                if j >= 2:
                    dve.wait_ge(aT_used, j - 1)
                dve.tensor_scalar(masks[:, j % 2, 0, :], aT[j % 3], 0.0, None, ALU.is_gt)
                dve.tensor_scalar(masks[:, j % 2, 1, :], aT[j % 3], 0.0, None, ALU.is_lt).then_inc(masks_ok, 1)
            for q in range(NS):
                dve.wait_ge(bc_sb, NC * (q + 1))
                dve.scalar_tensor_tensor(eb[:, q, :], eb[:, q, :], GAT_ALPHA, eb[:, q, :],
                                         ALU.mult, ALU.min).then_inc(eb_ok, 1)
            dve.wait_ge(ld_gru, 96)
            dve.tensor_tensor(gbs, gb[:, 0:4:2, :], gb[:, 1:4:2, :], ALU.add).then_inc(gbs_ok, 1)

            def gru(n):
                for q in range(NC):
                    u, c = q % 2, n * NC + q
                    b = GRU_BANK(q)
                    dve.wait_ge(gru_r, c + 1)
                    dve.wait_ge(gru_mm, 4 * c + 3)
                    if q >= 2:
                        dve.wait_ge(gru_out, c - 1)
                    link(dve.scalar_tensor_tensor(gt[u], ps[:, b + 2, :], gb[:, 2 * n + 1, 2:3], gr[u],
                                                  ALU.add, ALU.mult))
                    dve.wait_ge(gru_mm, 4 * c + 4)
                    dve.tensor_tensor(gt[u], gt[u], ps[:, b + 3, :], ALU.add).then_inc(gru_t, 1)

            gru(0)

            def tile_prep(i, u):
                t = 2 * i + u
                dve.wait_ge(row_in[u], 16 * (i + 1))
                blk = arow[:, u, bass.ds(t * P, P)]
                dve.tensor_tensor(blk, blk, noteye[:, :], ALU.mult).then_inc(row_free, 1)
                dve.wait_ge(row_free, t + 1)
                dve.tensor_scalar(nb[:, :], arow[:, u, :], 0.0, NEG, ALU.is_equal, ALU.mult)
                dve.tensor_scalar(mneg[:, :], arow[:, u, :], 0.0, None, ALU.is_lt).then_inc(prep, 1)
                dve.wait_ge(prep, t + 1)

            def score(i, kk):
                h, s, k = kk % 3, kk % RING, 6 * i + kk
                if h < 2:
                    dve.wait_ge(e_act, 2 * (2 * i + kk // 3) + h + 1)
                else:
                    dve.wait_ge(e_pool, 2 * i + kk // 3 + 1)
                waited(dve)
                dve.copy_predicated(ring[:, s, :], mneg[:, :], eb[:, HEADS + h, :]).then_inc(picked, 1)
                dve.wait_ge(picked, k + 1)
                waited(dve)
                dve.tensor_tensor_reduce(ring[:, s, :], ring[:, s, :], nb[:, :], 1.0, FAR, ALU.add, ALU.min,
                                         mn[:, s:s + 1]).then_inc(s_ready, 1)

            def combine(i, kk):
                kk, i = (kk, i) if kk >= 0 else (kk + 6, i - 1)
                h, s, k, u = kk % 3, kk % RING, 6 * i + kk, kk // 3
                dve.wait_ge(z_ready, k + 1)
                dve.reciprocal(rden[:, s:s + 1], den[:, s:s + 1]).then_inc(rd_ok, 1)
                dve.wait_ge(rd_ok, k + 1)
                dve.wait_ge(mm_done, k + 1)
                o = ps[:, 4 + kk % 2, 0:D]
                if h == 0:
                    reached(dve, es_tp, 2 * i + u - 1)
                    dve.tensor_scalar(esb[:, u, :], o, rden[:, s:s + 1], None, ALU.mult).then_inc(es_acc, 1)
                else:
                    dve.wait_ge(es_acc, k)
                    dve.scalar_tensor_tensor(esb[:, u, :], o, rden[:, s:s + 1], esb[:, u, :],
                                             ALU.mult, ALU.add).then_inc(es_acc, 1)

            def steps(i, first=False):
                for kk in range(6):
                    if kk % 3 == 0:
                        tile_prep(i, kk // 3)
                    score(i, kk)
                    if not (first and kk < 4):
                        combine(i, kk - 4)

            dve.wait_ge(eb_ok, NS)
            steps(0, first=True)
            with dve.Fori(1, NT // 2) as i:
                steps(i)
            for kk in range(2, 6):
                combine(NT // 2 - 1, kk)

            gru(1)
            for t in range(NT):
                q = t // TC
                dve.wait_ge(x1_tp, (q + 1) * TC)
                dve.scalar_tensor_tensor(xr[:, t, :], ps[:, X1_BANK(q), (t % TC) * P:(t % TC + 1) * P],
                                         diag[:, t:t + 1], xr[:, t, :], ALU.mult, ALU.add).then_inc(x1_ok, 1)

            def hyd(name, ins):
                ins.then_inc(hy_dve, 1)
                dve.wait_ge(hy_dve, HY_DVE[name])

            dve.wait_ge(ld_slice, 80)
            hyd("bias_cols", dve.tensor_copy(bx_cols[0:64, :, :], bx[0:64, :].unsqueeze(2).broadcast_to([64, SLOPES, P])))
            hyd("inv_temp", dve.tensor_scalar(temp, temp, 1e-6, None, ALU.max))
            link(dve.reciprocal(temp, temp))
            by_head = lambda v: v.rearrange("p (h g) -> p h g", h=SLOPES)
            spread = lambda v: v.unsqueeze(2).broadcast_to([P, SLOPES, G])
            dve.wait_ge(hy_pe, HY_PE["slice_w"])
            hyd("slice_w", dve.tensor_tensor(by_head(w_slice), by_head(ps[:, 4, :]), spread(temp), ALU.mult))
            dve.wait_ge(hy_pe, HY_PE["slice_b"])
            hyd("slice_b1", dve.tensor_tensor(by_head(b_slice), by_head(ps[:, 5, :]),
                                              bsl.unsqueeze(1).broadcast_to([P, SLOPES, G]), ALU.add))
            hyd("slice_b", dve.tensor_tensor(by_head(b_slice), by_head(b_slice), spread(temp), ALU.mult))
            norm(1, lambda t: None)
            dve.memset(ones, 1.0).then_inc(ones_ok, 1)

            def slice_in(t):
                dve.wait_ge(lg_mm, t + 1)
                if t >= 8:
                    dve.wait_ge(sw_tp, t - 7)
                    dve.wait_ge(sw_sum, t - 7)
                dve.tensor_tensor(sw[t % 8], ps[:, 4 + t % 2, :], b_slice, ALU.add).then_inc(lg_in, 1)
                dve.wait_ge(lg_in, t + 1)
                dve.tensor_reduce(mx8[t % 4], by_head(sw[t % 8]), AX.X, ALU.max).then_inc(lg_max, 1)

            def slice_out(t):
                dve.wait_ge(lg_exp, t + 1)
                link(dve.tensor_reduce(rs8[t % 4], by_head(sw[t % 8]), AX.X, ALU.add))
                link(dve.reciprocal(rs8[t % 4], rs8[t % 4]))
                dve.tensor_tensor(by_head(sw[t % 8]), by_head(sw[t % 8]), spread(rs8[t % 4]), ALU.mult).then_inc(sw_ok, 1)

            for t in range(NT):
                slice_in(t)
                if t >= 2:
                    slice_out(t - 2)
            slice_out(NT - 2)
            slice_out(NT - 1)

            dve.wait_ge(ld_hy, 16 * len(HY_LOADS))
            dve.wait_ge(hy_pe, HY_PE["snorm"])
            snorm = ps[:, 7, :]
            hyd("snorm_eps", dve.tensor_scalar(rsn, snorm, 1e-5, None, ALU.add))
            hyd("snorm_inv", dve.reciprocal(rsn, rsn))
            hyd("tok_w", dve.tensor_tensor(tok_n, ps[:, 6, :], rsn, ALU.mult))
            hyd("snorm_n", dve.tensor_tensor(sn_n, snorm, rsn, ALU.mult))
            halves = ((slice(0, 64), slice(0, 64)), (slice(64, 128), slice(64, 128)))
            snv = sn_n.rearrange("p (m g) -> p m g", m=CB)
            for n, (r, g) in enumerate(halves):
                hyd(f"tok_b{n}", dve.tensor_tensor(tokb[r, :, :], snv[r, :, g], bfx[r, :].unsqueeze(2).broadcast_to([64, CB, G]),
                                                   ALU.mult))
            dve.wait_ge(hy_pe, HY_PE["tokens"])
            tps = ps[:, 0, :].rearrange("p (m g) -> p m g", m=CB)
            for n, (r, g) in enumerate(halves):
                hyd(f"tok{n}", dve.tensor_tensor(tokT[r, :, :], tps[r, :, g], tokb[r, :, :], ALU.add))
            link(dve.memset(xp, 0.0))
            link(dve.memset(xs, 0.0))
            link(dve.memset(bd, 0.0))
            dve.wait_ge(hy_pe, HY_PE["bcdt"])
            dve.wait_ge(hy_act, HY_ACT["z_copy"])
            link(dve.tensor_copy(xp[:, 0:CB, 2:PADW], ps[:, 1, CB * G:2 * CB * G].rearrange("p (k g) -> p k g", k=CB)))
            hyd("pad", dve.tensor_copy(xp[0:64, CB:6, 2:PADW], ps[0:64, 2, 0:2 * G].rearrange("p (k g) -> p k g", k=2)))
            hyd("dt_in", dve.tensor_tensor(dt_s[0], ps[:, 3, 0:SLOPES], dtb, ALU.add))
            hyd("dt_neg", dve.tensor_scalar(dt_s[1], dt_s[0], -1.0, None, ALU.mult))
            hyd("dt_nabs", dve.tensor_tensor(dt_s[1], dt_s[1], dt_s[0], ALU.min))
            tap = lambda k: cw[:, :, k].unsqueeze(2).broadcast_to([P, 6, G])
            hyd("conv0", dve.tensor_tensor(cva, xp[:, :, 0:G], tap(0), ALU.mult))
            hyd("conv1", dve.tensor_tensor(cvt, xp[:, :, 1:G + 1], tap(1), ALU.mult))
            hyd("conv01", dve.tensor_tensor(cva, cva, cvt, ALU.add))
            hyd("conv2", dve.tensor_tensor(cvt, xp[:, :, 2:G + 2], tap(2), ALU.mult))
            hyd("conv012", dve.tensor_tensor(cva, cva, cvt, ALU.add))
            hyd("conv_b", dve.tensor_tensor(cva, cva, cb.unsqueeze(2).broadcast_to([P, 6, G]), ALU.add))
            dve.wait_ge(hy_act, HY_ACT["dt_ln"])
            hyd("dt", dve.scalar_tensor_tensor(dt_s[4], dt_s[0], 0.0, dt_s[3], ALU.max, ALU.add))
            hyd("decay_rate", dve.scalar_tensor_tensor(dt_s[0], dt_s[4], -1.0, rate, ALU.mult, ALU.mult))
            hyd("decay_in", dve.tensor_tensor(dec, spread(dt_s[0]), m_rt.unsqueeze(1).broadcast_to([P, SLOPES, G]), ALU.mult))
            dve.wait_ge(hy_act, HY_ACT["conv_exp"])
            hyd("silu_den", dve.tensor_scalar(cvt, cvt, 1.0, None, ALU.add))
            hyd("silu_inv", dve.reciprocal(cvt, cvt))
            hyd("xbc", dve.tensor_tensor(xs[:, :, 1:G + 1], cva, cvt, ALU.mult))
            hyd("x_twice", dve.tensor_copy(xd, xs[:, 0:CB, 1:G + 1].unsqueeze(2).broadcast_to([P, CB, 2, G])))
            dve.wait_ge(hy_pe, HY_PE["gram"])
            hyd("gram", dve.tensor_tensor(gramm, ps[:, 3, G:2 * G], m_st, ALU.mult))
            dve.wait_ge(hy_act, HY_ACT["decay_exp"])
            hyd("weight_dt", dve.tensor_tensor(dec, dec, spread(dt_s[4]), ALU.mult))
            hyd("weight", dve.tensor_tensor(dec, dec, gramm.unsqueeze(1).broadcast_to([P, SLOPES, G]), ALU.mult))
            dve.wait_ge(hy_act, HY_ACT["z_exp"])
            hyd("z_den", dve.tensor_scalar(z1, z1, 1.0, None, ALU.add))
            hyd("z_inv", dve.reciprocal(z1, z1))
            hyd("z", dve.tensor_tensor(z1, z1, zz, ALU.mult))
            dve.wait_ge(hy_pe, HY_PE["skip"])
            skp = ps[:, 7, 0:CB * G].rearrange("p (k g) -> p k g", k=CB)
            cols = lambda v: v.unsqueeze(2).broadcast_to([P, CB, G])
            hyd("skip_d", dve.tensor_tensor(y1, skp, cols(dcol), ALU.add))
            hyd("skip", dve.tensor_tensor(y1, y1, xs[:, 0:CB, 1:G + 1], ALU.mult))
            dve.wait_ge(hy_pe, HY_PE["y"])
            hyd("y", dve.tensor_tensor(y1, ps[:, 6, 0:CB * G].rearrange("p (k g) -> p k g", k=CB), y1, ALU.add))
            hyd("yg", dve.tensor_tensor(y1, y1, z1, ALU.mult))
            hyd("sq", dve.tensor_tensor(ysq, y1, y1, ALU.mult))
            dve.wait_ge(hy_act, HY_ACT["rms_std"])
            hyd("rms", dve.reciprocal(rms, rms))
            hyd("yn", dve.tensor_tensor(y1, y1, rms.unsqueeze(1).broadcast_to([P, CB, G]), ALU.mult))
            hyd("ynw", dve.tensor_tensor(y1, y1, cols(nwcol), ALU.mult))
            dve.wait_ge(hy_pe, HY_PE["out"])
            ops_ = ps[:, 3, 0:CB * G].rearrange("p (k g) -> p k g", k=CB)
            for n, (r, g) in enumerate(halves):
                hyd(f"ot{n}", dve.tensor_copy(bd[r, :, g], ops_[r, :, :]))
            for q in range(NC):
                dve.wait_ge(x2_mm, q + 1)
                if q == 0:
                    dve.wait_ge(outb_ok, 1)
                rows_ = xr[:, q * TC:(q + 1) * TC, :]
                dve.tensor_tensor(rows_, ps[:, q % 4, :].rearrange("p (t d) -> p t d", t=TC), rows_,
                                  ALU.add).then_inc(x2_ok, 1)

            norm(2, lambda t: dve.wait_ge(x2_ok, t // TC + 1))
            dve.wait_ge(ld_moe, 16 * len(MOE_LOADS))
            dve.tensor_copy(hv_cols, hv.broadcast_to([P, D])).then_inc(hv_ok, 1)

            def g_scores(i, kk):
                kk, i = (kk, i) if kk < 4 else (kk - 4, i + 1)
                k, u, s = 4 * i + kk, kk % 2, kk % 4
                dve.wait_ge(row2_in[u], 16 * (2 * i + kk // 2 + 1))
                dve.tensor_scalar(nb[:, :], arow[:, u, :], 0.0, FLOOR, ALU.is_equal, ALU.mult).then_inc(g_mask, 1)
                dve.wait_ge(g_mask, k + 1)
                dve.wait_ge(g_prod, k + 1)
                waited(dve)
                dve.tensor_tensor_reduce(ring[:, s, :], ring[:, s, :], nb[:, :], 1.0, FAR, ALU.add, ALU.min,
                                         mn[:, s:s + 1]).then_inc(g_min, 1)
                dve.wait_ge(g_min, k + 1)
                dve.tensor_scalar(mn[:, s:s + 1], mn[:, s:s + 1], FLOOR / 2, None, ALU.min).then_inc(g_score, 1)

            def g_combine(i, kk):
                kk, i = (kk, i) if kk >= 0 else (kk + 4, i - 1)
                k, s = 4 * i + kk, kk % 4
                dve.wait_ge(g_exp, k + 1)
                dve.tensor_scalar(rden[:, s:s + 1], den[:, s:s + 1], 1e-30, None, ALU.max).then_inc(g_den, 1)
                dve.wait_ge(g_den, 2 * k + 1)
                dve.reciprocal(rden[:, s:s + 1], rden[:, s:s + 1]).then_inc(g_den, 1)
                dve.wait_ge(g_den, 2 * k + 2)
                dve.wait_ge(g_mm, k + 1)
                x = xr[:, k, :] if isinstance(k, int) else xr[:, bass.ds(k, 1), :].rearrange("p a d -> p (a d)")
                dve.scalar_tensor_tensor(x, ps[:, 4 + kk % 2, 0:D], rden[:, s:s + 1], x,
                                         ALU.mult, ALU.add).then_inc(x3_ok, 1)

            def g_steps(i, first=False, last=False):
                for kk in range(4):
                    if not (last and kk + 3 >= 4):
                        g_scores(i, kk + 3)
                    if not (first and kk < 1):
                        g_combine(i, kk - 1)

            for kk in range(3):
                g_scores(0, kk)
            g_steps(0, first=True)
            with dve.Fori(1, NT // 4 - 1) as i:
                g_steps(i)
            g_steps(NT // 4 - 1, last=True)
            g_combine(NT // 4 - 1, 3)

            norm(3, lambda t: dve.wait_ge(x3_ok, t + 1))
            by_node = lambda v: v.unsqueeze(2).broadcast_to([P, NT, EXPERTS])
            by_expert = lambda v: v.unsqueeze(1).broadcast_to([P, NT, EXPERTS])
            dve.wait_ge(r_mm, 1)
            link(dve.tensor_tensor(route, ps[:, 0, 0:NT * EXPERTS].rearrange("p (t e) -> p t e", t=NT), by_expert(br), ALU.add))
            for v, hot in ((v1, hot1), (v2, hot2)):
                link(dve.tensor_reduce(v, route, AX.X, ALU.max))
                link(dve.tensor_tensor(top, route, by_node(v), ALU.is_equal))
                link(dve.tensor_tensor(top, top, by_expert(prio), ALU.mult))
                link(dve.tensor_reduce(ky, top, AX.X, ALU.max))
                link(dve.tensor_tensor(hot, top, by_node(ky), ALU.is_equal))
                if hot is hot1:
                    link(dve.scalar_tensor_tensor(route, hot, -FAR, route, ALU.mult, ALU.add))
            dve.tensor_tensor(v2, v2, v1, ALU.subtract).then_inc(r_dlt, 1)
            dve.wait_ge(r_exp, 1)
            link(dve.tensor_scalar(w1, ew, 1.0, None, ALU.add))
            link(dve.reciprocal(w1, w1))
            link(dve.tensor_tensor(ew, ew, w1, ALU.mult))
            link(dve.tensor_tensor(hot1, hot1, by_node(w1), ALU.mult))
            link(dve.tensor_tensor(hot2, hot2, by_node(ew), ALU.mult))
            dve.tensor_tensor(wfull, hot1, hot2, ALU.add).then_inc(r_w, 1)
            for g in range(NC):
                dve.wait_ge(b2_mm, g + 1)
                rows_ = xr[:, g * TC:(g + 1) * TC, :]
                dve.tensor_tensor(rows_, ps[:, 4 + g, :].rearrange("p (t d) -> p t d", t=TC), rows_,
                                  ALU.add).then_inc(b2_ok, 1)

            def add_expert(i, v):
                for q in range(NC):
                    st = 8 * i + 4 * v + q
                    dve.wait_ge(down_mm, st + 1)
                    for j in range(TC):
                        t = q * TC + j
                        w = wfull[:, t, 2 * i + v:2 * i + v + 1] if isinstance(i, int) else wfull[:, t, bass.ds(2 * i + v, 1)]
                        ins = dve.scalar_tensor_tensor(xr[:, t, :], ps[:, 4 + q % 2, j * P:(j + 1) * P], w, xr[:, t, :],
                                                       ALU.mult, ALU.add)
                    ins.then_inc(acc_ok, 1)

            dve.wait_ge(b2_ok, NC)
            dve.wait_ge(r_w, 1)
            add_expert(0, 0)
            add_expert(0, 1)
            with dve.Fori(1, EXPERTS // 2) as i:
                add_expert(i, 0)
                add_expert(i, 1)

        @block.gpsimd
        def _(pool):
            count = [0]

            def link(ins):
                count[0] += 1
                ins.then_inc(gru_pool, 1)
                pool.wait_ge(gru_pool, count[0])

            def gru(n):
                for q in range(NC):
                    u, c = q % 2, n * NC + q
                    cols = slice(q * CH, (q + 1) * CH)
                    pool.wait_ge(gru_n, c + 1)
                    pool.wait_ge(gru_z, c + 1)
                    link(pool.tensor_tensor(gr[u], hT[:, cols], gt[u], ALU.subtract))
                    link(pool.tensor_tensor(gr[u], gr[u], gz[u], ALU.mult))
                    if n == 0:
                        pool.tensor_tensor(nsT[:, cols], gr[u], gt[u], ALU.add).then_inc(gru_out, 1)
                    else:
                        link(pool.tensor_tensor(gr[u], gr[u], gt[u], ALU.add))
                        pool.tensor_tensor(nsT[:, cols], nsT[:, cols], gr[u], ALU.add).then_inc(gru_out, 1)

            gru(0)

            def e_copy(i, kk):
                h, s = kk % 3, kk % RING
                if h == 2:
                    k = 6 * i + kk
                    if not isinstance(i, int) or k >= 6:
                        pool.wait_ge(tp_ready, 4 * (k - 5))
                    else:
                        pool.wait_ge(eb_ok, h + 1)
                    waited(pool)
                    pool.tensor_scalar(ring[:, s, :], eb[:, h, :], 1.0, 0.0, ALU.mult, ALU.add).then_inc(e_pool, 1)

            def weigh(i, kk):
                kk, i = (kk, i) if kk < 6 else (kk - 6, i + 1)
                s, k = kk % RING, 6 * i + kk
                pool.wait_ge(z_ready, k + 1)
                pool.tensor_tensor(ring[:, s, :], ring[:, s, :], arow[:, kk // 3, :], ALU.mult).then_inc(p_ready, 1)

            def steps(i, last=False):
                for kk in range(6):
                    if not (last and kk == 5):
                        weigh(i, kk + 1)
                    if not (last and kk + 4 >= 6):
                        e_copy(i, kk + 4)

            for kk in range(4):
                e_copy(0, kk)
            weigh(0, 0)
            steps(0)
            with pool.Fori(1, NT // 2 - 1) as i:
                steps(i)
            steps(NT // 2 - 1, last=True)
            gru(1)

            def slice_sum(t):
                pool.wait_ge(sw_ok, t + 1)
                if t == 0:
                    pool.tensor_copy(swsum, sw[0]).then_inc(sw_sum, 1)
                else:
                    pool.wait_ge(sw_sum, t)
                    pool.tensor_tensor(swsum, swsum, sw[t % 8], ALU.add).then_inc(sw_sum, 1)

            for t in range(NT):
                pool.wait_ge(lg_max, t + 1)
                v = sw[t % 8].rearrange("p (h g) -> p h g", h=SLOPES)
                pool.tensor_tensor(v, v, mx8[t % 4].unsqueeze(2).broadcast_to([P, SLOPES, G]),
                                   ALU.subtract).then_inc(lg_sub, 1)
                if t >= 3:
                    slice_sum(t - 3)
            for t in range(NT - 3, NT):
                slice_sum(t)
            pool.wait_ge(ld_hy, 16 * len(HY_LOADS))
            pool.wait_ge(ln_row, 2 * NT)
            pool.tensor_tensor(xr[:, :, :], xr[:, :, :], outb.unsqueeze(1).broadcast_to([P, NT, D]),
                               ALU.add).then_inc(outb_ok, 1)

            def product(i, kk):
                kk, i = (kk, i) if kk < 4 else (kk - 4, i + 1)
                k, u, s = 4 * i + kk, kk % 2, kk % 4
                pool.wait_ge(row2_in[u], 16 * (2 * i + kk // 2 + 1))
                reached(pool, g_tp, 4 * (k - 3))
                pool.tensor_tensor(ring[:, s, :], arow[:, u, :], sbn, ALU.mult).then_inc(g_prod, 1)

            pool.wait_ge(sc_ok, NC)
            for kk in range(4):
                product(0, kk)
            with pool.Fori(1, NT // 4) as i:
                for kk in range(4):
                    product(i, kk)

        @block.tensor
        def _(pe):
            def norm_T(n, banks):
                for t in range(NT):
                    if t == 0:
                        pe.wait_ge(ld_c, 32)
                    pe.wait_ge(ln_row, n * NT + t + 1)
                    ins = pe.transpose(ps[:, banks[t // TC], (t % TC) * P:(t % TC + 1) * P], hrow[:, t, :], ident[:, :])
                    if t % TC == TC - 1:
                        ins.then_inc(ln_tp, 1)

            norm_T(0, (0, 1, 2, 3))
            pe.wait_ge(ld_gat, 64)
            for h in range(HEADS):
                ins = pe.matmul(ps[:, 7, h:NS:HEADS], gatWT[:, h * D:(h + 1) * D], gatA[:, :, h], start=True, stop=True)
            ins.then_inc(wa_mm, 1)
            pe.wait_ge(wa_sb, 1)
            pe.wait_ge(ln_hT, NC)
            for t in range(NT):
                ins = pe.matmul(ps[:, 6, t * NS:(t + 1) * NS], hT[:, t * P:(t + 1) * P], wa, start=True, stop=True)
            ins.then_inc(u_mm, 1)
            for j in range(NT):
                if j in (2, 3):
                    pe.wait_ge(dve_seq, U_COPIED)
                if j >= 4:
                    pe.wait_ge(hw_sb, j - 3)
                pe.matmul(ps[:, 4 + j % 4, 0:HEADS * D], hT[:, j * P:(j + 1) * P], gatW,
                          start=True, stop=True).then_inc(hw_mm, 1)
            pe.wait_ge(parts_ok, 1)
            for j in range(NT):
                pe.wait_ge(masks_ok, j + 1)
                if j == 0:
                    pe.wait_ge(hw_sb, NT)
                for g in range(NC):
                    cols = slice(g * CH, (g + 1) * CH)
                    pe.matmul(ps[:, g, :], hrow[:, j, :], aT[j % 3][:, cols], start=(j == 0), stop=(j == NT - 1))
                for g in range(NC):
                    cols = slice(g * CH, (g + 1) * CH)
                    pe.matmul(ps[0:96, 4 + g, :], parts[:, 0, j, :], masks[:, j % 2, 0, cols],
                              start=(j == 0), stop=False)
                    ins = pe.matmul(ps[0:96, 4 + g, :], parts[:, 1, j, :], masks[:, j % 2, 1, cols],
                                    start=False, stop=(j == NT - 1))
                ins.then_inc(aT_used, 1)
            for n in range(NS * NC):
                g = n % NC
                if n < NC:
                    pe.wait_ge(mres_sb, g + 1)
                    pe.wait_ge(ns_sb, g + 1)
                else:
                    pe.wait_ge(bc_sb, n - 3)
                pe.matmul(ps[:, n % 4, :], sel[0:96, n // NC, :], mres[0:96, g * CH:(g + 1) * CH],
                          start=True, stop=True).then_inc(bc_mm, 1)

            def gru(n, srcT):
                for q in range(NC):
                    cols = slice(q * CH, (q + 1) * CH)
                    b = GRU_BANK(q)
                    c = n * NC + q
                    if n == 0:
                        if q == 0:
                            pe.wait_ge(ld_gru, 96)
                            pe.wait_ge(mres_sb, NC)
                        if q == 1:
                            pe.wait_ge(bc_sb, NS * NC)
                    if n == 1 and q == 0:
                        pe.wait_ge(es_T, NT)
                    if q >= 2:
                        pe.wait_ge(gru_z, c - 1)
                        pe.wait_ge(gru_t, c - 1)
                    for gate in range(2):
                        w = slice(gate * D, (gate + 1) * D)
                        pe.matmul(ps[:, b + gate, :], WT[2 * n][:, w], srcT[:, cols], start=True, stop=False)
                        pe.matmul(ps[:, b + gate, :], WT[2 * n + 1][:, w], hT[:, cols],
                                  start=False, stop=True).then_inc(gru_mm, 1)
                    w = slice(2 * D, 3 * D)
                    pe.matmul(ps[:, b + 2, :], WT[2 * n + 1][:, w], hT[:, cols], start=True, stop=True).then_inc(gru_mm, 1)
                    pe.matmul(ps[:, b + 3, :], WT[2 * n][:, w], srcT[:, cols], start=True, stop=True).then_inc(gru_mm, 1)

            gru(0, nsT)

            def turn(i, kk):
                kk, i = (kk, i) if kk < 6 else (kk - 6, i + 1)
                s, k = kk % RING, 6 * i + kk
                pe.wait_ge(p_ready, k + 1)
                for b in range(4):
                    reached(pe, tp_out, 4 * (k - 1) + b + 1)
                    for j in range(4):
                        c = (4 * b + j) * P
                        ins = pe.transpose(ps[:, b, j * P:(j + 1) * P], ring[:, s, c:c + P], ident[:, :])
                    ins.then_inc(tp_ready, 1)

            def attend(i, kk):
                h, k = kk % 3, 6 * i + kk
                pe.wait_ge(tp_out, 4 * (k + 1))
                reached(pe, es_acc, k - 1)
                for j in range(NT):
                    ins = pe.matmul(ps[:, 4 + kk % 2, 0:D], pat[:, kk % 2, j * P:(j + 1) * P],
                                    hW[:, j, h * D:(h + 1) * D], start=(j == 0), stop=(j == NT - 1))
                ins.then_inc(mm_done, 1)

            def es_turn(t, u):
                pe.wait_ge(es_acc, 3 * (t + 1))
                reached(pe, es_T, t - 1)
                pe.transpose(ps[:, 6 + u, 0:P], esb[:, u, :], ident[:, :]).then_inc(es_tp, 1)

            def steps(i, first=False, last=False):
                for kk in range(6):
                    if kk % 3 == 2 and not (first and kk == 2):
                        es_turn(2 * i + kk // 3 - 1, 1 - kk // 3)
                    if not (last and kk == 5):
                        turn(i, kk + 1)
                    attend(i, kk)

            pe.wait_ge(gru_t, NC)
            turn(0, 0)
            steps(0, first=True)
            with pe.Fori(1, NT // 2 - 1) as i:
                steps(i)
            steps(NT // 2 - 1, last=True)
            es_turn(NT - 1, 1)
            gru(1, esT)
            for t in range(NT):
                q = t // TC
                if t % TC == 0:
                    pe.wait_ge(gru_out, NC + q + 1)
                    if q == 0:
                        pe.wait_ge(gru_t, 2 * NC)
                        pe.wait_ge(gru_z, 2 * NC)
                pe.transpose(ps[:, X1_BANK(q), (t % TC) * P:(t % TC + 1) * P], nsT[:, t * P:(t + 1) * P],
                             ident[:, :]).then_inc(x1_tp, 1)
            pe.wait_ge(ld_slice, 80)
            for h in range(SLOPES):
                ins = pe.matmul(ps[:, 4, h * G:(h + 1) * G], wx[0:64, h, :], wsT[0:64, :], start=True, stop=True)
            ins.then_inc(hy_pe, 1)
            pe.wait_ge(hy_dve, HY_DVE["bias_cols"])
            for h in range(SLOPES):
                ins = pe.matmul(ps[:, 5, h * G:(h + 1) * G], bx_cols[0:64, h, :], wsT[0:64, :], start=True, stop=True)
            ins.then_inc(hy_pe, 1)
            norm_T(1, (0, 1, 2, 3))

            def logits(t):
                if t == 0:
                    pe.wait_ge(hy_dve, HY_DVE["slice_b"])
                if t % TC == 0:
                    pe.wait_ge(ln_hT, NC + t // TC + 1)
                if t >= 2:
                    pe.wait_ge(lg_in, t - 1)
                pe.matmul(ps[:, 4 + t % 2, :], hT[:, t * P:(t + 1) * P], w_slice, start=True, stop=True).then_inc(lg_mm, 1)

            def gather(t):
                pe.wait_ge(sw_ok, t + 1)
                if t == 0:
                    pe.wait_ge(ln_hT, 2 * NC)
                pe.matmul(ps[:, 6, :], hrow[:, t, :], sw[t % 8], start=(t == 0), stop=(t == NT - 1))
                if t >= 2:
                    pe.wait_ge(sw_T, t - 1)
                for m in range(CB):
                    ins = pe.transpose(ps[:, t % 2, m * P:(m + 1) * P], sw[t % 8][:, m * P:(m + 1) * P], ident[:, :])
                ins.then_inc(sw_tp, 1)

            for t in range(NT):
                logits(t)
                if t >= 3:
                    gather(t - 3)
            for t in range(NT - 3, NT):
                gather(t)

            pe.wait_ge(ones_ok, 1)
            pe.wait_ge(sw_sum, NT)
            pe.matmul(ps[:, 7, :], ones, swsum, start=True, stop=True).then_inc(hy_pe, 1)
            pe.wait_ge(hy_dve, HY_DVE["tok_w"])
            pe.wait_ge(sw_T, NT)
            for m in range(CB):
                ins = pe.matmul(ps[:, 0, m * P:(m + 1) * P], wfxT[:, m * P:(m + 1) * P], tok_n[:, m * P:(m + 1) * P],
                                start=True, stop=True)
            ins.then_inc(hy_pe, 1)
            pe.wait_ge(hy_dve, HY_DVE["tok1"])

            def project(o, w_of, x_of):
                for k in range(CB):
                    ins = pe.matmul(o, w_of(k), x_of(k), start=(k == 0), stop=(k == CB - 1))
                return ins

            for m in range(2 * CB):
                ins = project(ps[:, 1, m * G:(m + 1) * G], lambda k: in_wT[:, k, m * P:(m + 1) * P], lambda k: tokT[:, k, :])
            ins.then_inc(hy_pe, 1)
            for m in range(2):
                c = 2 * DI + m * G
                project(ps[0:64, 2, m * G:(m + 1) * G], lambda k: in_wT[:, k, c:c + G], lambda k: tokT[:, k, :])
            for v in range(2):
                c = 2 * DI + 2 * G + v * SLOPES
                ins = project(ps[64 * v:64 * v + 64, 3, 0:SLOPES], lambda k: tokT[:, k, :], lambda k: in_wT[:, k, c:c + SLOPES])
            ins.then_inc(hy_pe, 1)
            pe.wait_ge(hy_dve, HY_DVE["decay_in"])
            pe.matmul(ps[:, 5, :], m_rs, dec, start=True, stop=True).then_inc(hy_pe, 1)
            pe.wait_ge(hy_dve, HY_DVE["x_twice"])
            for v in range(2):
                ins = pe.matmul(ps[64 * v:64 * v + 64, 3, G:2 * G], xs[0:64, CB, 1:G + 1],
                                xs[0:64, CB + 1, 2 * v:2 * v + G], start=True, stop=True)
            ins.then_inc(hy_pe, 1)
            for m in range(CB):
                ins = pe.transpose(ps[:, 4, m * P:(m + 1) * P], xd[:, m, :, :].rearrange("p v g -> p (v g)"), ident[:, :])
            ins.then_inc(hy_pe, 1)
            for m in range(CB):
                ins = project(ps[:, 7, m * G:(m + 1) * G], lambda k: fcDT[:, k, m * P:(m + 1) * P],
                              lambda k: xs[:, k, 1:G + 1])
            ins.then_inc(hy_pe, 1)
            pe.wait_ge(hy_act, HY_ACT["x_rows"])
            pe.wait_ge(hy_dve, HY_DVE["weight"])
            for h in range(SLOPES):
                ins = pe.matmul(ps[64 * (h % 2):64 * (h % 2) + 64, 6, (h // 2) * G:(h // 2 + 1) * G],
                                x2[:, h * 64:(h + 1) * 64], dec[:, h, :], start=True, stop=True)
            ins.then_inc(hy_pe, 1)
            pe.wait_ge(hy_dve, HY_DVE["sq"])
            project(ps[:, 2, 0:G], lambda k: ones, lambda k: ysq[:, k, :]).then_inc(hy_pe, 1)
            pe.wait_ge(hy_dve, HY_DVE["ynw"])
            for m in range(CB):
                ins = project(ps[:, 3, m * G:(m + 1) * G], lambda k: outT[:, k, m * P:(m + 1) * P], lambda k: y1[:, k, :])
            ins.then_inc(hy_pe, 1)
            pe.wait_ge(hy_dve, HY_DVE["ot1"])
            for m in range(CB):
                ins = pe.matmul(ps[:, 4, m * P:(m + 1) * P], bd[:, m, :], outwT[:, m, :], start=True, stop=True)
            ins.then_inc(hy_pe, 1)
            pe.wait_ge(hy_act, HY_ACT["value"])
            for t in range(NT):
                for m in range(CB):
                    ins = pe.matmul(ps[:, (t // TC) % 4, (t % TC) * P:(t % TC + 1) * P], swT[:, m, t * P:(t + 1) * P],
                                    val[:, m, :], start=(m == 0), stop=(m == CB - 1))
                if t % TC == TC - 1:
                    ins.then_inc(x2_mm, 1)

            norm_T(2, (4, 5, 6, 7))
            pe.wait_ge(hv_ok, 1)
            for g in range(NC):
                pe.wait_ge(ln_hT, 2 * NC + g + 1)
                pe.matmul(ps[:, g, :], hv_cols, hT[:, g * CH:(g + 1) * CH], start=True, stop=True).then_inc(sc_mm, 1)

            def g_turn(i, kk):
                kk, i = (kk, i) if kk < 4 else (kk - 4, i + 1)
                k = 4 * i + kk
                pe.wait_ge(g_exp, k + 1)
                for b in range(4):
                    if isinstance(k, int) and k == 0:
                        pe.wait_ge(sc_ok, NC)
                    reached(pe, g_out, 4 * (k - 1) + b + 1)
                    for j in range(4):
                        c = (4 * b + j) * P
                        ins = pe.transpose(ps[:, b, j * P:(j + 1) * P], ring[:, kk, c:c + P], ident[:, :])
                    ins.then_inc(g_tp, 1)

            def g_attend(i, kk):
                k = 4 * i + kk
                pe.wait_ge(g_out, 4 * (k + 1))
                reached(pe, x3_ok, k - 1)
                for j in range(NT):
                    ins = pe.matmul(ps[:, 4 + kk % 2, 0:D], pat[:, kk % 2, j * P:(j + 1) * P], hrow[:, j, :],
                                    start=(j == 0), stop=(j == NT - 1))
                ins.then_inc(g_mm, 1)

            def g_steps(i, last=False):
                for kk in range(4):
                    if not (last and kk + 1 >= 4):
                        g_turn(i, kk + 1)
                    g_attend(i, kk)

            g_turn(0, 0)
            g_steps(0)
            with pe.Fori(1, NT // 4 - 1) as i:
                g_steps(i)
            g_steps(NT // 4 - 1, last=True)

            norm_T(3, (4, 5, 6, 7))
            for t in range(NT):
                if t % TC == 0:
                    pe.wait_ge(ln_hT, 3 * NC + t // TC + 1)
                ins = pe.matmul(ps[:, 0, t * EXPERTS:(t + 1) * EXPERTS], hT[:, t * P:(t + 1) * P], wr, start=True, stop=True)
            ins.then_inc(r_mm, 1)
            pe.wait_ge(r_w, 1)
            for t in range(NT):
                ins = pe.transpose(ps[0:EXPERTS, t // TC, (t % TC) * P:(t % TC + 1) * P], wfull[:, t, :], ident[:, :])
                if t % TC == TC - 1:
                    ins.then_inc(r_tp, 1)
            for t in range(NT):
                if t % TC == 0:
                    pe.wait_ge(r_wT, t // TC + 1)
                ins = pe.matmul(ps[:, 4 + t // TC, (t % TC) * P:(t % TC + 1) * P], wT[:, t * P:(t + 1) * P],
                                b2[0:EXPERTS, :], start=True, stop=True)
                if t % TC == TC - 1:
                    ins.then_inc(b2_mm, 1)

            def up(i, v, q, first=False):
                st = 8 * i + 4 * v + q
                if q == 0:
                    pe.wait_ge(ld_exp[v], 32 * (i + 1))
                if first and st < 2:
                    pe.wait_ge(r_wT, NC)
                for c in range(HC):
                    if not (first and st < 2):
                        pe.wait_ge(gelu_ok, HC * (st - 2) + c + 1)
                    pe.matmul(ps[:, 2 * (q % 2) + c, :], wexp[v][0][:, c * P:(c + 1) * P], hT[:, q * CH:(q + 1) * CH],
                              start=True, stop=True).then_inc(up_mm, 1)

            def down(i, v, q, first=False):
                v, i, q = (v, i, q) if q >= 0 else (1 - v, i - (1 - v), q + NC)
                st = 8 * i + 4 * v + q
                pe.wait_ge(gelu_ok, HC * (st + 1))
                if first and st < 2:
                    pe.wait_ge(b2_ok, NC)
                else:
                    pe.wait_ge(acc_ok, st - 1)
                for j in range(TC):
                    for c in range(HC):
                        ins = pe.matmul(ps[:, 4 + q % 2, j * P:(j + 1) * P], hid[:, q % 2, c, j * P:(j + 1) * P],
                                        wexp[v][1][:, c, :], start=(c == 0), stop=(c == HC - 1))
                ins.then_inc(down_mm, 1)

            def experts(i, first=False):
                for v in range(2):
                    for q in range(NC):
                        up(i, v, q, first)
                        if not (first and v == 0 and q == 0):
                            down(i, v, q - 1, first)

            experts(0, first=True)
            with pe.Fori(1, EXPERTS // 2) as i:
                experts(i)
            down(EXPERTS // 2 - 1, 1, NC - 1)


def GRU_BANK(q):
    return 4 if q % 2 == 0 else 0


def X1_BANK(q):
    return q


U_COPIED = 1 + NT + 1


def lay_out(inputs):
    c = np.ascontiguousarray
    i = {k: np.asarray(v) for k, v in inputs.items()}
    adj = i["adj"]
    T = lambda w: c(w.T)
    o = {"x": c(i["x"]), "adjT": c(adj.T), "adj_t": c(adj.reshape(NT, P, N)),
         "diag": c(np.diagonal(adj).reshape(NT, P).T)}
    eye = np.eye(P, dtype=np.float32)
    o["ident"] = eye
    o["noteye"] = np.ones((P, P), np.float32)
    np.fill_diagonal(o["noteye"], 0)
    sel = np.zeros((96, NS, P), np.float32)
    for q in range(NS):
        sel[q::32, q, :] = 1
    o["sel"] = sel
    W = i["L0_gnn_gat_W"]
    o["gat_WT"] = c(W.transpose(2, 0, 1).reshape(D, HEADS * D))
    o["gat_W"] = c(W.transpose(1, 0, 2).reshape(D, HEADS * D))
    o["gat_a"] = c(i["L0_gnn_gat_a"].reshape(HEADS, 2, D).transpose(2, 1, 0))
    gru = ("L0_gnn_edge_", "L0_gnn_node_")
    o["gru_WT"] = c(np.stack([i[g + w].T for g in gru for w in ("Wih", "Whh")]))
    o["gru_b"] = c(np.stack([i[g + b].reshape(3, D) for g in gru for b in ("bih", "bhh")]).transpose(2, 0, 1))
    f = "L0_ffn_"
    across = lambda v, n: c(np.broadcast_to(v, (n,) + v.shape))
    cols = lambda v: c(v.reshape(-1, P).T)
    o["wx"] = c(i[f + "W_x"].reshape(SLOPES, 64, D).transpose(1, 0, 2))
    o["wsT"] = T(i[f + "W_slice"])
    o["bx"] = T(i[f + "b_x"].reshape(SLOPES, 64))
    o["b_slice"] = across(i[f + "b_slice"], P)
    o["temp"] = across(i[f + "temperature"].reshape(-1), P)
    chunks = lambda w: c(w.T.reshape(CB, P, -1).transpose(1, 0, 2))
    o["in_wT"] = chunks(i[f + "hy_in_w"])
    o["wfxT"] = T(i[f + "W_fx"])
    o["bfx"] = cols(i[f + "b_fx"])
    cw, cb = i[f + "hy_conv_w"], i[f + "hy_conv_b"]
    w6, b6 = np.zeros((P, 6, 3), np.float32), np.zeros((P, 6), np.float32)
    w6[:, :CB] = cw[:DI].reshape(CB, P, 3).transpose(1, 0, 2)
    w6[:64, CB:] = cw[DI:].reshape(2, 64, 3).transpose(1, 0, 2)
    b6[:, :CB] = cb[:DI].reshape(CB, P).T
    b6[:64, CB:] = cb[DI:].reshape(2, 64).T
    o["cw"], o["cb"] = w6, b6
    o["dtb"] = across(i[f + "hy_dt_bias"], P)
    o["alog"] = across(i[f + "hy_A_log"], P)
    r = np.arange(64)
    m_rs, m_rt, m_st = np.zeros((P, P), np.float32), np.zeros((P, G), np.float32), np.zeros((P, G), np.float32)
    m_rs[:64, :64] = r[:, None] > r[None, :]
    m_rs[64:, 64:] = r[:, None] < r[None, :]
    m_rt[:64], m_rt[64:] = r[:, None] <= r[None, :] - 1, r[:, None] >= r[None, :] + 1
    m_st[:64], m_st[64:] = r[:, None] <= r[None, :] - 1, r[:, None] >= r[None, :] + 1
    o["m_rs"], o["m_rt"], o["m_st"] = m_rs, m_rt, m_st
    o["outb"] = across(i[f + "out_b"], P)
    o["fcDT"] = chunks(np.repeat(i[f + "hy_fcD_w"], 64, axis=0))
    o["dcol"] = cols(np.repeat(i[f + "hy_D"], 64))
    o["nwcol"] = cols(i[f + "hy_norm_w"])
    o["outT"] = chunks(i[f + "hy_out_w"])
    o["outwT"] = chunks(i[f + "out_w"])
    e = "L1_ffn_"
    o["hv"] = c(i["L1_gnn_H_v"])
    o["gamma"], o["beta"] = c(i[e + "gamma"][:, None]), c(i[e + "beta"][:, None])
    o["Wr"], o["br"] = c(i[e + "Wr"]), across(i[e + "br"], P)
    o["prio"] = across(np.arange(EXPERTS, 0, -1).astype(np.float32), P)
    o["b1"] = c(i[e + "b1"].reshape(EXPERTS, HC, P).transpose(2, 0, 1))
    o["b2"] = c(i[e + "b2"])
    o["W1"] = c(i[e + "W1"])
    o["W2"] = c(i[e + "W2"].reshape(EXPERTS, HC, P, D).transpose(0, 2, 1, 3))
    return o


def kernel(**inputs):
    import concourse.bacc as _bacc
    from concourse.bass_utils import run_bass_kernel_spmd as _run

    nc = _bacc.Bacc("TRN2", target_bir_lowering=False, num_devices=1)
    arrays, args = {}, {}
    for name, a in lay_out(inputs).items():
        arrays[f"in_{name}"] = a
        args[name] = nc.dram_tensor(f"in_{name}", a.shape, mybir.dt.from_np(a.dtype), kind="ExternalInput").ap()
    out = nc.dram_tensor("out_0", (N, D), F32, kind="ExternalOutput").ap()
    graph_block(nc, args, out)
    r = _run(nc, [arrays], core_ids=[0])
    return r.results[0]["out_0"]
```

```python
from contextlib import ExitStack

import numpy as np

import concourse.bass as bass
from concourse import mybir

ALU = mybir.AluOpType
ACT = mybir.ActivationFunctionType
AX = mybir.AxisListType
F32 = mybir.dt.float32
BF16 = mybir.dt.bfloat16
U8 = mybir.dt.uint8

P = 128
N = 2048
D = 128
NT = N // P
CH = 512
NC = N // CH
TC = CH // P
HEADS = 3
NS = 2 * HEADS
K = NT * HEADS
RING = 6
EPS = 1e-5
FLOOR = 1e30
NEG = 9e15
FAR = 3e38
GAT_ALPHA = 0.2
SLOPES = 8
G = 64
DI = 512
CB = DI // P
EXPERTS = 8
HID = 256
HC = HID // P


def numbered(*names):
    return {name: n + 1 for n, name in enumerate(names)}


HY_PE = numbered("slice_w", "slice_b", "snorm", "tokens", "bcdt", "x", "z", "decay", "gram", "x_rows", "skip", "y",
                 "power", "out", "value")
HY_DVE = numbered("bias_cols", "inv_temp", "slice_w", "slice_b1", "slice_b2", "slice_b", "snorm_eps", "snorm_inv", "tok_w", "snorm_n",
                  "tok_b0", "tok_b1", "tok0", "tok1", "dt_in", "dt_neg", "dt_nabs", "pad", "conv0", "conv1", "conv01",
                  "conv2", "conv012", "conv_b", "dt", "decay_rate", "decay_in", "silu_den", "silu_inv", "xbc", "x_twice",
                  "gram", "weight_dt", "weight", "z_den", "z_inv", "z", "skip_d", "skip", "y", "yg", "sq", "rms",
                  "yn", "ynw", "ot0", "ot1")
HY_ACT = numbered("rate", "dt_exp", "dt_ln", "conv_exp", "z_copy", "z_exp", "decay_exp", "x_rows", "rms_std", "value")


def reached(eng, sem, value):
    if isinstance(value, int) and value <= 0:
        return
    eng.wait_ge(sem, value)


def graph_block(nc: bass.Bass, a: dict, out: bass.AP):
    ctx = ExitStack()
    with ctx:
        def sb(name, shape, dt=F32):
            return ctx.enter_context(nc.sbuf_tensor(name, shape, dt))

        def sem(name):
            return ctx.enter_context(nc.semaphore(name))

        ps = ctx.enter_context(nc.psum_tensor("ps", [P, 8, CH], F32))

        ident = sb("ident", [P, P])
        noteye = sb("noteye", [P, P])
        eps_col = sb("eps_col", [P, 1])
        xr = sb("xr", [P, NT, D])
        hrow = sb("hrow", [P, NT, D])
        hT = sb("hT", [P, N])
        nsT = sb("nsT", [P, N])
        hW = sb("hW", [P, NT, HEADS * D])
        eb = sb("eb", [P, NS, N])
        arow = sb("arow", [P, 2, N])
        nb = sb("nb", [P, N])
        mneg = sb("mneg", [P, N], U8)
        ring = sb("ring", [P, RING, N])
        pat = sb("pat", [P, 2, N])
        esT = hrow[:, :, :].rearrange("p t d -> p (t d)")

        def cutter(area, size):
            at = [0]

            def piece(n):
                at[0] += n
                assert at[0] <= size, at
                return area[:, at[0] - n:at[0]]
            return piece

        st6 = sb("st6", [P, NT * 6])[:, :].rearrange("p (t s) -> p t s", t=NT)
        mv = sb("mv", [P, NT * 2])[:, :].rearrange("p (t s) -> p t s", t=NT)
        std = sb("std", [P, NT])[:, :]
        rstd = sb("rstd", [P, NT])[:, :]
        gatWT = sb("gatWT", [P, HEADS * D])[:, :]
        gatA = sb("gatA", [P, NS])[:, :].rearrange("p (s h) -> p s h", s=2)
        wa = sb("wa", [P, NS])[:, :]
        WT = [sb(f"WT{k}", [P, 3 * D])[:, :] for k in range(4)]
        gb = sb("gb", [P, 12])[:, :].rearrange("p (k g) -> p k g", k=4)
        gbs = sb("gbs", [P, 6])[:, :].rearrange("p (k g) -> p k g", k=2)
        diag = sb("diag", [P, NT])[:, :]
        mn = sb("mn", [P, RING])[:, :]
        den = sb("den", [P, RING])[:, :]
        rden = sb("rden", [P, RING])[:, :]
        esb = sb("esb", [P, 2 * D])[:, :].rearrange("p (u d) -> p u d", u=2)

        aT = [ring[:, s, :] for s in range(3)]
        masks = hW[:, :, :].rearrange("p t n -> p (t n)").bitcast(BF16).rearrange(
            "p (u s n) -> p u s n", u=3, s=2)
        mres = ring[:, 3, :]
        n_neg = sb("n_neg", [P, NT])
        n_neg1 = sb("n_neg1", [P, 1])
        n_one = sb("n_one", [P, 1])
        any_neg = sb("any_neg", [1, 1], mybir.dt.int32)
        parts = ring[:, 4, 0:NT * 96].bitcast(BF16).rearrange(
            "p (v t q) -> p v t q", v=2, t=NT)
        sel = ring[:, 5, 0:NS * P].rearrange("p (q m) -> p q m", q=NS)
        piece5 = cutter(ring[:, 5, NS * P:N], N - NS * P)
        gatW = piece5(HEADS * D)
        uu = [piece5(NT * NS).rearrange("p (t q) -> p t q", t=NT) for _ in range(4)]
        gr, gz = ([ring[:, 3, (2 * u + k) * CH:(2 * u + k + 1) * CH] for u in range(2)] for k in range(2))
        gts = [[ring[:, slot, u * CH:(u + 1) * CH] for u in range(2)] for slot in (4, 2)]

        swT = eb[:, 0:CB, :]
        sw = [ring[:, t % 4, (t // 4) * CH:(t // 4 + 1) * CH] for t in range(8)]
        hWf = hW[:, :, :].rearrange("p t d -> p (t d)")
        cut_h = cutter(hWf, NT * HEADS * D)
        ZX = 2 * DI + 2 * G + 2 * SLOPES
        in_wT = cut_h(CB * ZX).rearrange("p (k n) -> p k n", k=CB)
        wx = cut_h(SLOPES * D).rearrange("p (h d) -> p h d", h=SLOPES)
        wsT = cut_h(G)
        outT = eb[:, 4, :].rearrange("p (k n) -> p k n", k=CB)
        fcDT = eb[:, 5, :].rearrange("p (k n) -> p k n", k=CB)
        cut4 = cutter(ring[:, 4, :], N)
        wfxT, w_slice, b_slice = cut4(DI), cut4(DI), cut4(DI)
        outwT = cut4(CB * D).rearrange("p (m d) -> p m d", m=CB)
        cut5 = cutter(ring[:, 5, :], N)
        bx_cols = cut5(SLOPES * P).rearrange("p (h m) -> p h m", h=SLOPES)
        swsum = cut5(DI)
        b_rows = sb("b_rows", [P, DI], BF16)[:, :]
        ones16 = sb("ones16", [P, P], BF16)
        b_part = sb("b_part", [P, DI], BF16)[:, :]
        b_rest = [pat[:, 0, k * DI:(k + 1) * DI] for k in range(2)]
        bsl, bx, temp = cut5(G), cut5(SLOPES), cut5(SLOPES)
        bfx, cw, cb = cut5(CB), cut5(6 * 3).rearrange("p (c k) -> p c k", c=6), cut5(6)
        dtb, alog, dcol, nwcol = cut5(SLOPES), cut5(SLOPES), cut5(CB), cut5(CB)
        dt_s = [cut5(SLOPES) for _ in range(5)]
        rate = cut5(SLOPES)
        mx8 = [cut5(SLOPES) for _ in range(4)]
        rs8 = [cut5(SLOPES) for _ in range(4)]
        cutn = cutter(nb, N)
        outb = cutn(D)
        m_rs, m_rt, m_st = cutn(P), cutn(G), cutn(G)
        ones = cutn(P)
        tok_n, sn_n, rsn = cutn(DI), cutn(DI), cutn(DI)
        hy = [ring[:, k, 2 * CH:4 * CH] for k in range(4)]
        tokT = hy[0][:, 0:CB * G].rearrange("p (k g) -> p k g", k=CB)
        tokb = hy[0][:, CB * G:2 * CB * G].rearrange("p (k g) -> p k g", k=CB)
        PADW = G + 2
        xp = hy[0][:, 512:512 + 6 * PADW].rearrange("p (c l) -> p c l", c=6)
        xs = hy[1][:, 0:6 * PADW].rearrange("p (c l) -> p c l", c=6)
        cva = hy[1][:, 400:400 + 6 * G].rearrange("p (c l) -> p c l", c=6)
        cvt = hy[2][:, 0:6 * G].rearrange("p (c l) -> p c l", c=6)
        gramm = hy[2][:, 384:384 + G]
        x2 = hy[2][:, 512:1024]
        dec = hy[3][:, 0:512].rearrange("p (h t) -> p h t", h=SLOPES)
        xd = hy[3][:, 512:1024].rearrange("p (m v g) -> p m v g", m=CB, v=2)
        cutp = cutter(pat[:, 0, :], N)
        zz, z1, y1, ysq = (cutp(CB * G).rearrange("p (k g) -> p k g", k=CB) for _ in range(4))
        bd = cutp(CB * P).rearrange("p (m r) -> p m r", m=CB)
        rms = cutp(G)
        val = pat[:, 1, 0:CB * D].rearrange("p (m d) -> p m d", m=CB)

        sbn = eb[:, 0, :]
        hv_cols = nsT[:, 0:D]
        cute = cutter(nsT[:, D:N], N - D)
        wexp = [(cute(HID), cute(HC * D).rearrange("p (c d) -> p c d", c=HC)) for _ in range(2)]
        wr, hv, gamma, beta = cute(EXPERTS), cute(1), cute(1), cute(1)
        b1 = cute(EXPERTS * HC).rearrange("p (e c) -> p e c", e=EXPERTS)
        b2, br, prio = cute(D), cute(EXPERTS), cute(EXPERTS)
        hid = pat[:, :, 0:2 * CH].rearrange("p u (c n) -> p u c n", c=HC)
        cutr = cutter(nb, N)
        route, top, hot1, hot2, wfull = (cutr(NT * EXPERTS).rearrange("p (t e) -> p t e", t=NT) for _ in range(5))
        v1, v2, ky, ew, w1 = (cutr(NT) for _ in range(5))
        wT = eb[0:EXPERTS, 1, :]
        OUT_COUNT = 16 * NC

        ld_x = [sem(f"ld_x{q}") for q in range(NC)]
        ld_c, ld_gat, ld_gru = sem("ld_c"), sem("ld_gat"), sem("ld_gru")
        aT_in = [sem(f"aT_in{s}") for s in range(3)]
        dve_seq, u_sb = sem("dve_seq"), sem("u_sb")
        out_stored = sem("out_stored")
        ln_bn, ln_stats, ln_std, ln_rstd, ln_row, ln_tp, ln_hT = (
            sem("ln_" + s) for s in ("bn", "stats", "std", "rstd", "row", "tp", "hT"))
        LN_PARTS = (NC, 1, NC, 1)
        LN_BEFORE = (0, NC, NC + 1, 2 * NC + 1)
        aggregated = [0]
        wa_mm, wa_sb, u_mm, parts_ok = sem("wa_mm"), sem("wa_sb"), sem("u_mm"), sem("parts_ok")
        hw_mm, hw_sb = sem("hw_mm"), sem("hw_sb")
        aT_diag, neg_mm, neg_ok = sem("aT_diag"), sem("neg_mm"), sem("neg_ok")
        masks_ok, aT_used, masks_used, ns_sb, mres_sb = sem("masks_ok"), sem("aT_used"), sem("masks_used"), sem("ns_sb"), sem("mres_sb")
        bc_mm, bc_sb, eb_ok = sem("bc_mm"), sem("bc_sb"), sem("eb_ok")
        gru_mm, gru_r, gru_z, gru_t, gru_n, gru_out = (
            sem("gru_" + s) for s in ("mm", "r", "z", "t", "n", "out"))
        gbs_ok = sem("gbs_ok")
        row_in = [sem("row_in0"), sem("row_in1")]
        row_free, picked, s_ready, z_ready, p_ready = (
            sem(s) for s in ("row_free", "picked", "s_ready", "z_ready", "p_ready"))
        prep = sem("prep")
        e_copied, tp_ready, tp_out, mm_done, es_acc = (
            sem(s) for s in ("e_copied", "tp_ready", "tp_out", "mm_done", "es_acc"))
        rd_ok = sem("rd_ok")
        es_tp, es_T = sem("es_tp"), sem("es_T")
        x1_tp, x1_ok = sem("x1_tp"), sem("x1_ok")
        ld_slice, ld_hy = sem("ld_slice"), sem("ld_hy")
        hy_pe, hy_dve, hy_act = sem("hy_pe"), sem("hy_dve"), sem("hy_act")
        lg_mm, lg_max, lg_sub, lg_exp, lg_sum, sw_ok, sw_sum, sw_tp, sw_T, x2_mm, x2_ok, outb_ok = (
            sem(x) for x in ("lg_mm", "lg_max", "lg_sub", "lg_exp", "lg_sum", "sw_ok", "sw_sum", "sw_tp", "sw_T",
                             "x2_mm", "x2_ok", "outb_ok"))
        ones_ok = sem("ones_ok")
        ld_moe, ld_exp = sem("ld_moe"), [sem("ld_exp0"), sem("ld_exp1")]
        hv_ok, sc_mm, sc_ok = sem("hv_ok"), sem("sc_mm"), sem("sc_ok")
        row2_in = [sem(f"row2_in{u}") for u in range(2)]
        g_prod, g_mask, g_min, g_score, g_exp, g_tp, g_out, g_mm, g_den, x3_ok = (
            sem("g_" + x) for x in ("prod", "mask", "min", "score", "exp", "tp", "out", "mm", "den", "x3_ok"))
        r_mm, r_dlt, r_exp, r_w, r_tp, r_wT, b2_mm, b2_ok = (
            sem(x) for x in ("r_mm", "r_dlt", "r_exp", "r_w", "r_tp", "r_wT", "b2_mm", "b2_ok"))
        up_mm, gelu_ok, down_mm, acc_ok = sem("up_mm"), sem("gelu_ok"), sem("down_mm"), sem("acc_ok")

        HY_LOADS = ((in_wT, "in_wT"), (wfxT, "wfxT"), (bfx, "bfx"), (cw, "cw"), (cb, "cb"), (dtb, "dtb"), (alog, "alog"),
                    (m_rs, "m_rs"), (m_rt, "m_rt"), (m_st, "m_st"), (outb, "outb"), (fcDT, "fcDT"), (dcol, "dcol"),
                    (nwcol, "nwcol"), (outT, "outT"), (outwT, "outwT"))

        MOE_LOADS = ((wr, "Wr"), (hv, "hv"), (gamma, "gamma"), (beta, "beta"), (b1, "b1"), (b2[0:EXPERTS, :], "b2"),
                     (br, "br"), (prio, "prio"))

        loop_waits = sem("loop_waits")

        def waited(eng):
            eng.sem_inc(loop_waits, 1)

        block = ctx.enter_context(nc.Block())

        @block.sync
        def _(sp):
            for q in range(NC):
                sp.dma_start(xr[:, q * TC:(q + 1) * TC, :],
                             a["x"][q * CH:(q + 1) * CH, :].rearrange("(t p) d -> p t d", p=P)).then_inc(ld_x[q], 16)
                if q == 0:
                    sp.dma_start(ident[:, :], a["ident"]).then_inc(ld_c, 16)
                    sp.dma_start(noteye[:, :], a["noteye"]).then_inc(ld_c, 16)
            sp.dma_start(gatWT, a["gat_WT"]).then_inc(ld_gat, 16)
            sp.dma_start(gatA, a["gat_a"]).then_inc(ld_gat, 16)
            sp.dma_start(gatW, a["gat_W"]).then_inc(ld_gat, 16)
            sp.dma_start(sel[0:96, :, :], a["sel"]).then_inc(ld_gat, 16)
            for j in range(NT):
                if j >= 3:
                    sp.wait_ge(aT_used, j - 2)
                    sp.wait_ge(masks_ok, j - 2)
                sp.dma_start(aT[j % 3], a["adjT"][j * P:(j + 1) * P, :]).then_inc(aT_in[j % 3], 16)
                if j == 2:
                    for k in range(4):
                        sp.dma_start(WT[k], a["gru_WT"][k]).then_inc(ld_gru, 16)
                    sp.dma_start(gb, a["gru_b"]).then_inc(ld_gru, 16)
                    sp.dma_start(diag, a["diag"]).then_inc(ld_gru, 16)

            def rows(t, u, i):
                reached(sp, p_ready, 3 * (t - 1))
                sp.dma_start(arow[:, u, :], a["adj_t"][t, :, :] if isinstance(t, int) else
                             a["adj_t"][bass.ds(t, 1), :, :].rearrange("a p n -> (a p) n")).then_inc(row_in[u], 16)
            rows(0, 0, 0)
            rows(1, 1, 0)
            with sp.Fori(1, NT // 2) as i:
                for u in range(2):
                    rows(2 * i + u, u, i)

            sp.wait_ge(es_T, NT)
            for to, name in ((wx[0:64, :, :], "wx"), (wsT[0:64, :], "wsT"), (bx[0:64, :], "bx"), (bsl, "b_slice"),
                             (temp, "temp")):
                sp.dma_start(to, a[name]).then_inc(ld_slice, 16)
            for to, name in HY_LOADS:
                sp.dma_start(to, a[name]).then_inc(ld_hy, 16)

            def rows2(t, u, i):
                reached(sp, g_prod, t - 1)
                reached(sp, g_mask, t - 1)
                sp.dma_start(arow[:, u, :], a["adj_t"][t, :, :] if isinstance(t, int) else
                             a["adj_t"][bass.ds(t, 1), :, :].rearrange("a p n -> (a p) n")).then_inc(row2_in[u], 16)
            rows2(0, 0, 0)
            rows2(1, 1, 0)
            sp.wait_ge(x1_tp, NT)
            for to, name in MOE_LOADS:
                sp.dma_start(to, a[name]).then_inc(ld_moe, 16)

            def expert(e, u):
                reached(sp, down_mm, 4 * (e - 1))
                for to, name in ((wexp[u][0], "W1"), (wexp[u][1], "W2")):
                    src = a[name][e] if isinstance(e, int) else a[name][bass.ds(e, 1)].rearrange(
                        "a p n -> (a p) n" if name == "W1" else "a p c n -> (a p) c n")
                    sp.dma_start(to, src).then_inc(ld_exp[u], 16)
            expert(0, 0)
            expert(1, 1)
            with sp.Fori(1, NT // 2) as i:
                for u in range(2):
                    rows2(2 * i + u, u, i)
            with sp.Fori(1, EXPERTS // 2) as i:
                for u in range(2):
                    expert(2 * i + u, u)
            for q in range(NC):
                sp.wait_ge(acc_ok, NC * (EXPERTS - 1) + q + 1)
                sp.dma_start(out[q * CH:(q + 1) * CH, :].rearrange("(t p) d -> p t d", p=P),
                             xr[:, q * TC:(q + 1) * TC, :]).then_inc(out_stored, 16)
            sp.wait_ge(out_stored, 16 * NC)

        @block.scalar
        def _(act):
            def norm_std(n, q):
                cols = slice(q * TC, (q + 1) * TC) if LN_PARTS[n] == NC else slice(0, NT)
                act.wait_ge(ln_stats, LN_BEFORE[n] + q + 1)
                act.activation(std[:, cols], mv[:, cols, 1], ACT.Sqrt, bias=eps_col[:, 0:1]).then_inc(ln_std, 1)

            def norm_T(n, banks):
                if n == 3:
                    act.wait_ge(ld_moe, 16 * len(MOE_LOADS))
                for g in range(NC):
                    if g < LN_PARTS[n]:
                        norm_std(n, g)
                    act.wait_ge(ln_tp, n * NC + g + 1)
                    if n == 3:
                        act.activation(hT[:, g * CH:(g + 1) * CH], ps[:, banks[g], :], ACT.Identity,
                                       scale=gamma, bias=beta).then_inc(ln_hT, 1)
                        continue
                    act.activation(hT[:, g * CH:(g + 1) * CH], ps[:, banks[g], :], ACT.Copy).then_inc(ln_hT, 1)

            norm_T(0, (0, 1, 2, 3))
            act.wait_ge(aT_used, NT)
            act.wait_ge(masks_used, NT)
            for g in range(NC):
                act.activation(mres[0:96, g * CH:(g + 1) * CH], ps[0:96, 4 + g, :], ACT.Copy).then_inc(mres_sb, 1)
                act.activation(nsT[:, g * CH:(g + 1) * CH], ps[:, g, :], ACT.Copy).then_inc(ns_sb, 1)
            for n in range(NS * NC):
                act.wait_ge(bc_mm, n + 1)
                act.activation(eb[:, n // NC, (n % NC) * CH:(n % NC + 1) * CH], ps[:, n % 4, :], ACT.Copy,
                               scale=-1.0).then_inc(bc_sb, 1)

            def exps(i, kk):
                kk, i = (kk, i) if kk < 6 else (kk - 6, i + 1)
                k, s = 6 * i + kk, kk % RING
                reached(act, rd_ok, k - 5)
                act.wait_ge(s_ready, k + 1)
                act.activation(ring[:, s, :], ring[:, s, :], ACT.Exp, bias=mn[:, s:s + 1], scale=-1.0,
                               accum_out=den[:, s:s + 1]).then_inc(z_ready, 1)

            for j in range(NT):
                act.wait_ge(hw_mm, j + 1)
                act.activation(hW[:, j, :], ps[:, 4 + j % 2, 0:HEADS * D], ACT.Copy).then_inc(hw_sb, 1)

            def gru(n):
                act.wait_ge(gbs_ok, 1)
                gt = gts[n]
                for q in range(NC):
                    u, c = q % 2, n * NC + q
                    b = GRU_BANK(q)
                    act.wait_ge(gru_mm, 4 * c + 1)
                    if q >= 2:
                        act.wait_ge(gru_out, c - 1)
                    act.activation(gr[u], ps[:, b, :], ACT.Sigmoid, bias=gbs[:, n, 0:1]).then_inc(gru_r, 1)
                    act.wait_ge(gru_mm, 4 * c + 2)
                    act.activation(gz[u], ps[:, b + 1, :], ACT.Sigmoid, bias=gbs[:, n, 1:2]).then_inc(gru_z, 1)
                    act.wait_ge(gru_t, c + 1)
                    act.activation(gt[u], gt[u], ACT.Tanh, bias=gb[:, 2 * n, 2:3]).then_inc(gru_n, 1)
                    if n == 0 and q in (0, 1):
                        exps(0, q + 1)

            exps(0, 0)
            gru(0)

            def evac(i, kk):
                k = 6 * i + kk
                for b in range(4):
                    if b == 0:
                        reached(act, mm_done, k - 1)
                    act.wait_ge(tp_ready, 4 * k + b + 1)
                    act.activation(pat[:, kk % 2, b * CH:(b + 1) * CH], ps[:, b, :], ACT.Copy).then_inc(tp_out, 1)

            def es_out(t, u):
                act.wait_ge(es_tp, t + 1)
                waited(act)
                act.activation(esT[:, bass.ds(t * P, P)], ps[:, 6 + u, 0:P], ACT.Copy,
                               scale=1.0 / HEADS).then_inc(es_T, 1)

            def steps(i, first=False, last=False):
                for kk in range(6):
                    if kk % 3 == 0 and not first:
                        es_out(2 * i + kk // 3 - 2, kk // 3)
                    evac(i, kk)
                    if not (last and kk + 3 >= 6):
                        exps(i, kk + 3)

            steps(0, first=True)
            with act.Fori(1, NT // 2 - 1) as i:
                steps(i)
            steps(NT // 2 - 1, last=True)
            es_out(NT - 2, 0)
            es_out(NT - 1, 1)
            gru(1)

            norm_T(1, (0, 1, 2, 3))

            def sw_out(t):
                act.wait_ge(sw_tp, t + 1)
                act.activation(swT[:, :, t * P:(t + 1) * P], ps[:, t % 2, :].rearrange("p (m n) -> p m n", m=CB),
                               ACT.Copy).then_inc(sw_T, 1)

            for t in range(NT):
                act.wait_ge(lg_sub, t + 1)
                act.activation(sw[t % 8], sw[t % 8], ACT.Exp).then_inc(lg_exp, 1)
                if t >= 3:
                    sw_out(t - 3)
            for t in range(NT - 3, NT):
                sw_out(t)

            def hyd(name, ins):
                ins.then_inc(hy_act, 1)
                act.wait_ge(hy_act, HY_ACT[name])

            act.wait_ge(ld_hy, 16 * len(HY_LOADS))
            hyd("rate", act.activation(rate, alog, ACT.Exp))
            act.wait_ge(hy_dve, HY_DVE["dt_nabs"])
            hyd("dt_exp", act.activation(dt_s[2], dt_s[1], ACT.Exp))
            hyd("dt_ln", act.activation(dt_s[3], dt_s[2], ACT.Ln, bias=1.0))
            act.wait_ge(hy_dve, HY_DVE["conv_b"])
            hyd("conv_exp", act.activation(cvt, cva, ACT.Exp, scale=-1.0))
            act.wait_ge(hy_pe, HY_PE["z"])
            hyd("z_copy", act.activation(zz, ps[:, 0, 0:CB * G].rearrange("p (k g) -> p k g", k=CB), ACT.Copy))
            hyd("z_exp", act.activation(z1, zz, ACT.Exp, scale=-1.0))
            act.wait_ge(hy_pe, HY_PE["decay"])
            hyd("decay_exp", act.activation(dec, ps[:, 5, :].rearrange("p (h t) -> p h t", h=SLOPES), ACT.Exp))
            act.wait_ge(hy_pe, HY_PE["x_rows"])
            hyd("x_rows", act.activation(x2, ps[:, 4, :], ACT.Copy))
            act.wait_ge(hy_pe, HY_PE["power"])
            hyd("rms_std", act.activation(rms, ps[:, 2, 0:G], ACT.Sqrt, scale=1.0 / DI, bias=eps_col[:, 0:1]))
            act.wait_ge(hy_pe, HY_PE["value"])
            hyd("value", act.activation(val, ps[:, 4, :].rearrange("p (m d) -> p m d", m=CB), ACT.Copy))

            norm_T(2, (4, 5, 6, 7))
            for g in range(NC):
                act.wait_ge(sc_mm, g + 1)
                act.activation(sbn[:, g * CH:(g + 1) * CH], ps[:, g, :], ACT.Copy, scale=-1.0).then_inc(sc_ok, 1)

            def g_exps(i, kk):
                k = 4 * i + kk
                act.wait_ge(g_score, k + 1)
                reached(act, g_den, 2 * k - 7)
                act.activation(ring[:, kk % 4, :], ring[:, kk % 4, :], ACT.Exp, bias=mn[:, kk % 4:kk % 4 + 1], scale=-1.0,
                               accum_out=den[:, kk % 4:kk % 4 + 1]).then_inc(g_exp, 1)

            def g_evac(i, kk):
                k = 4 * i + kk
                for b in range(4):
                    if b == 0:
                        reached(act, g_mm, k - 1)
                    act.wait_ge(g_tp, 4 * k + b + 1)
                    act.activation(pat[:, kk % 2, b * CH:(b + 1) * CH], ps[:, b, :], ACT.Copy).then_inc(g_out, 1)

            def g_steps(i, last=False):
                for kk in range(4):
                    g_evac(i, kk)
                    if not (last and kk + 2 >= 4):
                        g_exps(i, kk + 2)

            g_exps(0, 0)
            g_exps(0, 1)
            g_steps(0)
            with act.Fori(1, NT // 4 - 1) as i:
                g_steps(i)
            g_steps(NT // 4 - 1, last=True)

            norm_T(3, (4, 5, 6, 7))
            act.wait_ge(r_dlt, 1)
            act.activation(ew, v2, ACT.Exp).then_inc(r_exp, 1)
            def gelus(i, v, first=False):
                for q in range(NC):
                    st = 8 * i + 4 * v + q
                    if not (first and st < 2):
                        act.wait_ge(down_mm, st - 1)
                    for c in range(HC):
                        act.wait_ge(up_mm, HC * st + c + 1)
                        waited(act)
                        act.activation(hid[:, q % 2, c, :], ps[:, 2 * (q % 2) + c, :], ACT.Gelu,
                                       bias=b1[:, 2 * i + v, c:c + 1] if isinstance(i, int) else
                                       b1[:, bass.ds(2 * i + v, 1), c]).then_inc(gelu_ok, 1)

            def router_T(g):
                act.wait_ge(r_tp, g + 1)
                act.activation(wT[:, g * CH:(g + 1) * CH], ps[0:EXPERTS, 6 + g % 2, :], ACT.Copy).then_inc(r_wT, 1)

            gelus(0, 0, first=True)
            router_T(0)
            router_T(1)
            gelus(0, 1)
            router_T(2)
            router_T(3)
            gelus(1, 0)
            gelus(1, 1)
            with act.Fori(2, EXPERTS // 2) as i:
                gelus(i, 0)
                gelus(i, 1)

        @block.vector
        def _(dve):
            count = [0]

            def link(ins):
                count[0] += 1
                ins.then_inc(dve_seq, 1)
                dve.wait_ge(dve_seq, count[0])

            def stats(t):
                dve.bn_stats(st6[:, t, :], xr[:, t, :]).then_inc(ln_bn, 1)

            def aggregate(n, ts):
                dve.wait_ge(ln_bn, n * NT + ts[-1] + 1)
                for t in ts:
                    ins = dve.bn_aggr(mv[:, t, :], st6[:, t, :])
                ins.then_inc(ln_stats, 1)

            def finish(n, q):
                cols = slice(q * TC, (q + 1) * TC)
                dve.wait_ge(ln_std, LN_BEFORE[n] + (q + 1 if LN_PARTS[n] == NC else 1))
                dve.reciprocal(rstd[:, cols], std[:, cols]).then_inc(ln_rstd, 1)
                dve.wait_ge(ln_rstd, n * NC + q + 1)
                for t in range(q * TC, (q + 1) * TC):
                    dve.tensor_scalar(hrow[:, t, :], xr[:, t, :], mv[:, t, 0:1], rstd[:, t:t + 1],
                                      ALU.subtract, ALU.mult).then_inc(ln_row, 1)

            def norm_by_chunk(n, chunk_ready):
                for q in range(NC):
                    chunk_ready(q)
                    ts = range(q * TC, (q + 1) * TC)
                    for t in ts:
                        stats(t)
                    aggregate(n, ts)
                    finish(n, q)

            dve.memset(eps_col[:, :], EPS)
            link(dve.memset(parts, 0.0))
            norm_by_chunk(0, lambda q: dve.wait_ge(ld_x[q], 16))
            dve.memset(n_one[:, :], 1.0)
            dve.wait_ge(wa_mm, 1)
            dve.tensor_copy(wa, ps[:, 7, 0:NS]).then_inc(wa_sb, 1)
            swap = (slice(HEADS, NS), slice(0, HEADS))

            def part(c, src):
                dve.tensor_copy(parts[:, 0, :, 32 * c:32 * c + NS], src)
                dve.tensor_copy(parts[:, 1, :, 32 * c:32 * c + HEADS], src[:, :, swap[0]])
                return dve.tensor_copy(parts[:, 1, :, 32 * c + HEADS:32 * c + NS], src[:, :, swap[1]])

            def split():
                dve.wait_ge(u_mm, 1)
                dve.tensor_copy(uu[0], ps[:, 6, 0:NT * NS].rearrange("p (t q) -> p t q", t=NT)).then_inc(u_sb, 1)
                dve.wait_ge(u_sb, 1)
                link(part(0, uu[0]))
                link(dve.tensor_tensor(uu[1], uu[0], parts[:, 0, :, 0:NS], ALU.subtract))
                link(part(1, uu[1]))
                link(dve.tensor_tensor(uu[2], uu[1], parts[:, 0, :, 32:32 + NS], ALU.subtract))
                part(2, uu[2]).then_inc(parts_ok, 1)

            def masks_of(j):
                if j >= 3:
                    dve.wait_ge(masks_used, j - 2)
                dve.tensor_scalar(masks[:, j % 3, 0, :], aT[j % 3], 0.0, None, ALU.is_gt)
                dve.tensor_scalar(masks[:, j % 3, 1, :], aT[j % 3], 0.0, 0.0, ALU.is_lt, ALU.add,
                                  accum_out=n_neg[:, j:j + 1]).then_inc(masks_ok, 1)

            for j in range(NT):
                dve.wait_ge(aT_in[j % 3], 16 * (j // 3 + 1))
                blk = aT[j % 3][:, j * P:(j + 1) * P]
                dve.tensor_tensor(blk, blk, noteye[:, :], ALU.mult).then_inc(aT_diag, 1)
                dve.wait_ge(aT_diag, j + 1)
                masks_of(j)
                if j == 1:
                    split()
            dve.wait_ge(masks_ok, NT)
            dve.tensor_reduce(n_neg1[:, :], n_neg[:, :], AX.X, ALU.add).then_inc(neg_ok, 1)
            dve.wait_ge(neg_mm, 1)
            dve.tensor_copy(any_neg[:, :], ps[0:1, 6, 0:1]).then_inc(neg_ok, 1)
            def leaky(q):
                dve.wait_ge(bc_sb, NC * (q + 1))
                dve.scalar_tensor_tensor(eb[:, q, :], eb[:, q, :], GAT_ALPHA, eb[:, q, :],
                                         ALU.mult, ALU.min).then_inc(eb_ok, 1)

            for q in range(HEADS):
                leaky(q)
            dve.wait_ge(ld_gru, 96)
            dve.tensor_tensor(gbs, gb[:, 0:4:2, :], gb[:, 1:4:2, :], ALU.add).then_inc(gbs_ok, 1)

            def gru(n):
                gt = gts[n]
                for q in range(NC + 1):
                    if q < NC:
                        u, c = q % 2, n * NC + q
                        b = GRU_BANK(q)
                        dve.wait_ge(gru_r, c + 1)
                        dve.wait_ge(gru_mm, 4 * c + 3)
                        link(dve.scalar_tensor_tensor(gt[u], ps[:, b + 2, :], gb[:, 2 * n + 1, 2:3], gr[u],
                                                      ALU.add, ALU.mult))
                        dve.wait_ge(gru_mm, 4 * c + 4)
                        dve.tensor_tensor(gt[u], gt[u], ps[:, b + 3, :], ALU.add).then_inc(gru_t, 1)
                    if q >= 1:
                        u, c = (q - 1) % 2, n * NC + q - 1
                        cols = slice((q - 1) * CH, q * CH)
                        dve.wait_ge(gru_n, c + 1)
                        dve.wait_ge(gru_z, c + 1)
                        link(dve.tensor_tensor(gr[u], hT[:, cols], gt[u], ALU.subtract))
                        link(dve.tensor_tensor(gr[u], gr[u], gz[u], ALU.mult))
                        if n == 0:
                            dve.tensor_tensor(nsT[:, cols], gr[u], gt[u], ALU.add).then_inc(gru_out, 1)
                        else:
                            link(dve.tensor_tensor(gr[u], gr[u], gt[u], ALU.add))
                            dve.tensor_tensor(nsT[:, cols], nsT[:, cols], gr[u], ALU.add).then_inc(gru_out, 1)

            def tile_prep(i, u, negatives):
                t = 2 * i + u
                dve.wait_ge(row_in[u], 16 * (i + 1))
                blk = arow[:, u, bass.ds(t * P, P)]
                dve.tensor_tensor(blk, blk, noteye[:, :], ALU.mult).then_inc(row_free, 1)
                dve.wait_ge(row_free, t + 1)
                if negatives:
                    dve.tensor_scalar(mneg[:, :], arow[:, u, :], 0.0, None, ALU.is_lt)
                dve.tensor_scalar(nb[:, :], arow[:, u, :], 0.0, NEG, ALU.is_equal, ALU.mult).then_inc(prep, 1)
                dve.wait_ge(prep, t + 1)

            def score(i, kk, negatives):
                h, s, k = kk % 3, kk % RING, 6 * i + kk
                reached(dve, tp_ready, 4 * (k - 5))
                if negatives:
                    dve.tensor_copy(ring[:, s, :], eb[:, h, :]).then_inc(e_copied, 1)
                    dve.wait_ge(e_copied, k + 1)
                    waited(dve)
                    dve.copy_predicated(ring[:, s, :], mneg[:, :], eb[:, HEADS + h, :]).then_inc(picked, 1)
                    dve.wait_ge(picked, k + 1)
                waited(dve)
                dve.tensor_tensor_reduce(ring[:, s, :], ring[:, s, :] if negatives else eb[:, h, :], nb[:, :], 1.0, FAR,
                                         ALU.add, ALU.min, mn[:, s:s + 1]).then_inc(s_ready, 1)

            def combine(i, kk):
                kk, i = (kk, i) if kk >= 0 else (kk + 6, i - 1)
                h, s, k, u = kk % 3, kk % RING, 6 * i + kk, kk // 3
                dve.wait_ge(z_ready, k + 1)
                dve.reciprocal(rden[:, s:s + 1], den[:, s:s + 1]).then_inc(rd_ok, 1)
                dve.wait_ge(rd_ok, k + 1)
                dve.wait_ge(mm_done, k + 1)
                o = ps[:, 4 + kk % 2, 0:D]
                if h == 0:
                    reached(dve, es_tp, 2 * i + u - 1)
                    dve.tensor_scalar(esb[:, u, :], o, rden[:, s:s + 1], None, ALU.mult).then_inc(es_acc, 1)
                else:
                    dve.wait_ge(es_acc, k)
                    dve.scalar_tensor_tensor(esb[:, u, :], o, rden[:, s:s + 1], esb[:, u, :],
                                             ALU.mult, ALU.add).then_inc(es_acc, 1)

            def steps(i, negatives, first=False):
                for kk in range(6):
                    if first and kk < 3:
                        continue
                    if kk % 3 == 0:
                        tile_prep(i, kk // 3, negatives)
                    score(i, kk, negatives)
                    if not (first and kk < 4):
                        combine(i, kk - 4)

            def attention(negatives):
                tile_prep(0, 0, negatives)
                for kk in range(3):
                    score(0, kk, negatives)
                gru(0)
                dve.wait_ge(gru_out, NC)
                steps(0, negatives, first=True)
                with dve.Fori(1, NT // 2) as i:
                    steps(i, negatives)
                for kk in range(2, 6):
                    combine(NT // 2 - 1, kk)

            dve.wait_ge(eb_ok, HEADS)
            before = count[0]
            negative = dve.value_load(any_neg[0:1, 0:1], min_val=0, max_val=N * N)
            with dve.If(negative > 0):
                for q in range(HEADS, NS):
                    leaky(q)
                dve.wait_ge(eb_ok, NS)
                attention(True)
            count[0] = before
            with dve.Else():
                attention(False)
            gru(1)
            for t in range(NT):
                q = t // TC
                dve.wait_ge(x1_tp, (q + 1) * TC)
                dve.scalar_tensor_tensor(xr[:, t, :], ps[:, X1_BANK(q), (t % TC) * P:(t % TC + 1) * P],
                                         diag[:, t:t + 1], xr[:, t, :], ALU.mult, ALU.add).then_inc(x1_ok, 1)
                if t % TC == TC - 1:
                    dve.wait_ge(x1_ok, t + 1)
                    for r in range(t - TC + 1, t + 1):
                        stats(r)

            def hyd(name, ins):
                ins.then_inc(hy_dve, 1)
                dve.wait_ge(hy_dve, HY_DVE[name])

            dve.wait_ge(ld_slice, 80)
            hyd("bias_cols", dve.tensor_copy(bx_cols[0:64, :, :], bx[0:64, :].unsqueeze(2).broadcast_to([64, SLOPES, P])))
            hyd("inv_temp", dve.tensor_scalar(temp, temp, 1e-6, None, ALU.max))
            link(dve.reciprocal(temp, temp))
            by_head = lambda v: v.rearrange("p (h g) -> p h g", h=SLOPES)
            spread = lambda v: v.unsqueeze(2).broadcast_to([P, SLOPES, G])
            dve.wait_ge(hy_pe, HY_PE["slice_w"])
            hyd("slice_w", dve.tensor_tensor(by_head(w_slice), by_head(ps[:, 4, :]), spread(temp), ALU.mult))
            dve.wait_ge(hy_pe, HY_PE["slice_b"])
            hyd("slice_b1", dve.tensor_tensor(by_head(b_slice), by_head(ps[:, 5, :]),
                                              bsl.unsqueeze(1).broadcast_to([P, SLOPES, G]), ALU.add))
            hyd("slice_b2", dve.tensor_tensor(by_head(b_slice), by_head(b_slice), spread(temp), ALU.mult))
            link(dve.memset(b_rows, 0.0))
            dve.memset(ones16[:, :], 1.0)
            rest = b_slice
            for n in range(3):
                link(dve.tensor_copy(b_part, rest))
                ins = dve.tensor_copy(b_rows[32 * n:32 * n + 1, :], b_part[32 * n:32 * n + 1, :])
                if n < 2:
                    link(dve.tensor_tensor(b_rest[n], rest, b_part, ALU.subtract))
                    rest = b_rest[n]
            hyd("slice_b", ins)
            aggregate(1, range(NT))
            for q in range(NC):
                finish(1, q)
            dve.memset(ones, 1.0).then_inc(ones_ok, 1)

            def slice_in(t):
                dve.wait_ge(lg_mm, t + 1)
                if t >= 8:
                    dve.wait_ge(sw_tp, t - 7)
                    dve.wait_ge(sw_sum, t - 7)
                lg = by_head(ps[:, 4 + t % 2, :])
                dve.tensor_reduce(mx8[t % 4], lg, AX.X, ALU.max).then_inc(lg_max, 1)
                dve.wait_ge(lg_max, t + 1)
                dve.tensor_tensor(by_head(sw[t % 8]), lg, spread(mx8[t % 4]), ALU.subtract).then_inc(lg_sub, 1)

            def slice_out(t):
                dve.wait_ge(lg_exp, t + 1)
                link(dve.tensor_reduce(rs8[t % 4], by_head(sw[t % 8]), AX.X, ALU.add))
                dve.reciprocal(rs8[t % 4], rs8[t % 4]).then_inc(lg_sum, 1)

            for t in range(NT):
                slice_in(t)
                if t >= 2:
                    slice_out(t - 2)
            slice_out(NT - 2)
            slice_out(NT - 1)

            dve.wait_ge(ld_hy, 16 * len(HY_LOADS))
            dve.wait_ge(hy_pe, HY_PE["snorm"])
            snorm = ps[:, 7, :]
            hyd("snorm_eps", dve.tensor_scalar(rsn, snorm, 1e-5, None, ALU.add))
            hyd("snorm_inv", dve.reciprocal(rsn, rsn))
            hyd("tok_w", dve.tensor_tensor(tok_n, ps[:, 6, :], rsn, ALU.mult))
            hyd("snorm_n", dve.tensor_tensor(sn_n, snorm, rsn, ALU.mult))
            halves = ((slice(0, 64), slice(0, 64)), (slice(64, 128), slice(64, 128)))
            snv = sn_n.rearrange("p (m g) -> p m g", m=CB)
            for n, (r, g) in enumerate(halves):
                hyd(f"tok_b{n}", dve.tensor_tensor(tokb[r, :, :], snv[r, :, g], bfx[r, :].unsqueeze(2).broadcast_to([64, CB, G]),
                                                   ALU.mult))
            dve.wait_ge(hy_pe, HY_PE["tokens"])
            tps = ps[:, 0, :].rearrange("p (m g) -> p m g", m=CB)
            for n, (r, g) in enumerate(halves):
                hyd(f"tok{n}", dve.tensor_tensor(tokT[r, :, :], tps[r, :, g], tokb[r, :, :], ALU.add))
            link(dve.memset(xp, 0.0))
            link(dve.memset(xs, 0.0))
            link(dve.memset(bd, 0.0))
            dve.wait_ge(hy_pe, HY_PE["bcdt"])
            hyd("dt_in", dve.tensor_tensor(dt_s[0], ps[:, 3, 0:SLOPES], dtb, ALU.add))
            hyd("dt_neg", dve.tensor_scalar(dt_s[1], dt_s[0], -1.0, None, ALU.mult))
            hyd("dt_nabs", dve.tensor_tensor(dt_s[1], dt_s[1], dt_s[0], ALU.min))
            link(dve.tensor_copy(xp[0:64, CB:6, 2:PADW], ps[0:64, 2, 0:2 * G].rearrange("p (k g) -> p k g", k=2)))
            dve.wait_ge(hy_pe, HY_PE["x"])
            hyd("pad", dve.tensor_copy(xp[:, 0:CB, 2:PADW], ps[:, 1, 0:CB * G].rearrange("p (k g) -> p k g", k=CB)))
            tap = lambda k: cw[:, :, k].unsqueeze(2).broadcast_to([P, 6, G])
            hyd("conv0", dve.tensor_tensor(cva, xp[:, :, 0:G], tap(0), ALU.mult))
            hyd("conv1", dve.tensor_tensor(cvt, xp[:, :, 1:G + 1], tap(1), ALU.mult))
            hyd("conv01", dve.tensor_tensor(cva, cva, cvt, ALU.add))
            hyd("conv2", dve.tensor_tensor(cvt, xp[:, :, 2:G + 2], tap(2), ALU.mult))
            hyd("conv012", dve.tensor_tensor(cva, cva, cvt, ALU.add))
            hyd("conv_b", dve.tensor_tensor(cva, cva, cb.unsqueeze(2).broadcast_to([P, 6, G]), ALU.add))
            dve.wait_ge(hy_act, HY_ACT["dt_ln"])
            hyd("dt", dve.scalar_tensor_tensor(dt_s[4], dt_s[0], 0.0, dt_s[3], ALU.max, ALU.add))
            hyd("decay_rate", dve.scalar_tensor_tensor(dt_s[0], dt_s[4], -1.0, rate, ALU.mult, ALU.mult))
            hyd("decay_in", dve.tensor_tensor(dec, spread(dt_s[0]), m_rt.unsqueeze(1).broadcast_to([P, SLOPES, G]), ALU.mult))
            dve.wait_ge(hy_act, HY_ACT["conv_exp"])
            hyd("silu_den", dve.tensor_scalar(cvt, cvt, 1.0, None, ALU.add))
            hyd("silu_inv", dve.reciprocal(cvt, cvt))
            hyd("xbc", dve.tensor_tensor(xs[:, :, 1:G + 1], cva, cvt, ALU.mult))
            hyd("x_twice", dve.tensor_copy(xd, xs[:, 0:CB, 1:G + 1].unsqueeze(2).broadcast_to([P, CB, 2, G])))
            dve.wait_ge(hy_pe, HY_PE["gram"])
            hyd("gram", dve.tensor_tensor(gramm, ps[:, 3, G:2 * G], m_st, ALU.mult))
            dve.wait_ge(hy_act, HY_ACT["decay_exp"])
            hyd("weight_dt", dve.tensor_tensor(dec, dec, spread(dt_s[4]), ALU.mult))
            hyd("weight", dve.tensor_tensor(dec, dec, gramm.unsqueeze(1).broadcast_to([P, SLOPES, G]), ALU.mult))
            dve.wait_ge(hy_act, HY_ACT["z_exp"])
            hyd("z_den", dve.tensor_scalar(z1, z1, 1.0, None, ALU.add))
            hyd("z_inv", dve.reciprocal(z1, z1))
            hyd("z", dve.tensor_tensor(z1, z1, zz, ALU.mult))
            dve.wait_ge(hy_pe, HY_PE["skip"])
            skp = ps[:, 7, 0:CB * G].rearrange("p (k g) -> p k g", k=CB)
            cols = lambda v: v.unsqueeze(2).broadcast_to([P, CB, G])
            hyd("skip_d", dve.tensor_tensor(y1, skp, cols(dcol), ALU.add))
            hyd("skip", dve.tensor_tensor(y1, y1, xs[:, 0:CB, 1:G + 1], ALU.mult))
            dve.wait_ge(hy_pe, HY_PE["y"])
            hyd("y", dve.tensor_tensor(y1, ps[:, 6, 0:CB * G].rearrange("p (k g) -> p k g", k=CB), y1, ALU.add))
            hyd("yg", dve.tensor_tensor(y1, y1, z1, ALU.mult))
            hyd("sq", dve.tensor_tensor(ysq, y1, y1, ALU.mult))
            dve.wait_ge(hy_act, HY_ACT["rms_std"])
            hyd("rms", dve.reciprocal(rms, rms))
            hyd("yn", dve.tensor_tensor(y1, y1, rms.unsqueeze(1).broadcast_to([P, CB, G]), ALU.mult))
            hyd("ynw", dve.tensor_tensor(y1, y1, cols(nwcol), ALU.mult))
            dve.wait_ge(hy_pe, HY_PE["out"])
            ops_ = ps[:, 3, 0:CB * G].rearrange("p (k g) -> p k g", k=CB)
            for n, (r, g) in enumerate(halves):
                hyd(f"ot{n}", dve.tensor_copy(bd[r, :, g], ops_[r, :, :]))
            for q in range(NC):
                dve.wait_ge(x2_mm, q + 1)
                if q == 0:
                    dve.wait_ge(outb_ok, 1)
                rows_ = xr[:, q * TC:(q + 1) * TC, :]
                dve.tensor_tensor(rows_, ps[:, q % 4, :].rearrange("p (t d) -> p t d", t=TC), rows_,
                                  ALU.add).then_inc(x2_ok, 1)
                dve.wait_ge(x2_ok, q + 1)
                ts = range(q * TC, (q + 1) * TC)
                for t in ts:
                    stats(t)
                aggregate(2, ts)
                finish(2, q)

            dve.wait_ge(ld_moe, 16 * len(MOE_LOADS))
            dve.tensor_copy(hv_cols, hv.broadcast_to([P, D])).then_inc(hv_ok, 1)

            def g_scores(i, kk):
                kk, i = (kk, i) if kk < 4 else (kk - 4, i + 1)
                k, u, s = 4 * i + kk, kk % 2, kk % 4
                dve.wait_ge(row2_in[u], 16 * (2 * i + kk // 2 + 1))
                dve.tensor_scalar(nb[:, :], arow[:, u, :], 0.0, FLOOR, ALU.is_equal, ALU.mult).then_inc(g_mask, 1)
                dve.wait_ge(g_mask, k + 1)
                dve.wait_ge(g_prod, k + 1)
                waited(dve)
                dve.tensor_tensor_reduce(ring[:, s, :], ring[:, s, :], nb[:, :], 1.0, FAR, ALU.add, ALU.min,
                                         mn[:, s:s + 1]).then_inc(g_min, 1)
                dve.wait_ge(g_min, k + 1)
                dve.tensor_scalar(mn[:, s:s + 1], mn[:, s:s + 1], FLOOR / 2, None, ALU.min).then_inc(g_score, 1)

            def g_combine(i, kk):
                kk, i = (kk, i) if kk >= 0 else (kk + 4, i - 1)
                k, s = 4 * i + kk, kk % 4
                dve.wait_ge(g_exp, k + 1)
                dve.tensor_scalar(rden[:, s:s + 1], den[:, s:s + 1], 1e-30, None, ALU.max).then_inc(g_den, 1)
                dve.wait_ge(g_den, 2 * k + 1)
                dve.reciprocal(rden[:, s:s + 1], rden[:, s:s + 1]).then_inc(g_den, 1)
                dve.wait_ge(g_den, 2 * k + 2)
                dve.wait_ge(g_mm, k + 1)
                x = xr[:, k, :] if isinstance(k, int) else xr[:, bass.ds(k, 1), :].rearrange("p a d -> p (a d)")
                dve.scalar_tensor_tensor(x, ps[:, 4 + kk % 2, 0:D], rden[:, s:s + 1], x,
                                         ALU.mult, ALU.add).then_inc(x3_ok, 1)
                dve.wait_ge(x3_ok, k + 1)
                st = st6[:, k, :] if isinstance(k, int) else st6[:, bass.ds(k, 1), :].rearrange("p a d -> p (a d)")
                dve.bn_stats(st, x).then_inc(ln_bn, 1)

            def g_steps(i, first=False, last=False):
                for kk in range(4):
                    if not (last and kk + 3 >= 4):
                        g_scores(i, kk + 3)
                    if not (first and kk < 1):
                        g_combine(i, kk - 1)

            for kk in range(3):
                g_scores(0, kk)
            g_steps(0, first=True)
            with dve.Fori(1, NT // 4 - 1) as i:
                g_steps(i)
            g_steps(NT // 4 - 1, last=True)
            g_combine(NT // 4 - 1, 3)

            aggregate(3, range(NT))
            for q in range(NC):
                finish(3, q)
            by_node = lambda v: v.unsqueeze(2).broadcast_to([P, NT, EXPERTS])
            by_expert = lambda v: v.unsqueeze(1).broadcast_to([P, NT, EXPERTS])
            dve.wait_ge(r_mm, 1)
            link(dve.tensor_tensor(route, ps[:, 4, 0:NT * EXPERTS].rearrange("p (t e) -> p t e", t=NT), by_expert(br), ALU.add))
            for v, hot in ((v1, hot1), (v2, hot2)):
                link(dve.tensor_reduce(v, route, AX.X, ALU.max))
                link(dve.tensor_tensor(top, route, by_node(v), ALU.is_equal))
                link(dve.tensor_tensor(top, top, by_expert(prio), ALU.mult))
                link(dve.tensor_reduce(ky, top, AX.X, ALU.max))
                link(dve.tensor_tensor(hot, top, by_node(ky), ALU.is_equal))
                if hot is hot1:
                    link(dve.scalar_tensor_tensor(route, hot, -FAR, route, ALU.mult, ALU.add))
            dve.tensor_tensor(v2, v2, v1, ALU.subtract).then_inc(r_dlt, 1)
            dve.wait_ge(r_exp, 1)
            link(dve.tensor_scalar(w1, ew, 1.0, None, ALU.add))
            link(dve.reciprocal(w1, w1))
            link(dve.tensor_tensor(ew, ew, w1, ALU.mult))
            link(dve.tensor_tensor(hot1, hot1, by_node(w1), ALU.mult))
            link(dve.tensor_tensor(hot2, hot2, by_node(ew), ALU.mult))
            dve.tensor_tensor(wfull, hot1, hot2, ALU.add).then_inc(r_w, 1)
            def add_b2(g):
                dve.wait_ge(acc_ok, 8 * (g // 2 + 1))
                dve.wait_ge(b2_mm, g + 1)
                rows_ = xr[:, g * TC:(g + 1) * TC, :]
                dve.tensor_tensor(rows_, ps[:, 6 + g % 2, :].rearrange("p (t d) -> p t d", t=TC), rows_,
                                  ALU.add).then_inc(b2_ok, 1)

            def add_expert(i, v):
                for q in range(NC):
                    st = 8 * i + 4 * v + q
                    dve.wait_ge(down_mm, st + 1)
                    for j in range(TC):
                        t = q * TC + j
                        w = wfull[:, t, 2 * i + v:2 * i + v + 1] if isinstance(i, int) else wfull[:, t, bass.ds(2 * i + v, 1)]
                        ins = dve.scalar_tensor_tensor(xr[:, t, :], ps[:, 4 + q % 2, j * P:(j + 1) * P], w, xr[:, t, :],
                                                       ALU.mult, ALU.add)
                    ins.then_inc(acc_ok, 1)

            dve.wait_ge(r_w, 1)
            add_expert(0, 0)
            add_expert(0, 1)
            add_b2(0)
            add_b2(1)
            dve.wait_ge(b2_ok, 2)
            add_expert(1, 0)
            add_expert(1, 1)
            add_b2(2)
            add_b2(3)
            dve.wait_ge(b2_ok, 4)
            with dve.Fori(2, EXPERTS // 2) as i:
                add_expert(i, 0)
                add_expert(i, 1)

        @block.gpsimd
        def _(pool):
            def weigh(i, kk):
                kk, i = (kk, i) if kk < 6 else (kk - 6, i + 1)
                s, k = kk % RING, 6 * i + kk
                pool.wait_ge(z_ready, k + 1)
                pool.tensor_tensor(ring[:, s, :], ring[:, s, :], arow[:, kk // 3, :], ALU.mult).then_inc(p_ready, 1)

            def steps(i, last=False):
                for kk in range(6):
                    if not (last and kk + 2 >= 6):
                        weigh(i, kk + 2)

            weigh(0, 0)
            weigh(0, 1)
            steps(0)
            with pool.Fori(1, NT // 2 - 1) as i:
                steps(i)
            steps(NT // 2 - 1, last=True)

            def slice_sum(t):
                pool.wait_ge(sw_ok, t + 1)
                if t == 0:
                    pool.tensor_copy(swsum, sw[0]).then_inc(sw_sum, 1)
                else:
                    pool.wait_ge(sw_sum, t)
                    pool.tensor_tensor(swsum, swsum, sw[t % 8], ALU.add).then_inc(sw_sum, 1)

            for t in range(NT):
                pool.wait_ge(lg_sum, t + 1)
                v = sw[t % 8].rearrange("p (h g) -> p h g", h=SLOPES)
                pool.tensor_tensor(v, v, rs8[t % 4].unsqueeze(2).broadcast_to([P, SLOPES, G]), ALU.mult).then_inc(sw_ok, 1)
                if t >= 1:
                    slice_sum(t - 1)
            slice_sum(NT - 1)
            pool.wait_ge(ld_hy, 16 * len(HY_LOADS))
            pool.wait_ge(ln_row, 2 * NT)
            pool.tensor_tensor(xr[:, :, :], xr[:, :, :], outb.unsqueeze(1).broadcast_to([P, NT, D]),
                               ALU.add).then_inc(outb_ok, 1)

            def product(i, kk):
                kk, i = (kk, i) if kk < 4 else (kk - 4, i + 1)
                k, u, s = 4 * i + kk, kk % 2, kk % 4
                pool.wait_ge(row2_in[u], 16 * (2 * i + kk // 2 + 1))
                reached(pool, g_tp, 4 * (k - 3))
                pool.tensor_tensor(ring[:, s, :], arow[:, u, :], sbn, ALU.mult).then_inc(g_prod, 1)

            pool.wait_ge(sc_ok, NC)
            for kk in range(4):
                product(0, kk)
            with pool.Fori(1, NT // 4) as i:
                for kk in range(4):
                    product(i, kk)

        @block.tensor
        def _(pe):
            def norm_turn(n, q, bank):
                for t in range(q * TC, (q + 1) * TC):
                    pe.wait_ge(ln_row, n * NT + t + 1)
                    ins = pe.transpose(ps[:, bank, (t % TC) * P:(t % TC + 1) * P], hrow[:, t, :], ident[:, :])
                ins.then_inc(ln_tp, 1)

            def norm_T(n, banks):
                for q in range(NC):
                    norm_turn(n, q, banks[q])

            pe.wait_ge(ld_c, 32)
            norm_T(0, (0, 1, 2, 3))
            pe.wait_ge(ld_gat, 64)
            for h in range(HEADS):
                ins = pe.matmul(ps[:, 7, h:NS:HEADS], gatWT[:, h * D:(h + 1) * D], gatA[:, :, h], start=True, stop=True)
            ins.then_inc(wa_mm, 1)
            pe.wait_ge(wa_sb, 1)
            pe.wait_ge(ln_hT, NC)
            for t in range(NT):
                ins = pe.matmul(ps[:, 6, t * NS:(t + 1) * NS], hT[:, t * P:(t + 1) * P], wa, start=True, stop=True)
            ins.then_inc(u_mm, 1)
            for j in range(NT + 2):
                if j < NT:
                    pe.wait_ge(aT_diag, j + 1)
                    if j == 0:
                        pe.wait_ge(ln_hT, NC)
                    for g in range(NC):
                        cols = slice(g * CH, (g + 1) * CH)
                        ins = pe.matmul(ps[:, g, :], hrow[:, j, :], aT[j % 3][:, cols],
                                        start=(j == 0), stop=(j == NT - 1))
                    ins.then_inc(aT_used, 1)
                if j >= 2:
                    m = j - 2
                    pe.wait_ge(masks_ok, m + 1)
                    if m == 0:
                        pe.wait_ge(parts_ok, 1)
                    for g in range(NC):
                        cols = slice(g * CH, (g + 1) * CH)
                        pe.matmul(ps[0:96, 4 + g, :], parts[:, 0, m, :], masks[:, m % 3, 0, cols],
                                  start=(m == 0), stop=False)
                        ins = pe.matmul(ps[0:96, 4 + g, :], parts[:, 1, m, :], masks[:, m % 3, 1, cols],
                                        start=False, stop=(m == NT - 1))
                    ins.then_inc(masks_used, 1)
            for n in range(NS * NC):
                g = n % NC
                if n < NC:
                    pe.wait_ge(mres_sb, g + 1)
                    pe.wait_ge(ns_sb, g + 1)
                else:
                    pe.wait_ge(bc_sb, n - 3)
                pe.matmul(ps[:, n % 4, :], sel[0:96, n // NC, :], mres[0:96, g * CH:(g + 1) * CH],
                          start=True, stop=True).then_inc(bc_mm, 1)

            pe.wait_ge(neg_ok, 1)
            pe.matmul(ps[0:1, 6, 0:1], n_neg1[:, :], n_one[:, :], start=True, stop=True).then_inc(neg_mm, 1)
            for j in range(NT):
                if j >= 2:
                    pe.wait_ge(hw_sb, j - 1)
                pe.matmul(ps[:, 4 + j % 2, 0:HEADS * D], hT[:, j * P:(j + 1) * P], gatW,
                          start=True, stop=True).then_inc(hw_mm, 1)

            def gru(n, srcT):
                for q in range(NC):
                    cols = slice(q * CH, (q + 1) * CH)
                    b = GRU_BANK(q)
                    c = n * NC + q
                    if n == 0:
                        if q == 0:
                            pe.wait_ge(ld_gru, 96)
                            pe.wait_ge(hw_sb, NT)
                            pe.wait_ge(neg_ok, 2)
                        if q == 1:
                            pe.wait_ge(bc_sb, NS * NC)
                    if n == 1 and q == 0:
                        pe.wait_ge(es_T, NT)
                    if q >= 2:
                        pe.wait_ge(gru_z, c - 1)
                        pe.wait_ge(gru_t, c - 1)
                    for gate in range(2):
                        w = slice(gate * D, (gate + 1) * D)
                        pe.matmul(ps[:, b + gate, :], WT[2 * n][:, w], srcT[:, cols], start=True, stop=False)
                        pe.matmul(ps[:, b + gate, :], WT[2 * n + 1][:, w], hT[:, cols],
                                  start=False, stop=True).then_inc(gru_mm, 1)
                    w = slice(2 * D, 3 * D)
                    pe.matmul(ps[:, b + 2, :], WT[2 * n + 1][:, w], hT[:, cols], start=True, stop=True).then_inc(gru_mm, 1)
                    pe.matmul(ps[:, b + 3, :], WT[2 * n][:, w], srcT[:, cols], start=True, stop=True).then_inc(gru_mm, 1)

            gru(0, nsT)

            def turn(i, kk):
                kk, i = (kk, i) if kk < 6 else (kk - 6, i + 1)
                s, k = kk % RING, 6 * i + kk
                pe.wait_ge(p_ready, k + 1)
                for b in range(4):
                    reached(pe, tp_out, 4 * (k - 1) + b + 1)
                    for j in range(4):
                        c = (4 * b + j) * P
                        ins = pe.transpose(ps[:, b, j * P:(j + 1) * P], ring[:, s, c:c + P], ident[:, :])
                    ins.then_inc(tp_ready, 1)

            def attend(i, kk):
                h, k = kk % 3, 6 * i + kk
                pe.wait_ge(tp_out, 4 * (k + 1))
                reached(pe, es_acc, k - 1)
                for j in range(NT):
                    ins = pe.matmul(ps[:, 4 + kk % 2, 0:D], pat[:, kk % 2, j * P:(j + 1) * P],
                                    hW[:, j, h * D:(h + 1) * D], start=(j == 0), stop=(j == NT - 1))
                ins.then_inc(mm_done, 1)

            def es_turn(t, u):
                pe.wait_ge(es_acc, 3 * (t + 1))
                reached(pe, es_T, t - 1)
                pe.transpose(ps[:, 6 + u, 0:P], esb[:, u, :], ident[:, :]).then_inc(es_tp, 1)

            def steps(i, first=False, last=False):
                for kk in range(6):
                    if kk % 3 == 2 and not (first and kk == 2):
                        es_turn(2 * i + kk // 3 - 1, 1 - kk // 3)
                    if not (last and kk == 5):
                        turn(i, kk + 1)
                    attend(i, kk)

            pe.wait_ge(gru_t, NC)
            pe.wait_ge(gru_z, NC)
            turn(0, 0)
            steps(0, first=True)
            with pe.Fori(1, NT // 2 - 1) as i:
                steps(i)
            steps(NT // 2 - 1, last=True)
            es_turn(NT - 1, 1)
            gru(1, esT)
            for t in range(NT):
                q = t // TC
                if t % TC == 0:
                    pe.wait_ge(gru_out, NC + q + 1)
                    if q == 0:
                        pe.wait_ge(gru_t, 2 * NC)
                        pe.wait_ge(gru_z, 2 * NC)
                pe.transpose(ps[:, X1_BANK(q), (t % TC) * P:(t % TC + 1) * P], nsT[:, t * P:(t + 1) * P],
                             ident[:, :]).then_inc(x1_tp, 1)
            pe.wait_ge(ld_slice, 80)
            for h in range(SLOPES):
                ins = pe.matmul(ps[:, 4, h * G:(h + 1) * G], wx[0:64, h, :], wsT[0:64, :], start=True, stop=True)
            ins.then_inc(hy_pe, 1)
            pe.wait_ge(hy_dve, HY_DVE["bias_cols"])
            for h in range(SLOPES):
                ins = pe.matmul(ps[:, 5, h * G:(h + 1) * G], bx_cols[0:64, h, :], wsT[0:64, :], start=True, stop=True)
            ins.then_inc(hy_pe, 1)
            norm_T(1, (0, 1, 2, 3))

            def logits(t):
                if t == 0:
                    pe.wait_ge(hy_dve, HY_DVE["slice_b"])
                if t % TC == 0:
                    pe.wait_ge(ln_hT, NC + t // TC + 1)
                if t >= 2:
                    pe.wait_ge(lg_sub, t - 1)
                pe.matmul(ps[:, 4 + t % 2, :], ones16[0:96, :], b_rows[0:96, :], start=True, stop=False)
                pe.matmul(ps[:, 4 + t % 2, :], hT[:, t * P:(t + 1) * P], w_slice, start=False, stop=True).then_inc(lg_mm, 1)

            def gather(t):
                pe.wait_ge(sw_ok, t + 1)
                if t == 0:
                    pe.wait_ge(ln_hT, 2 * NC)
                pe.matmul(ps[:, 6, :], hrow[:, t, :], sw[t % 8], start=(t == 0), stop=(t == NT - 1))
                if t >= 2:
                    pe.wait_ge(sw_T, t - 1)
                for m in range(CB):
                    ins = pe.transpose(ps[:, t % 2, m * P:(m + 1) * P], sw[t % 8][:, m * P:(m + 1) * P], ident[:, :])
                ins.then_inc(sw_tp, 1)

            for t in range(NT):
                logits(t)
                if t >= 3:
                    gather(t - 3)
            for t in range(NT - 3, NT):
                gather(t)

            pe.wait_ge(ones_ok, 1)
            pe.wait_ge(sw_sum, NT)
            pe.matmul(ps[:, 7, :], ones, swsum, start=True, stop=True).then_inc(hy_pe, 1)
            pe.wait_ge(hy_dve, HY_DVE["tok_w"])
            pe.wait_ge(sw_T, NT)
            for m in range(CB):
                ins = pe.matmul(ps[:, 0, m * P:(m + 1) * P], wfxT[:, m * P:(m + 1) * P], tok_n[:, m * P:(m + 1) * P],
                                start=True, stop=True)
            ins.then_inc(hy_pe, 1)
            pe.wait_ge(hy_dve, HY_DVE["tok1"])

            def project(o, w_of, x_of):
                for k in range(CB):
                    ins = pe.matmul(o, w_of(k), x_of(k), start=(k == 0), stop=(k == CB - 1))
                return ins

            for m in range(2):
                c = 2 * DI + m * G
                project(ps[0:64, 2, m * G:(m + 1) * G], lambda k: in_wT[:, k, c:c + G], lambda k: tokT[:, k, :])
            for v in range(2):
                c = 2 * DI + 2 * G + v * SLOPES
                ins = project(ps[64 * v:64 * v + 64, 3, 0:SLOPES], lambda k: tokT[:, k, :], lambda k: in_wT[:, k, c:c + SLOPES])
            ins.then_inc(hy_pe, 1)
            for first, bank in ((DI, 1), (0, 0)):
                for m in range(CB):
                    c = first + m * P
                    ins = project(ps[:, bank, m * G:(m + 1) * G], lambda k: in_wT[:, k, c:c + P], lambda k: tokT[:, k, :])
                ins.then_inc(hy_pe, 1)
            pe.wait_ge(hy_dve, HY_DVE["decay_in"])
            pe.matmul(ps[:, 5, :], m_rs, dec, start=True, stop=True).then_inc(hy_pe, 1)
            pe.wait_ge(hy_dve, HY_DVE["x_twice"])
            for v in range(2):
                ins = pe.matmul(ps[64 * v:64 * v + 64, 3, G:2 * G], xs[0:64, CB, 1:G + 1],
                                xs[0:64, CB + 1, 2 * v:2 * v + G], start=True, stop=True)
            ins.then_inc(hy_pe, 1)
            for m in range(CB):
                ins = pe.transpose(ps[:, 4, m * P:(m + 1) * P], xd[:, m, :, :].rearrange("p v g -> p (v g)"), ident[:, :])
            ins.then_inc(hy_pe, 1)
            for m in range(CB):
                ins = project(ps[:, 7, m * G:(m + 1) * G], lambda k: fcDT[:, k, m * P:(m + 1) * P],
                              lambda k: xs[:, k, 1:G + 1])
            ins.then_inc(hy_pe, 1)
            pe.wait_ge(hy_act, HY_ACT["x_rows"])
            pe.wait_ge(hy_dve, HY_DVE["weight"])
            for h in range(SLOPES):
                ins = pe.matmul(ps[64 * (h % 2):64 * (h % 2) + 64, 6, (h // 2) * G:(h // 2 + 1) * G],
                                x2[:, h * 64:(h + 1) * 64], dec[:, h, :], start=True, stop=True)
            ins.then_inc(hy_pe, 1)
            pe.wait_ge(hy_dve, HY_DVE["sq"])
            project(ps[:, 2, 0:G], lambda k: ones, lambda k: ysq[:, k, :]).then_inc(hy_pe, 1)
            pe.wait_ge(hy_dve, HY_DVE["ynw"])
            for m in range(CB):
                ins = project(ps[:, 3, m * G:(m + 1) * G], lambda k: outT[:, k, m * P:(m + 1) * P], lambda k: y1[:, k, :])
            ins.then_inc(hy_pe, 1)
            pe.wait_ge(hy_dve, HY_DVE["ot1"])
            for m in range(CB):
                ins = pe.matmul(ps[:, 4, m * P:(m + 1) * P], bd[:, m, :], outwT[:, m, :], start=True, stop=True)
            ins.then_inc(hy_pe, 1)
            pe.wait_ge(hy_act, HY_ACT["value"])
            for t in range(NT):
                for m in range(CB):
                    ins = pe.matmul(ps[:, (t // TC) % 4, (t % TC) * P:(t % TC + 1) * P], swT[:, m, t * P:(t + 1) * P],
                                    val[:, m, :], start=(m == 0), stop=(m == CB - 1))
                if t % TC == TC - 1:
                    ins.then_inc(x2_mm, 1)
                    if t // TC >= 1:
                        norm_turn(2, t // TC - 1, 3 + t // TC)

            norm_turn(2, NC - 1, 3 + NC)
            pe.wait_ge(hv_ok, 1)
            for g in range(NC):
                pe.wait_ge(ln_hT, 2 * NC + g + 1)
                pe.matmul(ps[:, g, :], hv_cols, hT[:, g * CH:(g + 1) * CH], start=True, stop=True).then_inc(sc_mm, 1)

            def g_turn(i, kk):
                kk, i = (kk, i) if kk < 4 else (kk - 4, i + 1)
                k = 4 * i + kk
                pe.wait_ge(g_exp, k + 1)
                for b in range(4):
                    if isinstance(k, int) and k == 0:
                        pe.wait_ge(sc_ok, NC)
                    reached(pe, g_out, 4 * (k - 1) + b + 1)
                    for j in range(4):
                        c = (4 * b + j) * P
                        ins = pe.transpose(ps[:, b, j * P:(j + 1) * P], ring[:, kk, c:c + P], ident[:, :])
                    ins.then_inc(g_tp, 1)

            def g_attend(i, kk):
                k = 4 * i + kk
                pe.wait_ge(g_out, 4 * (k + 1))
                reached(pe, x3_ok, k - 1)
                for j in range(NT):
                    ins = pe.matmul(ps[:, 4 + kk % 2, 0:D], pat[:, kk % 2, j * P:(j + 1) * P], hrow[:, j, :],
                                    start=(j == 0), stop=(j == NT - 1))
                ins.then_inc(g_mm, 1)

            def g_steps(i, last=False):
                for kk in range(4):
                    if not (last and kk + 1 >= 4):
                        g_turn(i, kk + 1)
                    g_attend(i, kk)

            g_turn(0, 0)
            g_steps(0)
            with pe.Fori(1, NT // 4 - 1) as i:
                g_steps(i)
            g_steps(NT // 4 - 1, last=True)

            norm_T(3, (4, 5, 6, 7))
            for t in range(NT):
                if t % TC == 0:
                    pe.wait_ge(ln_hT, 3 * NC + t // TC + 1)
                ins = pe.matmul(ps[:, 4, t * EXPERTS:(t + 1) * EXPERTS], hT[:, t * P:(t + 1) * P], wr, start=True, stop=True)
            ins.then_inc(r_mm, 1)
            def router_turn(g):
                reached(pe, r_wT, g - 1)
                for t in range(g * TC, (g + 1) * TC):
                    ins = pe.transpose(ps[0:EXPERTS, 6 + g % 2, (t % TC) * P:(t % TC + 1) * P], wfull[:, t, :], ident[:, :])
                ins.then_inc(r_tp, 1)

            def second_bias(g):
                pe.wait_ge(r_wT, NC)
                reached(pe, b2_ok, g - 1)
                for t in range(g * TC, (g + 1) * TC):
                    ins = pe.matmul(ps[:, 6 + g % 2, (t % TC) * P:(t % TC + 1) * P], wT[:, t * P:(t + 1) * P],
                                    b2[0:EXPERTS, :], start=True, stop=True)
                ins.then_inc(b2_mm, 1)

            def up(i, v, q, first=False):
                st = 8 * i + 4 * v + q
                if q == 0:
                    pe.wait_ge(ld_exp[v], 32 * (i + 1))
                for c in range(HC):
                    if not (first and st < 2):
                        pe.wait_ge(gelu_ok, HC * (st - 2) + c + 1)
                    pe.matmul(ps[:, 2 * (q % 2) + c, :], wexp[v][0][:, c * P:(c + 1) * P], hT[:, q * CH:(q + 1) * CH],
                              start=True, stop=True).then_inc(up_mm, 1)

            def down(i, v, q, first=False):
                v, i, q = (v, i, q) if q >= 0 else (1 - v, i - (1 - v), q + NC)
                st = 8 * i + 4 * v + q
                pe.wait_ge(gelu_ok, HC * (st + 1))
                if first and st < 2:
                    pe.wait_ge(r_w, 1)
                else:
                    pe.wait_ge(acc_ok, st - 1)
                for j in range(TC):
                    for c in range(HC):
                        ins = pe.matmul(ps[:, 4 + q % 2, j * P:(j + 1) * P], hid[:, q % 2, c, j * P:(j + 1) * P],
                                        wexp[v][1][:, c, :], start=(c == 0), stop=(c == HC - 1))
                ins.then_inc(down_mm, 1)

            def expert(i, v, first=False):
                for q in range(NC):
                    up(i, v, q, first)
                    if first and v == 0 and q < 2:
                        if q == 1:
                            down(i, v, 0, first)
                        continue
                    down(i, v, q - 1, first)

            expert(0, 0, first=True)
            router_turn(0)
            router_turn(1)
            expert(0, 1, first=True)
            router_turn(2)
            router_turn(3)
            second_bias(0)
            second_bias(1)
            expert(1, 0)
            expert(1, 1)
            second_bias(2)
            second_bias(3)
            with pe.Fori(2, EXPERTS // 2) as i:
                expert(i, 0)
                expert(i, 1)
            down(EXPERTS // 2 - 1, 1, NC - 1)


def GRU_BANK(q):
    return 4 if q % 2 == 0 else 0


def X1_BANK(q):
    return q




def lay_out(inputs):
    c = np.ascontiguousarray
    i = {k: np.asarray(v) for k, v in inputs.items()}
    adj = i["adj"]
    T = lambda w: c(w.T)
    o = {"x": c(i["x"]), "adjT": c(adj.T), "adj_t": c(adj.reshape(NT, P, N)),
         "diag": c(np.diagonal(adj).reshape(NT, P).T)}
    eye = np.eye(P, dtype=np.float32)
    o["ident"] = eye
    o["noteye"] = np.ones((P, P), np.float32)
    np.fill_diagonal(o["noteye"], 0)
    sel = np.zeros((96, NS, P), np.float32)
    for q in range(NS):
        sel[q::32, q, :] = 1
    o["sel"] = sel
    W = i["L0_gnn_gat_W"]
    o["gat_WT"] = c(W.transpose(2, 0, 1).reshape(D, HEADS * D))
    o["gat_W"] = c(W.transpose(1, 0, 2).reshape(D, HEADS * D))
    o["gat_a"] = c(i["L0_gnn_gat_a"].reshape(HEADS, 2, D).transpose(2, 1, 0))
    gru = ("L0_gnn_edge_", "L0_gnn_node_")
    o["gru_WT"] = c(np.stack([i[g + w].T for g in gru for w in ("Wih", "Whh")]))
    o["gru_b"] = c(np.stack([i[g + b].reshape(3, D) for g in gru for b in ("bih", "bhh")]).transpose(2, 0, 1))
    f = "L0_ffn_"
    across = lambda v, n: c(np.broadcast_to(v, (n,) + v.shape))
    cols = lambda v: c(v.reshape(-1, P).T)
    o["wx"] = c(i[f + "W_x"].reshape(SLOPES, 64, D).transpose(1, 0, 2))
    o["wsT"] = T(i[f + "W_slice"])
    o["bx"] = T(i[f + "b_x"].reshape(SLOPES, 64))
    o["b_slice"] = across(i[f + "b_slice"], P)
    o["temp"] = across(i[f + "temperature"].reshape(-1), P)
    chunks = lambda w: c(w.T.reshape(CB, P, -1).transpose(1, 0, 2))
    o["in_wT"] = chunks(i[f + "hy_in_w"])
    o["wfxT"] = T(i[f + "W_fx"])
    o["bfx"] = cols(i[f + "b_fx"])
    cw, cb = i[f + "hy_conv_w"], i[f + "hy_conv_b"]
    w6, b6 = np.zeros((P, 6, 3), np.float32), np.zeros((P, 6), np.float32)
    w6[:, :CB] = cw[:DI].reshape(CB, P, 3).transpose(1, 0, 2)
    w6[:64, CB:] = cw[DI:].reshape(2, 64, 3).transpose(1, 0, 2)
    b6[:, :CB] = cb[:DI].reshape(CB, P).T
    b6[:64, CB:] = cb[DI:].reshape(2, 64).T
    o["cw"], o["cb"] = w6, b6
    o["dtb"] = across(i[f + "hy_dt_bias"], P)
    o["alog"] = across(i[f + "hy_A_log"], P)
    r = np.arange(64)
    m_rs, m_rt, m_st = np.zeros((P, P), np.float32), np.zeros((P, G), np.float32), np.zeros((P, G), np.float32)
    m_rs[:64, :64] = r[:, None] > r[None, :]
    m_rs[64:, 64:] = r[:, None] < r[None, :]
    m_rt[:64], m_rt[64:] = r[:, None] <= r[None, :] - 1, r[:, None] >= r[None, :] + 1
    m_st[:64], m_st[64:] = r[:, None] <= r[None, :] - 1, r[:, None] >= r[None, :] + 1
    o["m_rs"], o["m_rt"], o["m_st"] = m_rs, m_rt, m_st
    o["outb"] = across(i[f + "out_b"], P)
    o["fcDT"] = chunks(np.repeat(i[f + "hy_fcD_w"], 64, axis=0))
    o["dcol"] = cols(np.repeat(i[f + "hy_D"], 64))
    o["nwcol"] = cols(i[f + "hy_norm_w"])
    o["outT"] = chunks(i[f + "hy_out_w"])
    o["outwT"] = chunks(i[f + "out_w"])
    e = "L1_ffn_"
    o["hv"] = c(i["L1_gnn_H_v"])
    o["gamma"], o["beta"] = c(i[e + "gamma"][:, None]), c(i[e + "beta"][:, None])
    o["Wr"], o["br"] = c(i[e + "Wr"]), across(i[e + "br"], P)
    o["prio"] = across(np.arange(EXPERTS, 0, -1).astype(np.float32), P)
    o["b1"] = c(i[e + "b1"].reshape(EXPERTS, HC, P).transpose(2, 0, 1))
    o["b2"] = c(i[e + "b2"])
    o["W1"] = c(i[e + "W1"])
    o["W2"] = c(i[e + "W2"].reshape(EXPERTS, HC, P, D).transpose(0, 2, 1, 3))
    return o


def kernel(**inputs):
    import concourse.bacc as _bacc
    from concourse.bass_utils import run_bass_kernel_spmd as _run

    nc = _bacc.Bacc("TRN2", target_bir_lowering=False, num_devices=1)
    arrays, args = {}, {}
    for name, a in lay_out(inputs).items():
        arrays[f"in_{name}"] = a
        args[name] = nc.dram_tensor(f"in_{name}", a.shape, mybir.dt.from_np(a.dtype), kind="ExternalInput").ap()
    out = nc.dram_tensor("out_0", (N, D), F32, kind="ExternalOutput").ap()
    graph_block(nc, args, out)
    r = _run(nc, [arrays], core_ids=[0])
    return r.results[0]["out_0"]
```

```python
from contextlib import ExitStack

import numpy as np

import concourse.bass as bass
from concourse import mybir

ALU = mybir.AluOpType
ACT = mybir.ActivationFunctionType
AX = mybir.AxisListType
F32 = mybir.dt.float32
BF16 = mybir.dt.bfloat16
U8 = mybir.dt.uint8

P = 128
N = 2048
D = 128
NT = N // P
CH = 512
NC = N // CH
TC = CH // P
HEADS = 3
NS = 2 * HEADS
RING = 6
EPS = 1e-5
FLOOR = 1e30
NEG = 9e15
FAR = 3e38
GAT_ALPHA = 0.2
SLOPES = 8
G = 64
DI = 512
CB = DI // P
EXPERTS = 8
HID = 256
HC = HID // P


LOGIT_BANKS = (4, 5, 3)


def numbered(*names):
    return {name: n + 1 for n, name in enumerate(names)}


HY_PE = numbered("slice_w", "slice_b", "snorm", "tokens", "bcdt", "x", "decay", "z", "gram", "skip8", "x_rows", "skip",
                 "y", "power", "out", "value")
HY_DVE = numbered("bias_cols", "inv_temp", "slice_w", "slice_b", "snorm_eps", "snorm_inv", "tok_w", "snorm_n",
                  "tok_b0", "tok_b1", "tok0", "tok1", "dt_in", "dt_neg", "dt_nabs", "dt", "decay_rate", "decay_in",
                  "pad", "conv0", "conv1", "conv01", "conv2", "conv012", "conv_b", "weight_dt", "xbc", "x_twice",
                  "gram", "skip8", "weight", "z", "skip", "y", "yg", "sq", "rms", "yn", "ynw", "ot0", "ot1")
HY_ACT = numbered("rate", "dt_exp", "dt_ln", "decay_exp", "conv_sig", "z_sig", "x_rows", "rms_std", "value")


def reached(eng, sem, value):
    if isinstance(value, int) and value <= 0:
        return
    eng.wait_ge(sem, value)


def graph_block(nc: bass.Bass, a: dict, out: bass.AP):
    ctx = ExitStack()
    with ctx:
        def sb(name, shape, dt=F32):
            return ctx.enter_context(nc.sbuf_tensor(name, shape, dt))

        def sem(name):
            return ctx.enter_context(nc.semaphore(name))

        ps = ctx.enter_context(nc.psum_tensor("ps", [P, 8, CH], F32))

        ident = sb("ident", [P, P])
        noteye = sb("noteye", [P, P])
        eps_col = sb("eps_col", [P, 1])
        table_in = sb("table_in", [P, 8])
        xr = sb("xr", [P, NT, D])
        hrow = sb("hrow", [P, NT, D])
        hT = sb("hT", [P, N])
        nsT = sb("nsT", [P, N])
        hW = sb("hW", [P, NT, HEADS * D])
        eb = sb("eb", [P, NS, N])
        arow = sb("arow", [P, 2, N])
        nb = sb("nb", [P, N])
        mneg = sb("mneg", [P, N], U8)
        ring = sb("ring", [P, RING, N])
        pat = sb("pat", [P, 2, N])
        esT = hrow[:, :, :].rearrange("p t d -> p (t d)")

        def cutter(area, size):
            at = [0]

            def piece(n):
                at[0] += n
                assert at[0] <= size, at
                return area[:, at[0] - n:at[0]]
            return piece

        st6 = sb("st6", [P, NT * 6])[:, :].rearrange("p (t s) -> p t s", t=NT)
        mv = sb("mv", [P, NT * 2])[:, :].rearrange("p (t s) -> p t s", t=NT)
        std = sb("std", [P, NT])[:, :]
        rstd = sb("rstd", [P, NT])[:, :]
        gatWT = sb("gatWT", [P, HEADS * D])[:, :]
        gatA = sb("gatA", [P, NS])[:, :].rearrange("p (s h) -> p s h", s=2)
        wa = sb("wa", [P, NS])[:, :]
        WT = [sb(f"WT{k}", [P, 3 * D])[:, :] for k in range(4)]
        gb = sb("gb", [P, 12])[:, :].rearrange("p (k g) -> p k g", k=4)
        gbs = sb("gbs", [P, 6])[:, :].rearrange("p (k g) -> p k g", k=2)
        diag = sb("diag", [P, NT])[:, :]
        mn = sb("mn", [P, RING])[:, :]
        den = sb("den", [P, RING])[:, :]
        rden = sb("rden", [P, RING])[:, :]
        esb = sb("esb", [P, 2 * D])[:, :].rearrange("p (u d) -> p u d", u=2)

        aT = [ring[:, s, :] for s in range(3)]
        masks = pat[:, :, :].rearrange("p u n -> p (u n)").bitcast(BF16).rearrange(
            "p (u n) -> p u n", u=4)
        NEG_SLOT = [s for s in range(3) if s != (NT - 1) % 3]
        mres = ring[:, 3, :]
        n_neg = sb("n_neg", [P, NT])
        n_neg1 = sb("n_neg1", [P, 1])
        n_one = sb("n_one", [P, 1])
        any_neg = sb("any_neg", [1, 1], mybir.dt.int32)
        parts = ring[:, 4, 0:NT * 96].bitcast(BF16).rearrange(
            "p (v t q) -> p v t q", v=2, t=NT)
        sel = ring[:, 5, 0:NS * P].rearrange("p (q m) -> p q m", q=NS)
        piece5 = cutter(ring[:, 5, NS * P:N], N - NS * P)
        gatW = piece5(HEADS * D)
        uu = [piece5(NT * NS).rearrange("p (t q) -> p t q", t=NT) for _ in range(4)]
        gr, gz = ([pat[:, 1, (2 * u + k) * CH:(2 * u + k + 1) * CH] for u in range(2)] for k in range(2))
        gts = [[ring[:, slot, u * CH:(u + 1) * CH] for u in range(2)] for slot in (5, 2)]

        swT = eb[:, 0:CB, :]
        sw = [ring[:, t % 4, (t // 4) * CH:(t // 4 + 1) * CH] for t in range(8)]
        hWf = hW[:, :, :].rearrange("p t d -> p (t d)")
        cut_h = cutter(hWf, NT * HEADS * D)
        ZX = 2 * DI + 2 * G + 2 * SLOPES
        in_wT = cut_h(CB * ZX).rearrange("p (k n) -> p k n", k=CB)
        wx = cut_h(SLOPES * D).rearrange("p (h d) -> p h d", h=SLOPES)
        wsT = cut_h(G)
        outT = eb[:, 4, :].rearrange("p (k n) -> p k n", k=CB)
        cutf = cutter(eb[:, 5, :], N)
        fcDT = cutf(CB * SLOPES).rearrange("p (k h) -> p k h", k=CB)
        headsel = cutf(DI)[0:SLOPES, :].rearrange("p (m c) -> p m c", m=CB)
        d_head, skip8 = cutf(1)[0:SLOPES, :], cutf(G)[0:SLOPES, :]
        cut4 = cutter(ring[:, 4, :], N)
        wfxT, w_slice, b_slice = cut4(DI), cut4(DI), cut4(DI)
        outwT = cut4(CB * D).rearrange("p (m d) -> p m d", m=CB)
        cut5 = cutter(ring[:, 5, :], N)
        bx_cols = cut5(SLOPES * P).rearrange("p (h m) -> p h m", h=SLOPES)
        swsum = cut5(DI)
        b_rows = sb("b_rows", [P, DI], BF16)[:, :]
        ones16 = sb("ones16", [P, P], BF16)
        b_parts = pat[:, 0, 2 * DI:2 * DI + 3 * DI // 2].bitcast(BF16).rearrange("p (n m) -> p n m", n=3)
        b_rest = [pat[:, 0, k * DI:(k + 1) * DI] for k in range(2)]
        bsl, bx, temp = cut5(G), cut5(SLOPES), cut5(SLOPES)
        bfx, cw, cb = cut5(CB), cut5(6 * 3).rearrange("p (c k) -> p c k", c=6), cut5(6)
        dtb, alog, nwcol = cut5(SLOPES), cut5(SLOPES), cut5(CB)
        dt_s = [cut5(SLOPES) for _ in range(5)]
        rate = cut5(SLOPES)
        mx8 = [cut5(SLOPES) for _ in range(4)]
        rs8 = [cut5(SLOPES) for _ in range(4)]
        cutn = cutter(nb, N)
        outb = cutn(D)
        m_rs, m_rt, m_st = cutn(P), cutn(G), cutn(G)
        ones = cutn(P)
        tok_n, sn_n, rsn = cutn(DI), cutn(DI), cutn(DI)
        hy = [ring[:, k, 2 * CH:4 * CH] for k in range(4)]
        tokT = hy[0][:, 0:CB * G].rearrange("p (k g) -> p k g", k=CB)
        tokb = hy[0][:, CB * G:2 * CB * G].rearrange("p (k g) -> p k g", k=CB)
        PADW = G + 2
        xp = hy[0][:, 512:512 + 6 * PADW].rearrange("p (c l) -> p c l", c=6)
        xs = hy[1][:, 0:6 * PADW].rearrange("p (c l) -> p c l", c=6)
        cva = hy[1][:, 400:400 + 6 * G].rearrange("p (c l) -> p c l", c=6)
        cvt = hy[2][:, 0:6 * G].rearrange("p (c l) -> p c l", c=6)
        gramm = hy[2][:, 384:384 + G]
        x2 = hy[2][:, 512:1024]
        dec = hy[3][:, 0:512].rearrange("p (h t) -> p h t", h=SLOPES)
        xd = hy[3][:, 512:1024].rearrange("p (m v g) -> p m v g", m=CB, v=2)
        cutp = cutter(pat[:, 0, :], N)
        z1, y1, ysq = (cutp(CB * G).rearrange("p (k g) -> p k g", k=CB) for _ in range(3))
        bd = cutp(CB * P).rearrange("p (m r) -> p m r", m=CB)
        rms = cutp(G)
        val = pat[:, 1, 0:CB * D].rearrange("p (m d) -> p m d", m=CB)

        sbn = eb[:, 0, :]
        xrow = eb[:, 3, :].rearrange("p (t d) -> p t d", t=NT)
        hv_cols = nsT[:, 0:D]
        cute = cutter(nsT[:, D:N], N - D)
        wexp = [(cute(HID), cute(HC * D).rearrange("p (c d) -> p c d", c=HC)) for _ in range(2)]
        wr, hv, gamma, beta = cute(EXPERTS), cute(1), cute(1), cute(1)
        b1 = cute(EXPERTS * HC).rearrange("p (e c) -> p e c", e=EXPERTS)
        b2, br, prio = cute(D), cute(EXPERTS), cute(EXPERTS)
        hid = pat[:, :, 0:2 * CH].rearrange("p u (c n) -> p u c n", c=HC)
        cutr = cutter(nb, N)
        route, top, hot1, hot2, wfull = (cutr(NT * EXPERTS).rearrange("p (t e) -> p t e", t=NT) for _ in range(5))
        v1, v2, ky, ew, w1 = (cutr(NT) for _ in range(5))
        wT = eb[0:EXPERTS, 1, :]

        ld_x = [sem(f"ld_x{q}") for q in range(NC)]
        ld_c, ld_gat, ld_gru = sem("ld_c"), sem("ld_gat"), sem("ld_gru")
        aT_in = [sem(f"aT_in{s}") for s in range(3)]
        dve_seq, u_sb = sem("dve_seq"), sem("u_sb")
        out_stored = sem("out_stored")
        ln_bn, ln_stats, ln_std, ln_rstd, ln_row, ln_tp, ln_hT = (
            sem("ln_" + s) for s in ("bn", "stats", "std", "rstd", "row", "tp", "hT"))
        wa_mm, wa_sb, u_mm, parts_ok = sem("wa_mm"), sem("wa_sb"), sem("u_mm"), sem("parts_ok")
        hw_mm, hw_sb = sem("hw_mm"), sem("hw_sb")
        aT_diag, neg_mm, neg_ok = sem("aT_diag"), sem("neg_mm"), sem("neg_ok")
        neg_in = [sem(f"neg_in{u}") for u in range(3)]
        neg_diag, neg_masks, neg_used = sem("neg_diag"), sem("neg_masks"), sem("neg_used")
        minus_mm, minus_sb = sem("minus_mm"), sem("minus_sb")
        masks_ok, aT_used, masks_used, ns_sb, mres_sb = (
            sem(x) for x in ("masks_ok", "aT_used", "masks_used", "ns_sb", "mres_sb"))
        bc_mm, bc_sb, eb_ok = sem("bc_mm"), sem("bc_sb"), sem("eb_ok")
        gru_mm, gru_r, gru_z, gru_t, gru_n, gru_out = (
            sem("gru_" + s) for s in ("mm", "r", "z", "t", "n", "out"))
        gbs_ok, gru_sum = sem("gbs_ok"), sem("gru_sum")
        row_in = [sem("row_in0"), sem("row_in1")]
        row_free, picked, s_ready, z_ready, p_ready = (
            sem(s) for s in ("row_free", "picked", "s_ready", "z_ready", "p_ready"))
        prep = sem("prep")
        e_copied, tp_ready, tp_out, mm_done, es_acc = (
            sem(s) for s in ("e_copied", "tp_ready", "tp_out", "mm_done", "es_acc"))
        rd_ok = sem("rd_ok")
        es_tp, es_T = sem("es_tp"), sem("es_T")
        x1_tp, x1_ok = sem("x1_tp"), sem("x1_ok")
        ld_slice, ld_hy = sem("ld_slice"), sem("ld_hy")
        hy_pe, hy_dve, hy_act = sem("hy_pe"), sem("hy_dve"), sem("hy_act")
        lg_mm, lg_max, lg_sub, lg_exp, lg_sum, sw_ok, sw_sum, sw_tp, sw_T, x2_mm, x2_ok, outb_ok = (
            sem(x) for x in ("lg_mm", "lg_max", "lg_sub", "lg_exp", "lg_sum", "sw_ok", "sw_sum", "sw_tp", "sw_T",
                             "x2_mm", "x2_ok", "outb_ok"))
        ones_ok, lg_total, b_rows_ok, pool_seq = sem("ones_ok"), sem("lg_total"), sem("b_rows_ok"), sem("pool_seq")
        ld_moe, ld_exp = sem("ld_moe"), [sem("ld_exp0"), sem("ld_exp1")]
        hv_ok, sc_mm, sc_ok = sem("hv_ok"), sem("sc_mm"), sem("sc_ok")
        row2_in = [sem(f"row2_in{u}") for u in range(2)]
        g_prod, g_mask, g_min, g_score, g_exp, g_tp, g_out, g_mm, g_den, x3_ok = (
            sem("g_" + x) for x in ("prod", "mask", "min", "score", "exp", "tp", "out", "mm", "den", "x3_ok"))
        r_mm, r_dlt, r_exp, r_w, r_tp, r_wT, b2_mm, b2_ok = (
            sem(x) for x in ("r_mm", "r_dlt", "r_exp", "r_w", "r_tp", "r_wT", "b2_mm", "b2_ok"))
        up_mm, gelu_ok, down_mm, acc_ok = sem("up_mm"), sem("gelu_ok"), sem("down_mm"), sem("acc_ok")

        HY_LOADS = ((in_wT, "in_wT"), (wfxT, "wfxT"), (bfx, "bfx"), (cw, "cw"), (cb, "cb"), (dtb, "dtb"), (alog, "alog"),
                    (m_rs, "m_rs"), (m_rt, "m_rt"), (m_st, "m_st"), (outb, "outb"), (fcDT, "fcDT"), (headsel, "headsel"),
                    (d_head, "d_head"), (nwcol, "nwcol"), (outT, "outT"), (outwT, "outwT"))

        MOE_LOADS = ((wr, "Wr"), (hv, "hv"), (gamma, "gamma"), (beta, "beta"), (b1, "b1"), (b2[0:EXPERTS, :], "b2"),
                     (br, "br"), (prio, "prio"))

        loop_waits = sem("loop_waits")

        def waited(eng):
            eng.sem_inc(loop_waits, 1)

        block = ctx.enter_context(nc.Block())

        @block.sync
        def _(sp):
            for q in range(NC):
                sp.dma_start(xr[:, q * TC:(q + 1) * TC, :],
                             a["x"][q * CH:(q + 1) * CH, :].rearrange("(t p) d -> p t d", p=P)).then_inc(ld_x[q], 16)
                if q == 0:
                    sp.dma_start(ident[:, :], a["ident"]).then_inc(ld_c, 16)
                    sp.dma_start(noteye[:, :], a["noteye"]).then_inc(ld_c, 16)
                if q == 1:
                    sp.dma_start(aT[0], a["adjT"][0:P, :]).then_inc(aT_in[0], 16)
                if q == 2:
                    sp.dma_start(gatWT, a["gat_WT"]).then_inc(ld_gat, 16)
                    sp.dma_start(gatA, a["gat_a"]).then_inc(ld_gat, 16)
            sp.dma_start(aT[1], a["adjT"][P:2 * P, :]).then_inc(aT_in[1], 16)
            sp.dma_start(gatW, a["gat_W"]).then_inc(ld_gat, 16)
            sp.dma_start(sel[0:96, :, :], a["sel"]).then_inc(ld_gat, 16)
            for j in range(NT):
                if j >= 3:
                    sp.wait_ge(aT_used, j - 2)
                    sp.wait_ge(masks_ok, j - 2)
                if j >= 2:
                    sp.dma_start(aT[j % 3], a["adjT"][j * P:(j + 1) * P, :]).then_inc(aT_in[j % 3], 16)
                if j == 2:
                    for k in range(4):
                        sp.dma_start(WT[k], a["gru_WT"][k]).then_inc(ld_gru, 16)
                    sp.dma_start(gb, a["gru_b"]).then_inc(ld_gru, 16)
                    sp.dma_start(diag, a["diag"]).then_inc(ld_gru, 16)

            def rows(t, u, i):
                reached(sp, p_ready, 3 * (t - 1))
                sp.dma_start(arow[:, u, :], a["adj_t"][t, :, :] if isinstance(t, int) else
                             a["adj_t"][bass.ds(t, 1), :, :].rearrange("a p n -> (a p) n")).then_inc(row_in[u], 16)
            rows(0, 0, 0)
            rows(1, 1, 0)
            sp.wait_ge(neg_ok, 2)
            negative = sp.value_load(any_neg[0:1, 0:1], min_val=0, max_val=N * N)
            with sp.If(negative > 0):
                for j in range(NT):
                    if j == 0:
                        sp.wait_ge(aT_used, NT)
                        sp.wait_ge(masks_ok, NT)
                    if j >= 3:
                        sp.wait_ge(neg_masks, j - 2)
                    sp.dma_start(aT[j % 3], a["adjT"][j * P:(j + 1) * P, :]).then_inc(neg_in[j % 3], 16)
            with sp.Fori(1, NT // 2) as i:
                for u in range(2):
                    rows(2 * i + u, u, i)

            sp.wait_ge(es_T, NT)
            for to, name in ((wx[0:64, :, :], "wx"), (wsT[0:64, :], "wsT"), (bx[0:64, :], "bx"), (bsl, "b_slice"),
                             (temp, "temp")):
                sp.dma_start(to, a[name]).then_inc(ld_slice, 16)
            for to, name in HY_LOADS:
                sp.dma_start(to, a[name]).then_inc(ld_hy, 16)

            def rows2(t, u, i):
                reached(sp, g_prod, t - 1)
                reached(sp, g_mask, t - 1)
                sp.dma_start(arow[:, u, :], a["adj_t"][t, :, :] if isinstance(t, int) else
                             a["adj_t"][bass.ds(t, 1), :, :].rearrange("a p n -> (a p) n")).then_inc(row2_in[u], 16)
            rows2(0, 0, 0)
            rows2(1, 1, 0)
            sp.wait_ge(x1_tp, NC)
            for to, name in MOE_LOADS:
                sp.dma_start(to, a[name]).then_inc(ld_moe, 16)

            def expert(e, u):
                reached(sp, down_mm, 4 * (e - 1))
                for to, name in ((wexp[u][0], "W1"), (wexp[u][1], "W2")):
                    src = a[name][e] if isinstance(e, int) else a[name][bass.ds(e, 1)].rearrange(
                        "a p n -> (a p) n" if name == "W1" else "a p c n -> (a p) c n")
                    sp.dma_start(to, src).then_inc(ld_exp[u], 16)
            expert(0, 0)
            expert(1, 1)
            with sp.Fori(1, NT // 2) as i:
                for u in range(2):
                    rows2(2 * i + u, u, i)
            with sp.Fori(1, EXPERTS // 2) as i:
                for u in range(2):
                    expert(2 * i + u, u)
            for q in range(NC):
                sp.wait_ge(acc_ok, NC * (EXPERTS - 1) + q + 1)
                sp.dma_start(out[q * CH:(q + 1) * CH, :].rearrange("(t p) d -> p t d", p=P),
                             xr[:, q * TC:(q + 1) * TC, :]).then_inc(out_stored, 16)
            sp.wait_ge(out_stored, 16 * NC)

        @block.scalar
        def _(act):
            preloads = [0]

            def preload(function):
                k = preloads[0]
                preloads[0] += 1
                act.activation(table_in[:, k:k + 1], eps_col[:, 0:1], function)

            def norm_std(n, q):
                cols = slice(q * TC, (q + 1) * TC)
                act.wait_ge(ln_stats, n * NC + q + 1)
                act.activation(std[:, cols], mv[:, cols, 1], ACT.Sqrt, bias=eps_col[:, 0:1]).then_inc(ln_std, 1)

            def norm_out(n, q, bank):
                act.wait_ge(ln_tp, n * NC + q + 1)
                scaled = {"scale": gamma, "bias": beta} if n == 3 else {}
                act.activation(hT[:, q * CH:(q + 1) * CH], ps[:, bank, :], ACT.Identity if n == 3 else ACT.Copy,
                               **scaled).then_inc(ln_hT, 1)

            for q in range(NC):
                norm_std(0, q)
                if q < 2:
                    norm_out(0, q, 4 + q)
            norm_out(0, 2, 6)
            norm_out(0, 3, 7)

            def hw_out(j):
                act.wait_ge(hw_mm, j + 1)
                act.activation(hW[:, j, :], ps[:, 1 + j % 3, 0:HEADS * D], ACT.Copy).then_inc(hw_sb, 1)

            act.wait_ge(aT_used, NT)
            for g in range(NC):
                act.activation(nsT[:, g * CH:(g + 1) * CH], ps[:, g, :], ACT.Copy).then_inc(ns_sb, 1)
            for j in range(NT // 2):
                hw_out(j)
            act.wait_ge(masks_used, NT)
            for g in range(NC):
                act.activation(mres[0:96, g * CH:(g + 1) * CH], ps[0:96, 4 + g, :], ACT.Copy).then_inc(mres_sb, 1)
            for j in range(NT // 2, NT):
                hw_out(j)

            def broadcast_out(q, g, mm, out_sb, n):
                act.wait_ge(mm, n + 1)
                act.activation(eb[:, q, g * CH:(g + 1) * CH], ps[:, g, :], ACT.Copy, scale=-1.0).then_inc(out_sb, 1)

            for n in range(HEADS * NC):
                broadcast_out(n // NC, n % NC, bc_mm, bc_sb, n)
            act.wait_ge(neg_ok, 2)
            negative = act.value_load(any_neg[0:1, 0:1], min_val=0, max_val=N * N)
            with act.If(negative > 0):
                for n in range(HEADS * NC):
                    broadcast_out(HEADS + n // NC, n % NC, minus_mm, minus_sb, n)

            def exps(i, kk):
                kk, i = (kk, i) if kk < 6 else (kk - 6, i + 1)
                k, s = 6 * i + kk, kk % RING
                reached(act, rd_ok, k - 5)
                act.wait_ge(s_ready, k + 1)
                act.activation(ring[:, s, :], ring[:, s, :], ACT.Exp, bias=mn[:, s:s + 1], scale=-1.0,
                               accum_out=den[:, s:s + 1]).then_inc(z_ready, 1)

            def gru(n):
                act.wait_ge(gbs_ok, 1)
                gt = gts[n]
                for q in range(NC):
                    u, c = q % 2, n * NC + q
                    b = GRU_BANK(q)
                    act.wait_ge(gru_mm, 4 * c + 1)
                    if q >= 2:
                        act.wait_ge(gru_out, c - 1)
                    act.activation(gr[u], ps[:, b, :], ACT.Sigmoid, bias=gbs[:, n, 0:1]).then_inc(gru_r, 1)
                    act.wait_ge(gru_mm, 4 * c + 2)
                    act.activation(gz[u], ps[:, b + 1, :], ACT.Sigmoid, bias=gbs[:, n, 1:2]).then_inc(gru_z, 1)
                    act.wait_ge(gru_t, c + 1)
                    act.activation(gt[u], gt[u], ACT.Tanh, bias=gb[:, 2 * n, 2:3]).then_inc(gru_n, 1)
                    if n == 0 and q == 1:
                        exps(0, 1)
                        exps(0, 2)

            exps(0, 0)
            gru(0)

            def evac(i, kk, first=False):
                k = 6 * i + kk
                for b in range(4):
                    if b == 0:
                        reached(act, mm_done, k - 1)
                    if first and kk == 1 and b == 0:
                        act.wait_ge(gru_out, NC)
                    act.wait_ge(tp_ready, 4 * k + b + 1)
                    act.activation(pat[:, kk % 2, b * CH:(b + 1) * CH], ps[:, b, :], ACT.Copy).then_inc(tp_out, 1)

            def es_out(t, u):
                act.wait_ge(es_tp, t + 1)
                waited(act)
                act.activation(esT[:, bass.ds(t * P, P)], ps[:, 6 + u, 0:P], ACT.Copy,
                               scale=1.0 / HEADS).then_inc(es_T, 1)

            def steps(i, first=False, last=False):
                for kk in range(6):
                    if kk % 3 == 0 and not first:
                        es_out(2 * i + kk // 3 - 2, kk // 3)
                    evac(i, kk, first)
                    if not (last and kk + 3 >= 6):
                        exps(i, kk + 3)

            steps(0, first=True)
            with act.Fori(1, NT // 2 - 1) as i:
                steps(i)
            steps(NT // 2 - 1, last=True)
            es_out(NT - 2, 0)
            es_out(NT - 1, 1)
            gru(1)

            for q in range(NC):
                norm_std(1, q)
            for q in range(NC):
                norm_out(1, q, (2, 3, 6, 7)[q])
                if q == 1:
                    act.wait_ge(pool_seq, 6)
                    for n in range(3):
                        act.activation(b_rows[32 * n:32 * n + 1, :], b_parts[32 * n:32 * n + 1, n, :],
                                       ACT.Copy).then_inc(b_rows_ok, 1)

            def sw_out(t):
                act.wait_ge(sw_tp, t + 1)
                act.activation(swT[:, :, t * P:(t + 1) * P], ps[:, t % 2, :].rearrange("p (m n) -> p m n", m=CB),
                               ACT.Copy).then_inc(sw_T, 1)

            for t in range(NT):
                act.wait_ge(lg_sub, t + 1)
                act.activation(sw[t % 8], sw[t % 8], ACT.Exp).then_inc(lg_exp, 1)
                if t >= 3:
                    sw_out(t - 3)
            for t in range(NT - 3, NT):
                sw_out(t)

            def hyd(name, ins):
                ins.then_inc(hy_act, 1)
                act.wait_ge(hy_act, HY_ACT[name])

            act.wait_ge(ld_hy, 16 * len(HY_LOADS))
            hyd("rate", act.activation(rate, alog, ACT.Exp))
            act.wait_ge(hy_dve, HY_DVE["dt_nabs"])
            hyd("dt_exp", act.activation(dt_s[2], dt_s[1], ACT.Exp))
            hyd("dt_ln", act.activation(dt_s[3], dt_s[2], ACT.Ln, bias=1.0))
            preload(ACT.Exp)
            act.wait_ge(hy_pe, HY_PE["decay"])
            hyd("decay_exp", act.activation(dec, ps[:, 5, :].rearrange("p (h t) -> p h t", h=SLOPES), ACT.Exp))
            preload(ACT.Sigmoid)
            act.wait_ge(hy_dve, HY_DVE["conv_b"])
            hyd("conv_sig", act.activation(cvt, cva, ACT.Sigmoid))
            act.wait_ge(hy_pe, HY_PE["z"])
            hyd("z_sig", act.activation(z1, ps[:, 0, 0:CB * G].rearrange("p (k g) -> p k g", k=CB), ACT.Sigmoid))
            act.wait_ge(hy_pe, HY_PE["x_rows"])
            hyd("x_rows", act.activation(x2, ps[:, 4, :], ACT.Copy))
            preload(ACT.Sqrt)
            act.wait_ge(hy_pe, HY_PE["power"])
            hyd("rms_std", act.activation(rms, ps[:, 2, 0:G], ACT.Sqrt, scale=1.0 / DI, bias=eps_col[:, 0:1]))
            act.wait_ge(hy_pe, HY_PE["value"])
            hyd("value", act.activation(val, ps[:, 4, :].rearrange("p (m d) -> p m d", m=CB), ACT.Copy))

            def scores_out(g):
                act.wait_ge(sc_mm, g + 1)
                act.activation(sbn[:, g * CH:(g + 1) * CH], ps[:, g, :], ACT.Copy, scale=-1.0).then_inc(sc_ok, 1)

            for q in range(NC):
                norm_std(2, q)
                if q == NC - 1:
                    scores_out(NC - 2)
                norm_out(2, q, 4 + q)
                if 1 <= q < NC - 1:
                    scores_out(q - 1)
            scores_out(NC - 1)

            def g_exps(i, kk):
                k = 4 * i + kk
                act.wait_ge(g_score, k + 1)
                reached(act, g_den, 2 * k - 7)
                act.activation(ring[:, kk % 4, :], ring[:, kk % 4, :], ACT.Exp, bias=mn[:, kk % 4:kk % 4 + 1], scale=-1.0,
                               accum_out=den[:, kk % 4:kk % 4 + 1]).then_inc(g_exp, 1)

            def g_evac(i, kk):
                k = 4 * i + kk
                for b in range(4):
                    if b == 0:
                        reached(act, g_mm, k - 1)
                    act.wait_ge(g_tp, 4 * k + b + 1)
                    act.activation(pat[:, kk % 2, b * CH:(b + 1) * CH], ps[:, b, :], ACT.Copy).then_inc(g_out, 1)

            def g_steps(i, last=False):
                for kk in range(4):
                    g_evac(i, kk)
                    if not (last and kk + 2 >= 4):
                        g_exps(i, kk + 2)
                    if last and kk == 1:
                        for q in range(NC - 1):
                            norm_std(3, q)

            g_exps(0, 0)
            g_exps(0, 1)
            g_steps(0)
            with act.Fori(1, NT // 4 - 1) as i:
                g_steps(i)
            g_steps(NT // 4 - 1, last=True)

            act.wait_ge(ld_moe, 16 * len(MOE_LOADS))
            for q in range(NC - 1):
                norm_out(3, q, 6 + q % 2)
            norm_std(3, NC - 1)
            preload(ACT.Gelu)
            norm_out(3, NC - 1, 6 + (NC - 1) % 2)

            def gelu(i, v, q, first=False):
                st = 8 * i + 4 * v + q
                if not (first and st < 2):
                    act.wait_ge(down_mm, st - 1)
                for c in range(HC):
                    act.wait_ge(up_mm, HC * st + c + 1)
                    waited(act)
                    act.activation(hid[:, q % 2, c, :], ps[:, 2 * (q % 2) + c, :], ACT.Gelu,
                                   bias=b1[:, 2 * i + v, c:c + 1] if isinstance(i, int) else
                                   b1[:, bass.ds(2 * i + v, 1), c]).then_inc(gelu_ok, 1)

            def gelus(i, v):
                for q in range(NC):
                    gelu(i, v, q)

            def router_T(g):
                act.wait_ge(r_tp, g + 1)
                act.activation(wT[:, g * CH:(g + 1) * CH], ps[0:EXPERTS, 6 + g % 2, :], ACT.Copy).then_inc(r_wT, 1)

            gelu(0, 0, 0, first=True)
            gelu(0, 0, 1, first=True)
            preload(ACT.Exp)
            act.wait_ge(r_dlt, 1)
            act.activation(ew, v2, ACT.Exp).then_inc(r_exp, 1)
            gelu(0, 0, 2)
            gelu(0, 0, 3)
            router_T(0)
            router_T(1)
            gelus(0, 1)
            router_T(2)
            router_T(3)
            gelus(1, 0)
            gelus(1, 1)
            with act.Fori(2, EXPERTS // 2) as i:
                gelus(i, 0)
                gelus(i, 1)

        @block.vector
        def _(dve):
            count = [0]

            def link(ins):
                count[0] += 1
                ins.then_inc(dve_seq, 1)
                dve.wait_ge(dve_seq, count[0])

            def stats(t):
                dve.bn_stats(st6[:, t, :], xr[:, t, :]).then_inc(ln_bn, 1)

            def aggregate(n, ts):
                dve.wait_ge(ln_bn, n * NT + ts[-1] + 1)
                for t in ts:
                    ins = dve.bn_aggr(mv[:, t, :], st6[:, t, :])
                ins.then_inc(ln_stats, 1)

            def finish(n, q):
                cols = slice(q * TC, (q + 1) * TC)
                dve.wait_ge(ln_std, n * NC + q + 1)
                dve.reciprocal(rstd[:, cols], std[:, cols]).then_inc(ln_rstd, 1)
                dve.wait_ge(ln_rstd, n * NC + q + 1)
                for t in range(q * TC, (q + 1) * TC):
                    dve.tensor_scalar((hrow if n < 3 else xrow)[:, t, :], xr[:, t, :], mv[:, t, 0:1], rstd[:, t:t + 1],
                                      ALU.subtract, ALU.mult).then_inc(ln_row, 1)

            def chunk(q):
                return range(q * TC, (q + 1) * TC)

            def without_diagonal(j):
                dve.wait_ge(aT_in[j % 3], 16 * (j // 3 + 1))
                blk = aT[j % 3][:, j * P:(j + 1) * P]
                dve.tensor_tensor(blk, blk, noteye[:, :], ALU.mult).then_inc(aT_diag, 1)

            dve.memset(eps_col[:, :], EPS)
            link(dve.memset(parts, 0.0))
            for q in range(NC + 1):
                if q < NC:
                    dve.wait_ge(ld_x[q], 16)
                    for t in chunk(q):
                        stats(t)
                    aggregate(0, chunk(q))
                if q >= 1:
                    finish(0, q - 1)
                if q == 2:
                    dve.wait_ge(ld_c, 32)
                    without_diagonal(0)
            dve.memset(n_one[:, :], 1.0)
            dve.memset(ones16[:, :], 1.0)
            link(dve.memset(b_rows, 0.0))
            dve.wait_ge(wa_mm, 1)
            dve.tensor_copy(wa, ps[:, 4, 0:NS]).then_inc(wa_sb, 1)
            swap = (slice(HEADS, NS), slice(0, HEADS))

            def part(c, src):
                dve.tensor_copy(parts[:, 0, :, 32 * c:32 * c + NS], src)
                dve.tensor_copy(parts[:, 1, :, 32 * c:32 * c + HEADS], src[:, :, swap[0]])
                return dve.tensor_copy(parts[:, 1, :, 32 * c + HEADS:32 * c + NS], src[:, :, swap[1]])

            def split():
                dve.wait_ge(u_mm, 1)
                dve.tensor_copy(uu[0], ps[:, 5, 0:NT * NS].rearrange("p (t q) -> p t q", t=NT)).then_inc(u_sb, 1)
                dve.wait_ge(u_sb, 1)
                link(part(0, uu[0]))
                link(dve.tensor_tensor(uu[1], uu[0], parts[:, 0, :, 0:NS], ALU.subtract))
                link(part(1, uu[1]))
                link(dve.tensor_tensor(uu[2], uu[1], parts[:, 0, :, 32:32 + NS], ALU.subtract))
                part(2, uu[2]).then_inc(parts_ok, 1)

            def masks_of(j):
                if j >= 3:
                    dve.wait_ge(masks_used, j - 2)
                dve.tensor_scalar(masks[:, j % 3, :], aT[j % 3], 0.0, None, ALU.is_gt)
                if j >= 1:
                    dve.wait_ge(masks_ok, j)
                dve.tensor_scalar(masks[:, 3, :], aT[j % 3], 0.0, 0.0, ALU.is_lt, ALU.add,
                                  accum_out=n_neg[:, j:j + 1]).then_inc(masks_ok, 1)

            without_diagonal(1)
            for j in range(NT):
                dve.wait_ge(aT_diag, j + 1)
                masks_of(j)
                if j == 0:
                    without_diagonal(2)
                    split()
                elif j + 2 < NT:
                    without_diagonal(j + 2)
            dve.wait_ge(masks_ok, NT)
            dve.tensor_reduce(n_neg1[:, :], n_neg[:, :], AX.X, ALU.add).then_inc(neg_ok, 1)
            dve.wait_ge(neg_mm, 1)
            dve.tensor_copy(any_neg[:, :], ps[0:1, 0, 0:1]).then_inc(neg_ok, 1)
            dve.wait_ge(neg_ok, 2)
            negative = dve.value_load(any_neg[0:1, 0:1], min_val=0, max_val=N * N)
            with dve.If(negative > 0):
                for j in range(NT):
                    dve.wait_ge(neg_in[j % 3], 16 * (j // 3 + 1))
                    blk = aT[j % 3][:, j * P:(j + 1) * P]
                    dve.tensor_tensor(blk, blk, noteye[:, :], ALU.mult).then_inc(neg_diag, 1)
                    dve.wait_ge(neg_diag, j + 1)
                    if j < 2:
                        dve.wait_ge(masks_used, NT - 1)
                    else:
                        dve.wait_ge(neg_used, j - 1)
                    dve.tensor_scalar(masks[:, NEG_SLOT[j % 2], :], aT[j % 3], 0.0, None, ALU.is_lt).then_inc(neg_masks, 1)

            def leaky(q):
                if q < HEADS:
                    dve.wait_ge(bc_sb, NC * (q + 1))
                else:
                    dve.wait_ge(minus_sb, NC * (q - HEADS + 1))
                dve.scalar_tensor_tensor(eb[:, q, :], eb[:, q, :], GAT_ALPHA, eb[:, q, :],
                                         ALU.mult, ALU.min).then_inc(eb_ok, 1)

            dve.wait_ge(ld_gru, 96)
            dve.tensor_tensor(gbs, gb[:, 0:4:2, :], gb[:, 1:4:2, :], ALU.add).then_inc(gbs_ok, 1)

            def gru_start(n, q):
                gt, u, c, b = gts[n], q % 2, n * NC + q, GRU_BANK(q)
                dve.wait_ge(gru_r, c + 1)
                dve.wait_ge(gru_mm, 4 * c + 3)
                link(dve.scalar_tensor_tensor(gt[u], ps[:, b + 2, :], gb[:, 2 * n + 1, 2:3], gr[u],
                                              ALU.add, ALU.mult))
                dve.wait_ge(gru_mm, 4 * c + 4)
                dve.tensor_tensor(gt[u], gt[u], ps[:, b + 3, :], ALU.add).then_inc(gru_t, 1)

            def gru_end(n, q):
                gt, u, c = gts[n], q % 2, n * NC + q
                cols = slice(q * CH, (q + 1) * CH)
                dve.wait_ge(gru_n, c + 1)
                dve.wait_ge(gru_z, c + 1)
                link(dve.tensor_tensor(gr[u], hT[:, cols], gt[u], ALU.subtract))
                link(dve.tensor_tensor(gr[u], gr[u], gz[u], ALU.mult))
                if n == 0:
                    dve.tensor_tensor(nsT[:, cols], gr[u], gt[u], ALU.add).then_inc(gru_out, 1)
                else:
                    dve.wait_ge(gru_sum, q + 1)
                    dve.tensor_tensor(nsT[:, cols], nsT[:, cols], gr[u], ALU.add).then_inc(gru_out, 1)

            def tile_prep(i, u, negatives):
                t = 2 * i + u
                dve.wait_ge(row_in[u], 16 * (i + 1))
                blk = arow[:, u, bass.ds(t * P, P)]
                dve.tensor_tensor(blk, blk, noteye[:, :], ALU.mult).then_inc(row_free, 1)
                dve.wait_ge(row_free, t + 1)
                if negatives:
                    dve.tensor_scalar(mneg[:, :], arow[:, u, :], 0.0, None, ALU.is_lt)
                dve.tensor_scalar(nb[:, :], arow[:, u, :], 0.0, NEG, ALU.is_equal, ALU.mult).then_inc(prep, 1)
                dve.wait_ge(prep, t + 1)

            def score(i, kk, negatives):
                h, s, k = kk % 3, kk % RING, 6 * i + kk
                reached(dve, tp_ready, 4 * (k - 5))
                if negatives:
                    dve.tensor_copy(ring[:, s, :], eb[:, h, :]).then_inc(e_copied, 1)
                    dve.wait_ge(e_copied, k + 1)
                    waited(dve)
                    dve.copy_predicated(ring[:, s, :], mneg[:, :], eb[:, HEADS + h, :]).then_inc(picked, 1)
                    dve.wait_ge(picked, k + 1)
                waited(dve)
                dve.tensor_tensor_reduce(ring[:, s, :], ring[:, s, :] if negatives else eb[:, h, :], nb[:, :], 1.0, FAR,
                                         ALU.add, ALU.min, mn[:, s:s + 1]).then_inc(s_ready, 1)

            def combine(i, kk):
                kk, i = (kk, i) if kk >= 0 else (kk + 6, i - 1)
                h, s, k, u = kk % 3, kk % RING, 6 * i + kk, kk // 3
                dve.wait_ge(z_ready, k + 1)
                dve.reciprocal(rden[:, s:s + 1], den[:, s:s + 1]).then_inc(rd_ok, 1)
                dve.wait_ge(rd_ok, k + 1)
                dve.wait_ge(mm_done, k + 1)
                o = ps[:, 4 + kk % 2, 0:D]
                if h == 0:
                    reached(dve, es_tp, 2 * i + u - 1)
                    dve.tensor_scalar(esb[:, u, :], o, rden[:, s:s + 1], None, ALU.mult).then_inc(es_acc, 1)
                else:
                    dve.wait_ge(es_acc, k)
                    dve.scalar_tensor_tensor(esb[:, u, :], o, rden[:, s:s + 1], esb[:, u, :],
                                             ALU.mult, ALU.add).then_inc(es_acc, 1)

            def steps(i, negatives, first=False):
                for kk in range(6):
                    if not (first and kk < 5):
                        if kk % 3 == 0:
                            tile_prep(i, kk // 3, negatives)
                        score(i, kk, negatives)
                    if not (first and kk < 4):
                        combine(i, kk - 4)

            def attention(negatives):
                for kk in range(3):
                    if not negatives:
                        leaky(kk)
                        dve.wait_ge(eb_ok, kk + 1)
                    if kk == 0:
                        tile_prep(0, 0, negatives)
                    if kk < 2:
                        score(0, kk, negatives)
                for q in range(NC + 1):
                    if q < NC:
                        gru_start(0, q)
                    if q >= 1:
                        gru_end(0, q - 1)
                    if q == 0:
                        score(0, 2, negatives)
                    if q == 1:
                        dve.wait_ge(bc_sb, HEADS * NC)
                        tile_prep(0, 1, negatives)
                        score(0, 3, negatives)
                    if q == 3:
                        score(0, 4, negatives)
                dve.wait_ge(gru_out, NC)
                steps(0, negatives, first=True)
                with dve.Fori(1, NT // 2) as i:
                    steps(i, negatives)
                for kk in range(2, 6):
                    combine(NT // 2 - 1, kk)

            before = count[0]
            with dve.If(negative > 0):
                for q in range(NS):
                    leaky(q)
                dve.wait_ge(eb_ok, NS)
                attention(True)
            count[0] = before
            with dve.Else():
                attention(False)
            def hyd(name, ins):
                ins.then_inc(hy_dve, 1)
                dve.wait_ge(hy_dve, HY_DVE[name])

            def first_residual(q):
                dve.wait_ge(x1_tp, q + 1)
                for t in chunk(q):
                    dve.scalar_tensor_tensor(xr[:, t, :], ps[:, GRU_BANK(q) + 3, (t % TC) * P:(t % TC + 1) * P],
                                             diag[:, t:t + 1], xr[:, t, :], ALU.mult, ALU.add).then_inc(x1_ok, 1)
                dve.wait_ge(x1_ok, (q + 1) * TC)
                for t in chunk(q):
                    stats(t)
                aggregate(1, chunk(q))

            by_head = lambda v: v.rearrange("p (h g) -> p h g", h=SLOPES)
            spread = lambda v: v.unsqueeze(2).broadcast_to([P, SLOPES, G])
            for q in range(NC):
                if q >= 1:
                    gru_end(1, q - 1)
                gru_start(1, q)
                if q == 0:
                    dve.wait_ge(ld_slice, 80)
                    hyd("bias_cols", dve.tensor_copy(bx_cols[0:64, :, :],
                                                     bx[0:64, :].unsqueeze(2).broadcast_to([64, SLOPES, P])))
                    hyd("inv_temp", dve.tensor_scalar(temp, temp, 1e-6, None, ALU.max))
                    link(dve.reciprocal(temp, temp))
                elif q < NC - 1:
                    first_residual(q - 1)

            dve.wait_ge(hy_pe, HY_PE["slice_w"])
            dve.tensor_tensor(by_head(w_slice), by_head(ps[:, 0, :]), spread(temp), ALU.mult).then_inc(hy_dve, 1)
            dve.wait_ge(hy_pe, HY_PE["slice_b"])
            dve.tensor_tensor(by_head(b_slice), by_head(ps[:, 1, :]),
                              bsl.unsqueeze(1).broadcast_to([P, SLOPES, G]), ALU.add).then_inc(hy_dve, 1)
            gru_end(1, NC - 1)
            first_residual(NC - 2)
            first_residual(NC - 1)
            finish(1, 0)
            for q in range(1, NC):
                finish(1, q)
            dve.memset(ones, 1.0).then_inc(ones_ok, 1)

            for t in range(NT + 2):
                if t < NT:
                    dve.wait_ge(lg_mm, t + 1)
                    lg = by_head(ps[:, LOGIT_BANKS[t % 3], :])
                    dve.tensor_reduce(mx8[t % 4], lg, AX.X, ALU.max).then_inc(lg_max, 1)
                if t >= 2:
                    dve.wait_ge(lg_exp, t - 1)
                    dve.tensor_reduce(rs8[(t - 2) % 4], by_head(sw[(t - 2) % 8]), AX.X, ALU.add).then_inc(lg_total, 1)
                if t < NT:
                    if t >= 8:
                        dve.wait_ge(sw_tp, t - 7)
                        dve.wait_ge(sw_sum, t - 7)
                    dve.wait_ge(lg_max, t + 1)
                    dve.tensor_tensor(by_head(sw[t % 8]), lg, spread(mx8[t % 4]), ALU.subtract).then_inc(lg_sub, 1)
                if t >= 2:
                    dve.wait_ge(lg_total, t - 1)
                    dve.reciprocal(rs8[(t - 2) % 4], rs8[(t - 2) % 4]).then_inc(lg_sum, 1)

            dve.wait_ge(ld_hy, 16 * len(HY_LOADS))
            link(dve.memset(xp, 0.0))
            link(dve.memset(xs, 0.0))
            link(dve.memset(bd, 0.0))
            dve.wait_ge(hy_pe, HY_PE["snorm"])
            snorm = ps[:, 7, :]
            hyd("snorm_eps", dve.tensor_scalar(rsn, snorm, 1e-5, None, ALU.add))
            hyd("snorm_inv", dve.reciprocal(rsn, rsn))
            hyd("tok_w", dve.tensor_tensor(tok_n, ps[:, 6, :], rsn, ALU.mult))
            hyd("snorm_n", dve.tensor_tensor(sn_n, snorm, rsn, ALU.mult))
            halves = ((slice(0, 64), slice(0, 64)), (slice(64, 128), slice(64, 128)))
            snv = sn_n.rearrange("p (m g) -> p m g", m=CB)
            for n, (r, g) in enumerate(halves):
                hyd(f"tok_b{n}", dve.tensor_tensor(tokb[r, :, :], snv[r, :, g], bfx[r, :].unsqueeze(2).broadcast_to([64, CB, G]),
                                                   ALU.mult))
            dve.wait_ge(hy_pe, HY_PE["tokens"])
            tps = ps[:, 0, :].rearrange("p (m g) -> p m g", m=CB)
            for n, (r, g) in enumerate(halves):
                hyd(f"tok{n}", dve.tensor_tensor(tokT[r, :, :], tps[r, :, g], tokb[r, :, :], ALU.add))
            dve.wait_ge(hy_pe, HY_PE["bcdt"])
            hyd("dt_in", dve.tensor_tensor(dt_s[0], ps[:, 3, 0:SLOPES], dtb, ALU.add))
            hyd("dt_neg", dve.tensor_scalar(dt_s[1], dt_s[0], -1.0, None, ALU.mult))
            hyd("dt_nabs", dve.tensor_tensor(dt_s[1], dt_s[1], dt_s[0], ALU.min))
            link(dve.tensor_copy(xp[0:64, CB:6, 2:PADW], ps[0:64, 2, 0:2 * G].rearrange("p (k g) -> p k g", k=2)))
            dve.wait_ge(hy_act, HY_ACT["dt_ln"])
            hyd("dt", dve.scalar_tensor_tensor(dt_s[4], dt_s[0], 0.0, dt_s[3], ALU.max, ALU.add))
            hyd("decay_rate", dve.scalar_tensor_tensor(dt_s[0], dt_s[4], -1.0, rate, ALU.mult, ALU.mult))
            hyd("decay_in", dve.tensor_tensor(dec, spread(dt_s[0]), m_rt.unsqueeze(1).broadcast_to([P, SLOPES, G]), ALU.mult))
            dve.wait_ge(hy_pe, HY_PE["x"])
            hyd("pad", dve.tensor_copy(xp[:, 0:CB, 2:PADW], ps[:, 1, 0:CB * G].rearrange("p (k g) -> p k g", k=CB)))
            tap = lambda k: cw[:, :, k].unsqueeze(2).broadcast_to([P, 6, G])
            hyd("conv0", dve.tensor_tensor(cva, xp[:, :, 0:G], tap(0), ALU.mult))
            hyd("conv1", dve.tensor_tensor(cvt, xp[:, :, 1:G + 1], tap(1), ALU.mult))
            hyd("conv01", dve.tensor_tensor(cva, cva, cvt, ALU.add))
            hyd("conv2", dve.tensor_tensor(cvt, xp[:, :, 2:G + 2], tap(2), ALU.mult))
            hyd("conv012", dve.tensor_tensor(cva, cva, cvt, ALU.add))
            hyd("conv_b", dve.tensor_tensor(cva, cva, cb.unsqueeze(2).broadcast_to([P, 6, G]), ALU.add))
            dve.wait_ge(hy_act, HY_ACT["decay_exp"])
            hyd("weight_dt", dve.tensor_tensor(dec, dec, spread(dt_s[4]), ALU.mult))
            dve.wait_ge(hy_act, HY_ACT["conv_sig"])
            hyd("xbc", dve.tensor_tensor(xs[:, :, 1:G + 1], cva, cvt, ALU.mult))
            hyd("x_twice", dve.tensor_copy(xd, xs[:, 0:CB, 1:G + 1].unsqueeze(2).broadcast_to([P, CB, 2, G])))
            dve.wait_ge(hy_pe, HY_PE["gram"])
            hyd("gram", dve.tensor_tensor(gramm, ps[:, 3, G:2 * G], m_st, ALU.mult))
            dve.wait_ge(hy_pe, HY_PE["skip8"])
            hyd("skip8", dve.tensor_scalar(skip8, ps[0:SLOPES, 7, CB * G:(CB + 1) * G], d_head, None, ALU.add))
            hyd("weight", dve.tensor_tensor(dec, dec, gramm.unsqueeze(1).broadcast_to([P, SLOPES, G]), ALU.mult))
            dve.wait_ge(hy_act, HY_ACT["z_sig"])
            hyd("z", dve.tensor_tensor(z1, ps[:, 0, 0:CB * G].rearrange("p (k g) -> p k g", k=CB), z1, ALU.mult))
            dve.wait_ge(hy_pe, HY_PE["skip"])
            skp = ps[:, 7, 0:CB * G].rearrange("p (k g) -> p k g", k=CB)
            cols = lambda v: v.unsqueeze(2).broadcast_to([P, CB, G])
            hyd("skip", dve.tensor_tensor(y1, skp, xs[:, 0:CB, 1:G + 1], ALU.mult))
            dve.wait_ge(hy_pe, HY_PE["y"])
            hyd("y", dve.tensor_tensor(y1, ps[:, 6, 0:CB * G].rearrange("p (k g) -> p k g", k=CB), y1, ALU.add))
            hyd("yg", dve.tensor_tensor(y1, y1, z1, ALU.mult))
            hyd("sq", dve.tensor_tensor(ysq, y1, y1, ALU.mult))
            dve.wait_ge(hy_act, HY_ACT["rms_std"])
            hyd("rms", dve.reciprocal(rms, rms))
            hyd("yn", dve.tensor_tensor(y1, y1, rms.unsqueeze(1).broadcast_to([P, CB, G]), ALU.mult))
            hyd("ynw", dve.tensor_tensor(y1, y1, cols(nwcol), ALU.mult))
            dve.wait_ge(hy_pe, HY_PE["out"])
            ops_ = ps[:, 3, 0:CB * G].rearrange("p (k g) -> p k g", k=CB)
            for n, (r, g) in enumerate(halves):
                hyd(f"ot{n}", dve.tensor_copy(bd[r, :, g], ops_[r, :, :]))
            dve.wait_ge(ld_moe, 16 * len(MOE_LOADS))
            dve.tensor_copy(hv_cols, hv.broadcast_to([P, D])).then_inc(hv_ok, 1)
            for q in range(NC):
                dve.wait_ge(x2_mm, q + 1)
                if q == 0:
                    dve.wait_ge(outb_ok, 1)
                rows_ = xr[:, q * TC:(q + 1) * TC, :]
                dve.tensor_tensor(rows_, ps[:, q % 4, :].rearrange("p (t d) -> p t d", t=TC), rows_,
                                  ALU.add).then_inc(x2_ok, 1)
                dve.wait_ge(x2_ok, q + 1)
                ts = range(q * TC, (q + 1) * TC)
                for t in ts:
                    stats(t)
                aggregate(2, ts)
                finish(2, q)

            dve.wait_ge(row2_in[0], 16)
            dve.tensor_scalar(nb[:, :], arow[:, 0, :], 0.0, FLOOR, ALU.is_equal, ALU.mult).then_inc(g_mask, 1)
            for g in range(NC):
                cols = slice(g * CH, (g + 1) * CH)
                dve.wait_ge(sc_ok, g + 1)
                ins = dve.tensor_tensor(ring[:, 0, cols], arow[:, 0, cols], sbn[:, cols], ALU.mult)
            ins.then_inc(g_prod, 1)

            def g_scores(i, kk):
                kk, i = (kk, i) if kk < 4 else (kk - 4, i + 1)
                k, u, s = 4 * i + kk, kk % 2, kk % 4
                if not (isinstance(k, int) and k == 0):
                    dve.wait_ge(row2_in[u], 16 * (2 * i + kk // 2 + 1))
                    dve.tensor_scalar(nb[:, :], arow[:, u, :], 0.0, FLOOR, ALU.is_equal, ALU.mult).then_inc(g_mask, 1)
                dve.wait_ge(g_mask, k + 1)
                dve.wait_ge(g_prod, k + 1)
                waited(dve)
                dve.tensor_tensor_reduce(ring[:, s, :], ring[:, s, :], nb[:, :], 1.0, FAR, ALU.add, ALU.min,
                                         mn[:, s:s + 1]).then_inc(g_min, 1)
                dve.wait_ge(g_min, k + 1)
                dve.tensor_scalar(mn[:, s:s + 1], mn[:, s:s + 1], FLOOR / 2, None, ALU.min).then_inc(g_score, 1)

            def g_combine(i, kk):
                kk, i = (kk, i) if kk >= 0 else (kk + 4, i - 1)
                k, s = 4 * i + kk, kk % 4
                dve.wait_ge(g_exp, k + 1)
                dve.tensor_scalar(rden[:, s:s + 1], den[:, s:s + 1], 1e-30, None, ALU.max).then_inc(g_den, 1)
                dve.wait_ge(g_den, 2 * k + 1)
                dve.reciprocal(rden[:, s:s + 1], rden[:, s:s + 1]).then_inc(g_den, 1)
                dve.wait_ge(g_den, 2 * k + 2)
                dve.wait_ge(g_mm, k + 1)
                x = xr[:, k, :] if isinstance(k, int) else xr[:, bass.ds(k, 1), :].rearrange("p a d -> p (a d)")
                dve.scalar_tensor_tensor(x, ps[:, 4 + kk % 2, 0:D], rden[:, s:s + 1], x,
                                         ALU.mult, ALU.add).then_inc(x3_ok, 1)
                dve.wait_ge(x3_ok, k + 1)
                st = st6[:, k, :] if isinstance(k, int) else st6[:, bass.ds(k, 1), :].rearrange("p a d -> p (a d)")
                dve.bn_stats(st, x).then_inc(ln_bn, 1)

            def g_steps(i, first=False, last=False):
                for kk in range(4):
                    if not (last and kk + 3 >= 4):
                        g_scores(i, kk + 3)
                    if not (first and kk < 1):
                        g_combine(i, kk - 1)
                    if last and kk == 0:
                        for q in range(NC - 1):
                            aggregate(3, chunk(q))
                    if last and kk == 2:
                        finish(3, 0)
                        finish(3, 1)
                    if last and kk == 3:
                        finish(3, 2)

            for kk in range(3):
                g_scores(0, kk)
            g_steps(0, first=True)
            with dve.Fori(1, NT // 4 - 1) as i:
                g_steps(i)
            g_steps(NT // 4 - 1, last=True)
            g_combine(NT // 4 - 1, 3)

            aggregate(3, chunk(NC - 1))
            finish(3, NC - 1)
            by_node = lambda v: v.unsqueeze(2).broadcast_to([P, NT, EXPERTS])
            by_expert = lambda v: v.unsqueeze(1).broadcast_to([P, NT, EXPERTS])
            dve.wait_ge(r_mm, NC)
            link(dve.tensor_tensor(route, ps[:, 6, 0:NT * EXPERTS].rearrange("p (t e) -> p t e", t=NT), by_expert(br), ALU.add))
            for v, hot in ((v1, hot1), (v2, hot2)):
                link(dve.tensor_reduce(v, route, AX.X, ALU.max))
                link(dve.tensor_tensor(top, route, by_node(v), ALU.is_equal))
                link(dve.tensor_tensor(top, top, by_expert(prio), ALU.mult))
                link(dve.tensor_reduce(ky, top, AX.X, ALU.max))
                link(dve.tensor_tensor(hot, top, by_node(ky), ALU.is_equal))
                if hot is hot1:
                    link(dve.scalar_tensor_tensor(route, hot, -FAR, route, ALU.mult, ALU.add))
            dve.tensor_tensor(v2, v2, v1, ALU.subtract).then_inc(r_dlt, 1)
            dve.wait_ge(r_exp, 1)
            link(dve.tensor_scalar(w1, ew, 1.0, None, ALU.add))
            link(dve.reciprocal(w1, w1))
            link(dve.tensor_tensor(ew, ew, w1, ALU.mult))
            link(dve.tensor_tensor(hot1, hot1, by_node(w1), ALU.mult))
            link(dve.tensor_tensor(hot2, hot2, by_node(ew), ALU.mult))
            dve.tensor_tensor(wfull, hot1, hot2, ALU.add).then_inc(r_w, 1)

            def add_b2(g):
                dve.wait_ge(acc_ok, 8 * (g // 2 + 1))
                dve.wait_ge(b2_mm, g + 1)
                rows_ = xr[:, g * TC:(g + 1) * TC, :]
                dve.tensor_tensor(rows_, ps[:, 6 + g % 2, :].rearrange("p (t d) -> p t d", t=TC), rows_,
                                  ALU.add).then_inc(b2_ok, 1)

            def add_expert(i, v):
                for q in range(NC):
                    st = 8 * i + 4 * v + q
                    dve.wait_ge(down_mm, st + 1)
                    for j in range(TC):
                        t = q * TC + j
                        w = wfull[:, t, 2 * i + v:2 * i + v + 1] if isinstance(i, int) else wfull[:, t, bass.ds(2 * i + v, 1)]
                        ins = dve.scalar_tensor_tensor(xr[:, t, :], ps[:, 4 + q % 2, j * P:(j + 1) * P], w, xr[:, t, :],
                                                       ALU.mult, ALU.add)
                    ins.then_inc(acc_ok, 1)

            dve.wait_ge(r_w, 1)
            add_expert(0, 0)
            add_expert(0, 1)
            add_b2(0)
            add_b2(1)
            dve.wait_ge(b2_ok, 2)
            add_expert(1, 0)
            add_expert(1, 1)
            add_b2(2)
            add_b2(3)
            dve.wait_ge(b2_ok, 4)
            with dve.Fori(2, EXPERTS // 2) as i:
                add_expert(i, 0)
                add_expert(i, 1)

        @block.gpsimd
        def _(pool):
            def weigh(i, kk):
                kk, i = (kk, i) if kk < 6 else (kk - 6, i + 1)
                s, k = kk % RING, 6 * i + kk
                pool.wait_ge(z_ready, k + 1)
                pool.tensor_tensor(ring[:, s, :], ring[:, s, :], arow[:, kk // 3, :], ALU.mult).then_inc(p_ready, 1)

            def steps(i, last=False):
                for kk in range(6):
                    if not (last and kk + 2 >= 6):
                        weigh(i, kk + 2)

            weigh(0, 0)
            weigh(0, 1)
            steps(0)
            with pool.Fori(1, NT // 2 - 1) as i:
                steps(i)
            steps(NT // 2 - 1, last=True)

            for q in range(NC):
                cols = slice(q * CH, (q + 1) * CH)
                pool.wait_ge(gru_n, NC + q + 1)
                pool.tensor_tensor(nsT[:, cols], nsT[:, cols], gts[1][q % 2], ALU.add).then_inc(gru_sum, 1)

            pool_count = [0]

            def pool_link(ins):
                pool_count[0] += 1
                ins.then_inc(pool_seq, 1)
                pool.wait_ge(pool_seq, pool_count[0])

            pool.wait_ge(hy_dve, HY_DVE["slice_b"])
            by_head = lambda v: v.rearrange("p (h g) -> p h g", h=SLOPES)
            pool_link(pool.tensor_tensor(by_head(b_slice), by_head(b_slice),
                                         temp.unsqueeze(2).broadcast_to([P, SLOPES, G]), ALU.mult))
            rest = b_slice
            for n in range(3):
                pool_link(pool.tensor_copy(b_parts[:, n, :], rest))
                if n < 2:
                    pool_link(pool.tensor_tensor(b_rest[n], rest, b_parts[:, n, :], ALU.subtract))
                    rest = b_rest[n]

            def slice_sum(t):
                pool.wait_ge(sw_ok, t + 1)
                if t == 0:
                    pool.tensor_copy(swsum, sw[0]).then_inc(sw_sum, 1)
                else:
                    pool.wait_ge(sw_sum, t)
                    pool.tensor_tensor(swsum, swsum, sw[t % 8], ALU.add).then_inc(sw_sum, 1)

            for t in range(NT):
                pool.wait_ge(lg_sum, t + 1)
                v = sw[t % 8].rearrange("p (h g) -> p h g", h=SLOPES)
                pool.tensor_tensor(v, v, rs8[t % 4].unsqueeze(2).broadcast_to([P, SLOPES, G]), ALU.mult).then_inc(sw_ok, 1)
                if t >= 1:
                    slice_sum(t - 1)
            slice_sum(NT - 1)
            pool.wait_ge(ld_hy, 16 * len(HY_LOADS))
            pool.wait_ge(ln_row, 2 * NT)
            pool.tensor_tensor(xr[:, :, :], xr[:, :, :], outb.unsqueeze(1).broadcast_to([P, NT, D]),
                               ALU.add).then_inc(outb_ok, 1)

            def product(i, kk):
                kk, i = (kk, i) if kk < 4 else (kk - 4, i + 1)
                k, u, s = 4 * i + kk, kk % 2, kk % 4
                pool.wait_ge(row2_in[u], 16 * (2 * i + kk // 2 + 1))
                reached(pool, g_tp, 4 * (k - 3))
                pool.tensor_tensor(ring[:, s, :], arow[:, u, :], sbn, ALU.mult).then_inc(g_prod, 1)

            pool.wait_ge(sc_ok, NC)
            pool.wait_ge(g_prod, 1)
            for kk in range(1, 4):
                product(0, kk)
            with pool.Fori(1, NT // 4) as i:
                for kk in range(4):
                    product(i, kk)

        @block.tensor
        def _(pe):
            def norm_turn(n, q, bank):
                for t in range(q * TC, (q + 1) * TC):
                    pe.wait_ge(ln_row, n * NT + t + 1)
                    ins = pe.transpose(ps[:, bank, (t % TC) * P:(t % TC + 1) * P],
                                       (hrow if n < 3 else xrow)[:, t, :], ident[:, :])
                ins.then_inc(ln_tp, 1)

            def norm_T(n, banks):
                for q in range(NC):
                    norm_turn(n, q, banks[q])

            pe.wait_ge(ld_c, 32)
            def neighbour_sums(j):
                pe.wait_ge(aT_diag, j + 1)
                pe.wait_ge(ln_row, j + 1)
                for g in range(NC):
                    cols = slice(g * CH, (g + 1) * CH)
                    ins = pe.matmul(ps[:, g, :], hrow[:, j, :], aT[j % 3][:, cols],
                                    start=(j == 0), stop=(j == NT - 1))
                ins.then_inc(aT_used, 1)

            norm_turn(0, 0, 4)
            norm_turn(0, 1, 5)
            neighbour_sums(0)
            norm_turn(0, 2, 6)
            norm_turn(0, 3, 7)
            pe.wait_ge(ld_gat, 32)
            pe.wait_ge(ln_hT, 1)
            for h in range(HEADS):
                ins = pe.matmul(ps[:, 4, h:NS:HEADS], gatWT[:, h * D:(h + 1) * D], gatA[:, :, h], start=True, stop=True)
            ins.then_inc(wa_mm, 1)
            pe.wait_ge(wa_sb, 1)
            pe.wait_ge(ln_hT, NC)
            for t in range(NT):
                ins = pe.matmul(ps[:, 5, t * NS:(t + 1) * NS], hT[:, t * P:(t + 1) * P], wa, start=True, stop=True)
            ins.then_inc(u_mm, 1)
            neighbour_sums(1)
            def masked_sums(m):
                pe.wait_ge(masks_ok, m + 1)
                if m == 0:
                    pe.wait_ge(parts_ok, 1)
                for g in range(NC):
                    ins = pe.matmul(ps[0:96, 4 + g, :], parts[:, 0, m, :], masks[:, m % 3, g * CH:(g + 1) * CH],
                                    start=(m == 0), stop=(m == NT - 1))
                ins.then_inc(masks_used, 1)

            for j in range(2, NT + 1):
                if j < NT:
                    neighbour_sums(j)
                if j >= 2 and j - 2 < NT - 1:
                    masked_sums(j - 2)

            def h_w(j):
                if j < 3:
                    pe.wait_ge(ns_sb, j + 2)
                else:
                    pe.wait_ge(hw_sb, j - 2)
                pe.matmul(ps[:, 1 + j % 3, 0:HEADS * D], hT[:, j * P:(j + 1) * P], gatW,
                          start=True, stop=True).then_inc(hw_mm, 1)

            def broadcast(q, g, mm):
                pe.matmul(ps[:, g, :], sel[0:96, q, :], mres[0:96, g * CH:(g + 1) * CH],
                          start=True, stop=True).then_inc(mm, 1)

            pe.wait_ge(ns_sb, 1)
            pe.wait_ge(neg_ok, 1)
            pe.matmul(ps[0:1, 0, 0:1], n_neg1[:, :], n_one[:, :], start=True, stop=True).then_inc(neg_mm, 1)
            pe.wait_ge(ld_gat, 64)
            for j in range(NT // 2):
                h_w(j)
            pe.wait_ge(neg_ok, 2)
            negative = pe.value_load(any_neg[0:1, 0:1], min_val=0, max_val=N * N)
            with pe.If(negative > 0):
                for m in range(NT):
                    pe.wait_ge(neg_masks, m + 1)
                    for g in range(NC):
                        ins = pe.matmul(ps[0:96, 4 + g, :], parts[:, 1, m, :], masks[:, NEG_SLOT[m % 2], g * CH:(g + 1) * CH],
                                        start=False, stop=False)
                    ins.then_inc(neg_used, 1)
            masked_sums(NT - 1)
            for j in range(NT // 2, NT):
                h_w(j)
            pe.wait_ge(hw_sb, NT)
            for n in range(HEADS * NC):
                if n < NC:
                    pe.wait_ge(mres_sb, n + 1)
                else:
                    pe.wait_ge(bc_sb, n - 3)
                broadcast(n // NC, n % NC, bc_mm)
            with pe.If(negative > 0):
                for n in range(HEADS * NC):
                    if n < NC:
                        pe.wait_ge(bc_sb, HEADS * NC - NC + n + 1)
                    else:
                        pe.wait_ge(minus_sb, n - 3)
                    broadcast(HEADS + n // NC, n % NC, minus_mm)
                pe.wait_ge(minus_sb, HEADS * NC)

            def gru(n, srcT):
                for q in range(NC):
                    cols = slice(q * CH, (q + 1) * CH)
                    b = GRU_BANK(q)
                    c = n * NC + q
                    if n == 0:
                        if q == 0:
                            pe.wait_ge(ld_gru, 96)
                            pe.wait_ge(bc_sb, HEADS * NC)
                    if q >= 2:
                        pe.wait_ge(gru_z, c - 1)
                        pe.wait_ge(gru_t, c - 1)
                    for gate in range(2):
                        w = slice(gate * D, (gate + 1) * D)
                        pe.matmul(ps[:, b + gate, :], WT[2 * n + 1][:, w], hT[:, cols], start=True, stop=False)
                    if n == 1 and q == 0:
                        pe.wait_ge(es_T, NT)
                    for gate in range(2):
                        w = slice(gate * D, (gate + 1) * D)
                        pe.matmul(ps[:, b + gate, :], WT[2 * n][:, w], srcT[:, cols],
                                  start=False, stop=True).then_inc(gru_mm, 1)
                    w = slice(2 * D, 3 * D)
                    pe.matmul(ps[:, b + 2, :], WT[2 * n + 1][:, w], hT[:, cols], start=True, stop=True).then_inc(gru_mm, 1)
                    if n == 1 and q >= 2:
                        pe.wait_ge(x1_ok, (q - 1) * TC)
                    pe.matmul(ps[:, b + 3, :], WT[2 * n][:, w], srcT[:, cols], start=True, stop=True).then_inc(gru_mm, 1)
                    if n == 1 and q >= 1:
                        if q == NC - 1:
                            slice_weights()
                        rows_turn(q - 1)

            def rows_turn(q):
                pe.wait_ge(gru_out, NC + q + 1)
                for t in range(q * TC, (q + 1) * TC):
                    ins = pe.transpose(ps[:, GRU_BANK(q) + 3, (t % TC) * P:(t % TC + 1) * P],
                                       nsT[:, t * P:(t + 1) * P], ident[:, :])
                ins.then_inc(x1_tp, 1)

            def slice_weights():
                pe.wait_ge(ld_slice, 80)
                pe.wait_ge(gru_z, 2 * NC - 1)
                for h in range(SLOPES):
                    ins = pe.matmul(ps[:, 0, h * G:(h + 1) * G], wx[0:64, h, :], wsT[0:64, :], start=True, stop=True)
                ins.then_inc(hy_pe, 1)
                pe.wait_ge(hy_dve, HY_DVE["bias_cols"])
                for h in range(SLOPES):
                    ins = pe.matmul(ps[:, 1, h * G:(h + 1) * G], bx_cols[0:64, h, :], wsT[0:64, :], start=True, stop=True)
                ins.then_inc(hy_pe, 1)

            gru(0, nsT)

            def turn(i, kk):
                kk, i = (kk, i) if kk < 6 else (kk - 6, i + 1)
                s, k = kk % RING, 6 * i + kk
                pe.wait_ge(p_ready, k + 1)
                for b in range(4):
                    reached(pe, tp_out, 4 * (k - 1) + b + 1)
                    for j in range(4):
                        c = (4 * b + j) * P
                        ins = pe.transpose(ps[:, b, j * P:(j + 1) * P], ring[:, s, c:c + P], ident[:, :])
                    ins.then_inc(tp_ready, 1)

            def attend(i, kk):
                h, k = kk % 3, 6 * i + kk
                pe.wait_ge(tp_out, 4 * (k + 1))
                reached(pe, es_acc, k - 1)
                for j in range(NT):
                    ins = pe.matmul(ps[:, 4 + kk % 2, 0:D], pat[:, kk % 2, j * P:(j + 1) * P],
                                    hW[:, j, h * D:(h + 1) * D], start=(j == 0), stop=(j == NT - 1))
                ins.then_inc(mm_done, 1)

            def es_turn(t, u):
                pe.wait_ge(es_acc, 3 * (t + 1))
                reached(pe, es_T, t - 1)
                pe.transpose(ps[:, 6 + u, 0:P], esb[:, u, :], ident[:, :]).then_inc(es_tp, 1)

            def steps(i, first=False, last=False):
                for kk in range(6):
                    if kk % 3 == 2 and not (first and kk == 2):
                        es_turn(2 * i + kk // 3 - 1, 1 - kk // 3)
                    if not (last and kk == 5):
                        turn(i, kk + 1)
                    attend(i, kk)

            pe.wait_ge(gru_t, NC - 1)
            pe.wait_ge(gru_z, NC - 1)
            turn(0, 0)
            pe.wait_ge(gru_t, NC)
            pe.wait_ge(gru_z, NC)
            steps(0, first=True)
            with pe.Fori(1, NT // 2 - 1) as i:
                steps(i)
            steps(NT // 2 - 1, last=True)
            es_turn(NT - 1, 1)
            gru(1, esT)
            rows_turn(NC - 1)
            norm_T(1, (2, 3, 6, 7))

            def logits(t):
                if t == 0:
                    pe.wait_ge(b_rows_ok, 3)
                if t % TC == 0:
                    pe.wait_ge(ln_hT, NC + t // TC + 1)
                if t == 2:
                    pe.wait_ge(ln_hT, NC + 2)
                if t >= 3:
                    pe.wait_ge(lg_sub, t - 2)
                pe.matmul(ps[:, LOGIT_BANKS[t % 3], :], ones16[0:96, :], b_rows[0:96, :], start=True, stop=False)
                pe.matmul(ps[:, LOGIT_BANKS[t % 3], :], hT[:, t * P:(t + 1) * P], w_slice, start=False, stop=True).then_inc(lg_mm, 1)

            def gather(t):
                pe.wait_ge(sw_ok, t + 1)
                if t == 0:
                    pe.wait_ge(ln_hT, 2 * NC)
                pe.matmul(ps[:, 6, :], hrow[:, t, :], sw[t % 8], start=(t == 0), stop=(t == NT - 1))
                if t >= 2:
                    pe.wait_ge(sw_T, t - 1)
                for m in range(CB):
                    ins = pe.transpose(ps[:, t % 2, m * P:(m + 1) * P], sw[t % 8][:, m * P:(m + 1) * P], ident[:, :])
                ins.then_inc(sw_tp, 1)

            for t in range(NT):
                logits(t)
                if t >= 4:
                    gather(t - 4)
            for t in range(NT - 4, NT):
                gather(t)

            pe.wait_ge(ones_ok, 1)
            pe.wait_ge(sw_sum, NT)
            pe.matmul(ps[:, 7, :], ones, swsum, start=True, stop=True).then_inc(hy_pe, 1)
            pe.wait_ge(hy_dve, HY_DVE["tok_w"])
            pe.wait_ge(sw_T, NT)
            for m in range(CB):
                ins = pe.matmul(ps[:, 0, m * P:(m + 1) * P], wfxT[:, m * P:(m + 1) * P], tok_n[:, m * P:(m + 1) * P],
                                start=True, stop=True)
            ins.then_inc(hy_pe, 1)
            pe.wait_ge(hy_dve, HY_DVE["tok1"])

            def project(o, w_of, x_of):
                for k in range(CB):
                    ins = pe.matmul(o, w_of(k), x_of(k), start=(k == 0), stop=(k == CB - 1))
                return ins

            for m in range(2):
                c = 2 * DI + m * G
                project(ps[0:64, 2, m * G:(m + 1) * G], lambda k: in_wT[:, k, c:c + G], lambda k: tokT[:, k, :])
            for v in range(2):
                c = 2 * DI + 2 * G + v * SLOPES
                ins = project(ps[64 * v:64 * v + 64, 3, 0:SLOPES], lambda k: tokT[:, k, :], lambda k: in_wT[:, k, c:c + SLOPES])
            ins.then_inc(hy_pe, 1)
            for first, bank in ((DI, 1), (0, 0)):
                if bank == 0:
                    pe.wait_ge(hy_dve, HY_DVE["decay_in"])
                    pe.matmul(ps[:, 5, :], m_rs, dec, start=True, stop=True).then_inc(hy_pe, 1)
                for m in range(CB):
                    c = first + m * P
                    ins = project(ps[:, bank, m * G:(m + 1) * G], lambda k: in_wT[:, k, c:c + P], lambda k: tokT[:, k, :])
                ins.then_inc(hy_pe, 1)
            pe.wait_ge(hy_dve, HY_DVE["x_twice"])
            for v in range(2):
                ins = pe.matmul(ps[64 * v:64 * v + 64, 3, G:2 * G], xs[0:64, CB, 1:G + 1],
                                xs[0:64, CB + 1, 2 * v:2 * v + G], start=True, stop=True)
            ins.then_inc(hy_pe, 1)
            project(ps[0:SLOPES, 7, CB * G:(CB + 1) * G], lambda k: fcDT[:, k, :],
                    lambda k: xs[:, k, 1:G + 1]).then_inc(hy_pe, 1)
            for m in range(CB):
                ins = pe.transpose(ps[:, 4, m * P:(m + 1) * P], xd[:, m, :, :].rearrange("p v g -> p (v g)"), ident[:, :])
            ins.then_inc(hy_pe, 1)
            pe.wait_ge(hy_dve, HY_DVE["skip8"])
            for m in range(CB):
                ins = pe.matmul(ps[:, 7, m * G:(m + 1) * G], headsel[:, m, :], skip8, start=True, stop=True)
            ins.then_inc(hy_pe, 1)
            pe.wait_ge(hy_act, HY_ACT["x_rows"])
            pe.wait_ge(hy_dve, HY_DVE["weight"])
            for h in range(SLOPES):
                ins = pe.matmul(ps[64 * (h % 2):64 * (h % 2) + 64, 6, (h // 2) * G:(h // 2 + 1) * G],
                                x2[:, h * 64:(h + 1) * 64], dec[:, h, :], start=True, stop=True)
            ins.then_inc(hy_pe, 1)
            pe.wait_ge(hy_dve, HY_DVE["sq"])
            project(ps[:, 2, 0:G], lambda k: ones, lambda k: ysq[:, k, :]).then_inc(hy_pe, 1)
            pe.wait_ge(hy_dve, HY_DVE["ynw"])
            for m in range(CB):
                ins = project(ps[:, 3, m * G:(m + 1) * G], lambda k: outT[:, k, m * P:(m + 1) * P], lambda k: y1[:, k, :])
            ins.then_inc(hy_pe, 1)
            pe.wait_ge(hy_dve, HY_DVE["ot1"])
            for m in range(CB):
                ins = pe.matmul(ps[:, 4, m * P:(m + 1) * P], bd[:, m, :], outwT[:, m, :], start=True, stop=True)
            ins.then_inc(hy_pe, 1)
            pe.wait_ge(hy_act, HY_ACT["value"])
            def node_scores(g):
                pe.wait_ge(hv_ok, 1)
                pe.wait_ge(ln_hT, 2 * NC + g + 1)
                pe.matmul(ps[:, g, :], hv_cols, hT[:, g * CH:(g + 1) * CH], start=True, stop=True).then_inc(sc_mm, 1)

            for t in range(NT):
                for m in range(CB):
                    ins = pe.matmul(ps[:, (t // TC) % 4, (t % TC) * P:(t % TC + 1) * P], swT[:, m, t * P:(t + 1) * P],
                                    val[:, m, :], start=(m == 0), stop=(m == CB - 1))
                if t % TC == TC - 1:
                    ins.then_inc(x2_mm, 1)
                    if t // TC >= 1:
                        norm_turn(2, t // TC - 1, 3 + t // TC)
                    if t // TC >= 2:
                        node_scores(t // TC - 2)

            node_scores(NC - 2)
            norm_turn(2, NC - 1, 3 + NC)
            node_scores(NC - 1)

            def g_turn(i, kk):
                kk, i = (kk, i) if kk < 4 else (kk - 4, i + 1)
                k = 4 * i + kk
                pe.wait_ge(g_exp, k + 1)
                for b in range(4):
                    if isinstance(k, int) and k == 0:
                        pe.wait_ge(sc_ok, NC)
                    reached(pe, g_out, 4 * (k - 1) + b + 1)
                    for j in range(4):
                        c = (4 * b + j) * P
                        ins = pe.transpose(ps[:, b, j * P:(j + 1) * P], ring[:, kk, c:c + P], ident[:, :])
                    ins.then_inc(g_tp, 1)

            def g_attend(i, kk):
                k = 4 * i + kk
                pe.wait_ge(g_out, 4 * (k + 1))
                reached(pe, x3_ok, k - 1)
                for j in range(NT):
                    ins = pe.matmul(ps[:, 4 + kk % 2, 0:D], pat[:, kk % 2, j * P:(j + 1) * P], hrow[:, j, :],
                                    start=(j == 0), stop=(j == NT - 1))
                ins.then_inc(g_mm, 1)

            def g_steps(i, last=False):
                for kk in range(4):
                    if not (last and kk + 1 >= 4):
                        g_turn(i, kk + 1)
                    g_attend(i, kk)
                    if last and kk == 2:
                        norm_turn(3, 0, 6)
                        norm_turn(3, 1, 7)

            g_turn(0, 0)
            g_steps(0)
            with pe.Fori(1, NT // 4 - 1) as i:
                g_steps(i)
            g_steps(NT // 4 - 1, last=True)

            def router_logits(q):
                pe.wait_ge(ln_hT, 3 * NC + q + 1)
                for t in range(q * TC, (q + 1) * TC):
                    ins = pe.matmul(ps[:, 6, t * EXPERTS:(t + 1) * EXPERTS], hT[:, t * P:(t + 1) * P], wr,
                                    start=True, stop=True)
                ins.then_inc(r_mm, 1)

            def router_turn(g):
                pe.wait_ge(r_w, 1)
                reached(pe, r_wT, g - 1)
                for t in range(g * TC, (g + 1) * TC):
                    ins = pe.transpose(ps[0:EXPERTS, 6 + g % 2, (t % TC) * P:(t % TC + 1) * P], wfull[:, t, :], ident[:, :])
                ins.then_inc(r_tp, 1)

            def second_bias(g):
                pe.wait_ge(r_wT, NC)
                reached(pe, b2_ok, g - 1)
                for t in range(g * TC, (g + 1) * TC):
                    ins = pe.matmul(ps[:, 6 + g % 2, (t % TC) * P:(t % TC + 1) * P], wT[:, t * P:(t + 1) * P],
                                    b2[0:EXPERTS, :], start=True, stop=True)
                ins.then_inc(b2_mm, 1)

            def up(i, v, q, first=False):
                st = 8 * i + 4 * v + q
                if q == 0:
                    pe.wait_ge(ld_exp[v], 32 * (i + 1))
                if first and v == 0:
                    pe.wait_ge(ln_hT, 3 * NC + q + 1)
                for c in range(HC):
                    if not (first and st < 2):
                        pe.wait_ge(gelu_ok, HC * (st - 2) + c + 1)
                    pe.matmul(ps[:, 2 * (q % 2) + c, :], wexp[v][0][:, c * P:(c + 1) * P], hT[:, q * CH:(q + 1) * CH],
                              start=True, stop=True).then_inc(up_mm, 1)

            def down(i, v, q, first=False):
                v, i, q = (v, i, q) if q >= 0 else (1 - v, i - (1 - v), q + NC)
                st = 8 * i + 4 * v + q
                pe.wait_ge(gelu_ok, HC * (st + 1))
                if first and st < 2:
                    pe.wait_ge(x3_ok, NT)
                else:
                    pe.wait_ge(acc_ok, st - 1)
                for j in range(TC):
                    for c in range(HC):
                        ins = pe.matmul(ps[:, 4 + q % 2, j * P:(j + 1) * P], hid[:, q % 2, c, j * P:(j + 1) * P],
                                        wexp[v][1][:, c, :], start=(c == 0), stop=(c == HC - 1))
                ins.then_inc(down_mm, 1)

            def expert(i, v, first=False):
                for q in range(NC):
                    up(i, v, q, first)
                    down(i, v, q - 1, first)

            pe.wait_ge(ln_hT, 3 * NC + 1)
            norm_turn(3, 2, 6)
            up(0, 0, 0, first=True)
            up(0, 0, 1, first=True)
            pe.wait_ge(ln_hT, 3 * NC + 3)
            router_logits(0)
            router_logits(1)
            router_logits(2)
            norm_turn(3, 3, 7)
            router_logits(3)
            for q in range(2, NC):
                down(0, 0, q - 2, first=True)
                up(0, 0, q, first=True)
            down(0, 0, 2, first=True)
            router_turn(0)
            router_turn(1)
            expert(0, 1, first=True)
            router_turn(2)
            router_turn(3)
            second_bias(0)
            second_bias(1)
            expert(1, 0)
            expert(1, 1)
            second_bias(2)
            second_bias(3)
            with pe.Fori(2, EXPERTS // 2) as i:
                expert(i, 0)
                expert(i, 1)
            down(EXPERTS // 2 - 1, 1, NC - 1)


def GRU_BANK(q):
    return 0 if q % 2 == 0 else 4




def lay_out(inputs):
    c = np.ascontiguousarray
    i = {k: np.asarray(v) for k, v in inputs.items()}
    adj = i["adj"]
    T = lambda w: c(w.T)
    o = {"x": c(i["x"]), "adjT": c(adj.T), "adj_t": c(adj.reshape(NT, P, N)),
         "diag": c(np.diagonal(adj).reshape(NT, P).T)}
    eye = np.eye(P, dtype=np.float32)
    o["ident"] = eye
    o["noteye"] = np.ones((P, P), np.float32)
    np.fill_diagonal(o["noteye"], 0)
    sel = np.zeros((96, NS, P), np.float32)
    for q in range(NS):
        sel[q::32, q, :] = 1
    o["sel"] = sel
    W = i["L0_gnn_gat_W"]
    o["gat_WT"] = c(W.transpose(2, 0, 1).reshape(D, HEADS * D))
    o["gat_W"] = c(W.transpose(1, 0, 2).reshape(D, HEADS * D))
    o["gat_a"] = c(i["L0_gnn_gat_a"].reshape(HEADS, 2, D).transpose(2, 1, 0))
    gru = ("L0_gnn_edge_", "L0_gnn_node_")
    o["gru_WT"] = c(np.stack([i[g + w].T for g in gru for w in ("Wih", "Whh")]))
    o["gru_b"] = c(np.stack([i[g + b].reshape(3, D) for g in gru for b in ("bih", "bhh")]).transpose(2, 0, 1))
    f = "L0_ffn_"
    across = lambda v, n: c(np.broadcast_to(v, (n,) + v.shape))
    cols = lambda v: c(v.reshape(-1, P).T)
    o["wx"] = c(i[f + "W_x"].reshape(SLOPES, 64, D).transpose(1, 0, 2))
    o["wsT"] = T(i[f + "W_slice"])
    o["bx"] = T(i[f + "b_x"].reshape(SLOPES, 64))
    o["b_slice"] = across(i[f + "b_slice"], P)
    o["temp"] = across(i[f + "temperature"].reshape(-1), P)
    chunks = lambda w: c(w.T.reshape(CB, P, -1).transpose(1, 0, 2))
    o["in_wT"] = chunks(i[f + "hy_in_w"])
    o["wfxT"] = T(i[f + "W_fx"])
    o["bfx"] = cols(i[f + "b_fx"])
    cw, cb = i[f + "hy_conv_w"], i[f + "hy_conv_b"]
    w6, b6 = np.zeros((P, 6, 3), np.float32), np.zeros((P, 6), np.float32)
    w6[:, :CB] = cw[:DI].reshape(CB, P, 3).transpose(1, 0, 2)
    w6[:64, CB:] = cw[DI:].reshape(2, 64, 3).transpose(1, 0, 2)
    b6[:, :CB] = cb[:DI].reshape(CB, P).T
    b6[:64, CB:] = cb[DI:].reshape(2, 64).T
    o["cw"], o["cb"] = w6, b6
    o["dtb"] = across(i[f + "hy_dt_bias"], P)
    o["alog"] = across(i[f + "hy_A_log"], P)
    r = np.arange(64)
    m_rs, m_rt, m_st = np.zeros((P, P), np.float32), np.zeros((P, G), np.float32), np.zeros((P, G), np.float32)
    m_rs[:64, :64] = r[:, None] > r[None, :]
    m_rs[64:, 64:] = r[:, None] < r[None, :]
    m_rt[:64], m_rt[64:] = r[:, None] <= r[None, :] - 1, r[:, None] >= r[None, :] + 1
    m_st[:64], m_st[64:] = r[:, None] <= r[None, :] - 1, r[:, None] >= r[None, :] + 1
    o["m_rs"], o["m_rt"], o["m_st"] = m_rs, m_rt, m_st
    o["outb"] = across(i[f + "out_b"], P)
    o["fcDT"] = chunks(i[f + "hy_fcD_w"])
    o["d_head"] = c(i[f + "hy_D"][:, None])
    o["headsel"] = c(np.repeat(np.eye(SLOPES, dtype=np.float32), 64, axis=1).reshape(SLOPES, CB, P))
    o["nwcol"] = cols(i[f + "hy_norm_w"])
    o["outT"] = chunks(i[f + "hy_out_w"])
    o["outwT"] = chunks(i[f + "out_w"])
    e = "L1_ffn_"
    o["hv"] = c(i["L1_gnn_H_v"])
    o["gamma"], o["beta"] = c(i[e + "gamma"][:, None]), c(i[e + "beta"][:, None])
    o["Wr"], o["br"] = c(i[e + "Wr"]), across(i[e + "br"], P)
    o["prio"] = across(np.arange(EXPERTS, 0, -1).astype(np.float32), P)
    o["b1"] = c(i[e + "b1"].reshape(EXPERTS, HC, P).transpose(2, 0, 1))
    o["b2"] = c(i[e + "b2"])
    o["W1"] = c(i[e + "W1"])
    o["W2"] = c(i[e + "W2"].reshape(EXPERTS, HC, P, D).transpose(0, 2, 1, 3))
    return o


def kernel(**inputs):
    import concourse.bacc as _bacc
    from concourse.bass_utils import run_bass_kernel_spmd as _run

    nc = _bacc.Bacc("TRN2", target_bir_lowering=False, num_devices=1)
    arrays, args = {}, {}
    for name, a in lay_out(inputs).items():
        arrays[f"in_{name}"] = a
        args[name] = nc.dram_tensor(f"in_{name}", a.shape, mybir.dt.from_np(a.dtype), kind="ExternalInput").ap()
    out = nc.dram_tensor("out_0", (N, D), F32, kind="ExternalOutput").ap()
    graph_block(nc, args, out)
    r = _run(nc, [arrays], core_ids=[0])
    return r.results[0]["out_0"]
```
